# Optimizing a Trainium2 kernel written in Bass

```python
import numpy as np
import jax
import jax.numpy as jnp

def _softmax(x, axis=-1):
    return jax.nn.softmax(x, axis=axis)

def _gelu(x):
    return jax.nn.gelu(x, approximate=True)

def _silu(x):
    return jax.nn.silu(x)

def _sigmoid(x):
    return jax.nn.sigmoid(x)

def _layernorm(x, axis=-1, eps=1e-05):
    m = jnp.mean(x, axis=axis, keepdims=True)
    v = jnp.var(x, axis=axis, keepdims=True)
    return (x - m) / jnp.sqrt(v + eps)

def _scatter_add(tgt, idx, src, axis=0):
    return tgt.at[idx].add(src)

def _segment_sum(src, seg, n):
    return jax.ops.segment_sum(src, seg, n)
kernel_name = 'mk_xattn_seq_d2_seqx_r4_caff23'

def setup_inputs(seed: int=0):
    np.random.seed(seed)
    _w = jnp.asarray

    def _rec_inputs():
        import jax
        import jax.numpy as jnp
        _rk = jax.random.key(seed)
        x = -0.0005207 + 1.001 * jax.random.normal(jax.random.fold_in(_rk, 1), (8, 112, 512), jnp.float32)
        _lenS = 112 - jax.random.randint(jax.random.fold_in(_rk, 7), (8,), 0, max(1, 112 // 4) + 1, jnp.int32)
        _lenS2 = 375 - jax.random.randint(jax.random.fold_in(_rk, 8), (8,), 0, max(1, 375 // 4) + 1, jnp.int32)
        _ctx_2048P = jax.random.normal(jax.random.fold_in(_rk, 11), (8, 16, 512), jnp.float32)
        _ctx_2048c = jax.random.dirichlet(jax.random.fold_in(_rk, 511), 0.3 * jnp.ones((16,), jnp.float32), (8, 375))
        _ctx_2048t = jnp.einsum('bsk,bkd->bsd', _ctx_2048c, _ctx_2048P)
        _ctx_2048t = _ctx_2048t * jax.lax.rsqrt(jnp.mean(jnp.square(_ctx_2048t)) + 1e-12) * 0.953939
        ctx_2048 = 2.81802e-05 + 1.00001 * (_ctx_2048t + 0.3 * jax.random.normal(jax.random.fold_in(_rk, 611), (8, 375, 512), jnp.float32))
        _validS = jnp.arange(112)[None, :] < _lenS[:, None]
        _validS2 = jnp.arange(375)[None, :] < _lenS2[:, None]
        _causal = jnp.tril(jnp.ones((112, 112), dtype=bool))
        mask_Bx1xSxS2_ff0 = jnp.where(jnp.ones((8, 1, 112, 375), dtype=bool), 0.0, -1000000000.0).astype(jnp.float32)
        return (x, ctx_2048, mask_Bx1xSxS2_ff0)
    x, ctx_2048, mask_Bx1xSxS2_ff0 = _rec_inputs()

    def _L0_xattn_setup():
        import jax, jax.numpy as jnp
        import numpy as np
        B, Q, S1, S2 = (4, 64, 512, 512)
        D, H, K, F = (512, 16, 128, 2048)
        LN_EPS = 1e-05

        def _layer_norm(x, scale, offset):
            mu = jnp.mean(x, axis=-1, keepdims=True)
            var = jnp.var(x, axis=-1, keepdims=True)
            return (x - mu) * jax.lax.rsqrt(var + LN_EPS) * scale + offset

        def _cross_attention(q_in, kv_in, wq, bq, wk, bk, wv, bv, wo, bo, bias_k, bias_v):
            b, q_len, _ = q_in.shape
            t = kv_in.shape[1]
            qh = (q_in @ wq + bq).reshape(b, q_len, H, K)
            kh = (kv_in @ wk + bk).reshape(b, t, H, K)
            vh = (kv_in @ wv + bv).reshape(b, t, H, K)
            kh = jnp.concatenate([kh, jnp.broadcast_to(bias_k, (b, 1, H, K))], axis=1)
            vh = jnp.concatenate([vh, jnp.broadcast_to(bias_v, (b, 1, H, K))], axis=1)
            scale = jnp.sqrt(jnp.asarray(K, q_in.dtype))
            logits = jnp.einsum('bqhk,bthk->bhqt', qh, kh) / scale
            weights = jax.nn.softmax(logits, axis=-1)
            ctx = jnp.einsum('bhqt,bthk->bqhk', weights, vh).reshape(b, q_len, H * K)
            return ctx @ wo + bo

        def _forward(x, xf_1, xf_2, ln1_scale, ln1_offset, wq1, bq1, wk1, bk1, wv1, bv1, wo1, bo1, bias_k1, bias_v1, ln2_scale, ln2_offset, wq2, bq2, wk2, bk2, wv2, bv2, wo2, bo2, bias_k2, bias_v2, ln_mlp_scale, ln_mlp_offset, w_fc1, b_fc1, w_fc2, b_fc2):
            res = x
            h = _layer_norm(x, ln1_scale, ln1_offset)
            x = res + _cross_attention(h, xf_1, wq1, bq1, wk1, bk1, wv1, bv1, wo1, bo1, bias_k1, bias_v1)
            res = x
            h = _layer_norm(x, ln2_scale, ln2_offset)
            x = res + _cross_attention(h, xf_2, wq2, bq2, wk2, bk2, wv2, bv2, wo2, bo2, bias_k2, bias_v2)
            h = _layer_norm(x, ln_mlp_scale, ln_mlp_offset)
            h = jax.nn.gelu(h @ w_fc1 + b_fc1, approximate=False) @ w_fc2 + b_fc2
            return x + h
        key = jax.random.key(seed)
        ks = iter(jax.random.split(key, 64))

        def rn(shape, s=0.02):
            return jax.random.normal(next(ks), shape, jnp.float32) * s
        inp = {'x': rn((B, Q, D), 1.0), 'xf_1': rn((B, S1, D), 1.0), 'xf_2': rn((B, S2, D), 1.0)}
        for i in (1, 2):
            inp[f'ln{i}_scale'] = jnp.ones((D,), jnp.float32)
            inp[f'ln{i}_offset'] = jnp.zeros((D,), jnp.float32)
            inp[f'wq{i}'] = rn((D, H * K))
            inp[f'bq{i}'] = jnp.zeros((H * K,), jnp.float32)
            inp[f'wk{i}'] = rn((D, H * K))
            inp[f'bk{i}'] = jnp.zeros((H * K,), jnp.float32)
            inp[f'wv{i}'] = rn((D, H * K))
            inp[f'bv{i}'] = jnp.zeros((H * K,), jnp.float32)
            inp[f'wo{i}'] = rn((H * K, D))
            inp[f'bo{i}'] = jnp.zeros((D,), jnp.float32)
            inp[f'bias_k{i}'] = rn((1, 1, H, K))
            inp[f'bias_v{i}'] = rn((1, 1, H, K))
        inp['ln_mlp_scale'] = jnp.ones((D,), jnp.float32)
        inp['ln_mlp_offset'] = jnp.zeros((D,), jnp.float32)
        inp['w_fc1'] = rn((D, F))
        inp['b_fc1'] = jnp.zeros((F,), jnp.float32)
        inp['w_fc2'] = rn((F, D))
        inp['b_fc2'] = jnp.zeros((D,), jnp.float32)
        return inp
    _L0_xattn_all = _L0_xattn_setup()
    _L0_xattn_in = {k: v for k, v in _L0_xattn_all.items() if k in ('ln1_scale', 'ln1_offset', 'wq1', 'bq1', 'wk1', 'bk1', 'wv1', 'bv1', 'wo1', 'bo1', 'bias_k1', 'bias_v1', 'ln2_scale', 'ln2_offset', 'wq2', 'bq2', 'wk2', 'bk2', 'wv2', 'bv2', 'wo2', 'bo2', 'bias_k2', 'bias_v2', 'ln_mlp_scale', 'ln_mlp_offset', 'w_fc1', 'b_fc1', 'w_fc2', 'b_fc2')}
    del _L0_xattn_all

    def _L1_xattn_setup():
        import jax, jax.numpy as jnp
        import numpy as np
        H = 512
        NH = 32
        KVH = 8
        HD = H // NH
        GROUPS = NH // KVH
        EPS = 1e-06
        B, L, S = (4, 256, 256)

        def _gqa_forward(hidden_state, encoder_hidden_state, encoder_attention_mask, Wq, bq, Wk, bk, Wv, bv, Wo, bo, gamma, beta):
            b, l, _ = hidden_state.shape
            s = encoder_hidden_state.shape[1]
            q = hidden_state @ Wq + bq
            k = encoder_hidden_state @ Wk + bk
            v = encoder_hidden_state @ Wv + bv
            q = q.reshape(b, l, KVH, GROUPS, HD).transpose(0, 2, 3, 1, 4)
            k = k.reshape(b, s, KVH, HD).transpose(0, 2, 1, 3)
            v = v.reshape(b, s, KVH, HD).transpose(0, 2, 1, 3)
            scale = 1.0 / jnp.sqrt(jnp.asarray(HD, q.dtype))
            scores = jnp.einsum('bkgld,bksd->bkgls', q, k) * scale
            scores = scores + encoder_attention_mask[:, :, None, :, :]
            attn = jax.nn.softmax(scores, axis=-1)
            out = jnp.einsum('bkgls,bksd->bkgld', attn, v)
            out = out.transpose(0, 3, 1, 2, 4).reshape(b, l, H)
            out = out @ Wo + bo
            x = out + hidden_state
            mu = jnp.mean(x, axis=-1, keepdims=True)
            var = jnp.var(x, axis=-1, keepdims=True)
            return (x - mu) * jax.lax.rsqrt(var + EPS) * gamma + beta
        key = jax.random.key(seed)
        ks = jax.random.split(key, 12)
        sd = 0.02
        return {'hidden_state': jax.random.normal(ks[0], (B, L, H), jnp.float32), 'encoder_hidden_state': jax.random.normal(ks[1], (B, S, H), jnp.float32), 'encoder_attention_mask': jnp.zeros((B, 1, L, S), jnp.float32), 'Wq': jax.random.normal(ks[2], (H, H), jnp.float32) * sd, 'bq': jnp.zeros((H,), jnp.float32), 'Wk': jax.random.normal(ks[3], (H, KVH * HD), jnp.float32) * sd, 'bk': jnp.zeros((KVH * HD,), jnp.float32), 'Wv': jax.random.normal(ks[4], (H, KVH * HD), jnp.float32) * sd, 'bv': jnp.zeros((KVH * HD,), jnp.float32), 'Wo': jax.random.normal(ks[5], (H, H), jnp.float32) * sd, 'bo': jnp.zeros((H,), jnp.float32), 'gamma': jnp.ones((H,), jnp.float32), 'beta': jnp.zeros((H,), jnp.float32)}
    _L1_xattn_all = _L1_xattn_setup()
    _L1_xattn_in = {k: v for k, v in _L1_xattn_all.items() if k in ('Wq', 'bq', 'Wk', 'bk', 'Wv', 'bv', 'Wo', 'bo', 'gamma', 'beta')}
    del _L1_xattn_all
    return {'x': x, 'ctx_2048': ctx_2048, 'mask_Bx1xSxS2_ff0': mask_Bx1xSxS2_ff0, 'L0_xattn_ln1_scale': _L0_xattn_in['ln1_scale'], 'L0_xattn_ln1_offset': _L0_xattn_in['ln1_offset'], 'L0_xattn_wq1': _L0_xattn_in['wq1'], 'L0_xattn_bq1': _L0_xattn_in['bq1'], 'L0_xattn_wk1': _L0_xattn_in['wk1'], 'L0_xattn_bk1': _L0_xattn_in['bk1'], 'L0_xattn_wv1': _L0_xattn_in['wv1'], 'L0_xattn_bv1': _L0_xattn_in['bv1'], 'L0_xattn_wo1': _L0_xattn_in['wo1'], 'L0_xattn_bo1': _L0_xattn_in['bo1'], 'L0_xattn_bias_k1': _L0_xattn_in['bias_k1'], 'L0_xattn_bias_v1': _L0_xattn_in['bias_v1'], 'L0_xattn_ln2_scale': _L0_xattn_in['ln2_scale'], 'L0_xattn_ln2_offset': _L0_xattn_in['ln2_offset'], 'L0_xattn_wq2': _L0_xattn_in['wq2'], 'L0_xattn_bq2': _L0_xattn_in['bq2'], 'L0_xattn_wk2': _L0_xattn_in['wk2'], 'L0_xattn_bk2': _L0_xattn_in['bk2'], 'L0_xattn_wv2': _L0_xattn_in['wv2'], 'L0_xattn_bv2': _L0_xattn_in['bv2'], 'L0_xattn_wo2': _L0_xattn_in['wo2'], 'L0_xattn_bo2': _L0_xattn_in['bo2'], 'L0_xattn_bias_k2': _L0_xattn_in['bias_k2'], 'L0_xattn_bias_v2': _L0_xattn_in['bias_v2'], 'L0_xattn_ln_mlp_scale': _L0_xattn_in['ln_mlp_scale'], 'L0_xattn_ln_mlp_offset': _L0_xattn_in['ln_mlp_offset'], 'L0_xattn_w_fc1': _L0_xattn_in['w_fc1'], 'L0_xattn_b_fc1': _L0_xattn_in['b_fc1'], 'L0_xattn_w_fc2': _L0_xattn_in['w_fc2'], 'L0_xattn_b_fc2': _L0_xattn_in['b_fc2'], 'L1_xattn_Wq': _L1_xattn_in['Wq'], 'L1_xattn_bq': _L1_xattn_in['bq'], 'L1_xattn_Wk': _L1_xattn_in['Wk'], 'L1_xattn_bk': _L1_xattn_in['bk'], 'L1_xattn_Wv': _L1_xattn_in['Wv'], 'L1_xattn_bv': _L1_xattn_in['bv'], 'L1_xattn_Wo': _L1_xattn_in['Wo'], 'L1_xattn_bo': _L1_xattn_in['bo'], 'L1_xattn_gamma': _L1_xattn_in['gamma'], 'L1_xattn_beta': _L1_xattn_in['beta']}

def reference(x, ctx_2048, mask_Bx1xSxS2_ff0, L0_xattn_ln1_scale, L0_xattn_ln1_offset, L0_xattn_wq1, L0_xattn_bq1, L0_xattn_wk1, L0_xattn_bk1, L0_xattn_wv1, L0_xattn_bv1, L0_xattn_wo1, L0_xattn_bo1, L0_xattn_bias_k1, L0_xattn_bias_v1, L0_xattn_ln2_scale, L0_xattn_ln2_offset, L0_xattn_wq2, L0_xattn_bq2, L0_xattn_wk2, L0_xattn_bk2, L0_xattn_wv2, L0_xattn_bv2, L0_xattn_wo2, L0_xattn_bo2, L0_xattn_bias_k2, L0_xattn_bias_v2, L0_xattn_ln_mlp_scale, L0_xattn_ln_mlp_offset, L0_xattn_w_fc1, L0_xattn_b_fc1, L0_xattn_w_fc2, L0_xattn_b_fc2, L1_xattn_Wq, L1_xattn_bq, L1_xattn_Wk, L1_xattn_bk, L1_xattn_Wv, L1_xattn_bv, L1_xattn_Wo, L1_xattn_bo, L1_xattn_gamma, L1_xattn_beta):
    import jax
    import jax.numpy as jnp

    def _L0_xattn_ref(x, xf_1, xf_2, ln1_scale, ln1_offset, wq1, bq1, wk1, bk1, wv1, bv1, wo1, bo1, bias_k1, bias_v1, ln2_scale, ln2_offset, wq2, bq2, wk2, bk2, wv2, bv2, wo2, bo2, bias_k2, bias_v2, ln_mlp_scale, ln_mlp_offset, w_fc1, b_fc1, w_fc2, b_fc2):
        import jax, jax.numpy as jnp
        import numpy as np
        B, Q, S1, S2 = (4, 64, 512, 512)
        D, H, K, F = (512, 16, 128, 2048)
        LN_EPS = 1e-05

        def _layer_norm(x, scale, offset):
            mu = jnp.mean(x, axis=-1, keepdims=True)
            var = jnp.var(x, axis=-1, keepdims=True)
            return (x - mu) * jax.lax.rsqrt(var + LN_EPS) * scale + offset

        def _cross_attention(q_in, kv_in, wq, bq, wk, bk, wv, bv, wo, bo, bias_k, bias_v):
            b, q_len, _ = q_in.shape
            t = kv_in.shape[1]
            qh = (q_in @ wq + bq).reshape(b, q_len, H, K)
            kh = (kv_in @ wk + bk).reshape(b, t, H, K)
            vh = (kv_in @ wv + bv).reshape(b, t, H, K)
            kh = jnp.concatenate([kh, jnp.broadcast_to(bias_k, (b, 1, H, K))], axis=1)
            vh = jnp.concatenate([vh, jnp.broadcast_to(bias_v, (b, 1, H, K))], axis=1)
            scale = jnp.sqrt(jnp.asarray(K, q_in.dtype))
            logits = jnp.einsum('bqhk,bthk->bhqt', qh, kh) / scale
            weights = jax.nn.softmax(logits, axis=-1)
            ctx = jnp.einsum('bhqt,bthk->bqhk', weights, vh).reshape(b, q_len, H * K)
            return ctx @ wo + bo

        def _forward(x, xf_1, xf_2, ln1_scale, ln1_offset, wq1, bq1, wk1, bk1, wv1, bv1, wo1, bo1, bias_k1, bias_v1, ln2_scale, ln2_offset, wq2, bq2, wk2, bk2, wv2, bv2, wo2, bo2, bias_k2, bias_v2, ln_mlp_scale, ln_mlp_offset, w_fc1, b_fc1, w_fc2, b_fc2):
            res = x
            h = _layer_norm(x, ln1_scale, ln1_offset)
            x = res + _cross_attention(h, xf_1, wq1, bq1, wk1, bk1, wv1, bv1, wo1, bo1, bias_k1, bias_v1)
            res = x
            h = _layer_norm(x, ln2_scale, ln2_offset)
            x = res + _cross_attention(h, xf_2, wq2, bq2, wk2, bk2, wv2, bv2, wo2, bo2, bias_k2, bias_v2)
            h = _layer_norm(x, ln_mlp_scale, ln_mlp_offset)
            h = jax.nn.gelu(h @ w_fc1 + b_fc1, approximate=False) @ w_fc2 + b_fc2
            return x + h
        return _forward(x, xf_1, xf_2, ln1_scale, ln1_offset, wq1, bq1, wk1, bk1, wv1, bv1, wo1, bo1, bias_k1, bias_v1, ln2_scale, ln2_offset, wq2, bq2, wk2, bk2, wv2, bv2, wo2, bo2, bias_k2, bias_v2, ln_mlp_scale, ln_mlp_offset, w_fc1, b_fc1, w_fc2, b_fc2)

    def _L1_xattn_ref(hidden_state, encoder_hidden_state, encoder_attention_mask, Wq, bq, Wk, bk, Wv, bv, Wo, bo, gamma, beta):
        import jax, jax.numpy as jnp
        import numpy as np
        H = 512
        NH = 32
        KVH = 8
        HD = H // NH
        GROUPS = NH // KVH
        EPS = 1e-06
        B, L, S = (4, 256, 256)

        def _gqa_forward(hidden_state, encoder_hidden_state, encoder_attention_mask, Wq, bq, Wk, bk, Wv, bv, Wo, bo, gamma, beta):
            b, l, _ = hidden_state.shape
            s = encoder_hidden_state.shape[1]
            q = hidden_state @ Wq + bq
            k = encoder_hidden_state @ Wk + bk
            v = encoder_hidden_state @ Wv + bv
            q = q.reshape(b, l, KVH, GROUPS, HD).transpose(0, 2, 3, 1, 4)
            k = k.reshape(b, s, KVH, HD).transpose(0, 2, 1, 3)
            v = v.reshape(b, s, KVH, HD).transpose(0, 2, 1, 3)
            scale = 1.0 / jnp.sqrt(jnp.asarray(HD, q.dtype))
            scores = jnp.einsum('bkgld,bksd->bkgls', q, k) * scale
            scores = scores + encoder_attention_mask[:, :, None, :, :]
            attn = jax.nn.softmax(scores, axis=-1)
            out = jnp.einsum('bkgls,bksd->bkgld', attn, v)
            out = out.transpose(0, 3, 1, 2, 4).reshape(b, l, H)
            out = out @ Wo + bo
            x = out + hidden_state
            mu = jnp.mean(x, axis=-1, keepdims=True)
            var = jnp.var(x, axis=-1, keepdims=True)
            return (x - mu) * jax.lax.rsqrt(var + EPS) * gamma + beta
        return _gqa_forward(hidden_state, encoder_hidden_state, encoder_attention_mask, Wq, bq, Wk, bk, Wv, bv, Wo, bo, gamma, beta)
    x = _L0_xattn_ref(x, ctx_2048, ctx_2048, L0_xattn_ln1_scale, L0_xattn_ln1_offset, L0_xattn_wq1, L0_xattn_bq1, L0_xattn_wk1, L0_xattn_bk1, L0_xattn_wv1, L0_xattn_bv1, L0_xattn_wo1, L0_xattn_bo1, L0_xattn_bias_k1, L0_xattn_bias_v1, L0_xattn_ln2_scale, L0_xattn_ln2_offset, L0_xattn_wq2, L0_xattn_bq2, L0_xattn_wk2, L0_xattn_bk2, L0_xattn_wv2, L0_xattn_bv2, L0_xattn_wo2, L0_xattn_bo2, L0_xattn_bias_k2, L0_xattn_bias_v2, L0_xattn_ln_mlp_scale, L0_xattn_ln_mlp_offset, L0_xattn_w_fc1, L0_xattn_b_fc1, L0_xattn_w_fc2, L0_xattn_b_fc2)
    x = _L1_xattn_ref(x, ctx_2048, mask_Bx1xSxS2_ff0, L1_xattn_Wq, L1_xattn_bq, L1_xattn_Wk, L1_xattn_bk, L1_xattn_Wv, L1_xattn_bv, L1_xattn_Wo, L1_xattn_bo, L1_xattn_gamma, L1_xattn_beta)
    return x

_drawn_inputs = setup_inputs


def setup_inputs(seed=0):
    import zlib

    import numpy as np

    out = dict(_drawn_inputs(seed))
    spreads = {'L0_xattn_ln1_scale': (1.0, 0.6),
     'L0_xattn_ln1_offset': (0.0, 0.8),
     'L0_xattn_bq1': (0.0, 0.8),
     'L0_xattn_bk1': (0.0, 2.0),
     'L0_xattn_bv1': (0.0, 0.1),
     'L0_xattn_bo1': (0.0, 0.1),
     'L0_xattn_ln2_scale': (1.0, 0.6),
     'L0_xattn_ln2_offset': (0.0, 0.8),
     'L0_xattn_bq2': (0.0, 0.8),
     'L0_xattn_bk2': (0.0, 2.0),
     'L0_xattn_bv2': (0.0, 0.1),
     'L0_xattn_bo2': (0.0, 0.1),
     'L0_xattn_ln_mlp_scale': (1.0, 0.2),
     'L0_xattn_ln_mlp_offset': (0.0, 0.359),
     'L0_xattn_b_fc1': (0.0, 0.1),
     'L0_xattn_b_fc2': (0.0, 0.1),
     'L1_xattn_bq': (0.0, 0.8),
     'L1_xattn_bk': (0.0, 2.0),
     'L1_xattn_bv': (0.0, 0.1),
     'L1_xattn_bo': (0.0, 0.1),
     'L1_xattn_gamma': (1.0, 0.2),
     'L1_xattn_beta': (0.0, 0.1)}
    factors = {'L0_xattn_wq1': 3.835,
     'L0_xattn_wk1': 3.746,
     'L0_xattn_bias_k1': 64.0,
     'L0_xattn_bias_v1': 64.0,
     'L0_xattn_wq2': 3.963,
     'L0_xattn_wk2': 3.891,
     'L0_xattn_bias_k2': 64.0,
     'L0_xattn_bias_v2': 64.0,
     'L1_xattn_Wq': 7.558,
     'L1_xattn_Wk': 7.371}
    for name, (base, spread) in spreads.items():
        noise = np.random.default_rng([zlib.crc32(name.encode()), seed]).standard_normal(out[name].shape)
        drawn = base * np.exp(spread * noise) if base else spread * noise
        out[name] = jnp.asarray(drawn.astype(out[name].dtype))
    for name, factor in factors.items():
        out[name] = (out[name] * factor).astype(out[name].dtype)
    return out
```

```python
from contextlib import ExitStack

import numpy as np
import concourse.bass as bass
from concourse import mybir
from concourse.alu_op_type import AluOpType as ALU

F32 = mybir.dt.float32
F32R = mybir.dt.float32r
ACT = mybir.ActivationFunctionType
AX = mybir.AxisListType

P = 128
B, S, D = 8, 112, 512
T = 375
T1 = T + 1
C = D // P
LAYERS = 2
H, HD = 16, 128
G = 4
HG = H // G
TILES = [(0, 128), (128, 128), (256, T1 - 256)]
NT = len(TILES)
F = 2048
MG = F // D
FT = D // P
KV, HS = 8, 16
J = 4
HB = B // 2
SETS = LAYERS * G
BODIES = SETS * B
MLP_BLOCK = SETS * 4
LAST_BLOCK = MLP_BLOCK + 2 * MG
SCALE0 = float(HD) ** -0.5
SCALE1 = float(HS) ** -0.5
EPS0, EPS1 = 1e-5, 1e-6
CREDIT = 8
LN_STEPS = 2 * B + 6
PASSES = ((0, 0), (0, 1), (1, 0))

P_BK, P_BIASK, P_LAYER = 0, H, 2 * H
P_NORM = LAYERS * P_LAYER
P_FC1 = P_NORM + 3 * 2 * C
P_BK1 = P_FC1 + F // P
P_MASK = P_BK1 + 1
P_ALL = P_MASK + KV


def build(nc, x_d, ctx_d, mask_d, w_d, wkv_d, par_d, rows_d, wrow_d, gb_d, out_d, stop_after=None):
    st = ExitStack()
    with st:
        def sb(name, shape, dt=F32):
            return st.enter_context(nc.sbuf_tensor(name, shape, dt))

        def sem(name):
            return st.enter_context(nc.semaphore(name))

        bank = [st.enter_context(nc.psum_tensor(f"bank{i}", [P, 512], F32)) for i in range(8)]
        k_ps, s_ps, t_ps, o_ps, a_ps, b_ps = bank[0:2], bank[2:4], bank[4], bank[5], bank[6], bank[7]
        x_sb = sb("x_sb", [S, B, D])
        hT = sb("hT", [P, C, B, S])
        w_split = sb("w_split", [P, 4, 2, 4 * D], F32R)
        w_raw = sb("w_raw", [P, 2, 4 * D])
        ctx_raw = sb("ctx_raw", [P, 2, C, T])

        sizes = [2 * 2 * C * T1, 2 * C * S, 2 * HG * S, 2 * 2 * T1, 2 * HG * S]
        arena_r = sb("arena_r", [P, sum(sizes)], F32R)
        at = [sum(sizes[:i]) for i in range(6)]
        ctx_s = arena_r[:, at[0]:at[1]].rearrange("p (s l c t) -> p s l c t", s=2, l=2, c=C)
        hb_s = arena_r[:, at[1]:at[2]].rearrange("p (l c q) -> p l c q", l=2, c=C)
        qT_s = arena_r[:, at[2]:at[3]].rearrange("p (l h q) -> p l h q", l=2, h=HG)
        kT_s = arena_r[:, at[3]:at[4]].rearrange("p (s l t) -> p s l t", s=2, l=2)
        oT_s = arena_r[:, at[4]:at[5]].rearrange("p (l h q) -> p l h q", l=2, h=HG)
        half_ctx = at[1] // 2
        hm_s = arena_r[:, half_ctx:half_ctx + 2 * C * B * S].rearrange("p (l c n) -> p l c n", l=2, c=C)
        g_s = w_split[:, 2:4].rearrange("p k l n -> p (k l n)")[:, 0:2 * FT * B * S].rearrange(
            "p (l f n) -> p l f n", l=2, f=FT)

        kbias_s = sb("kbias_s", [P, 2, H], F32R)
        DIAG = HS * (KV + 1) * KV
        v_all = sb("v_all", [P, 2 * NT * D + DIAG - KV * P])
        v_sb = v_all[:, 0:2 * NT * D].rearrange("p (s i n) -> p s i n", s=2, i=NT)
        q_sb = sb("q_sb", [S, D])
        p_sb = sb("p_sb", [S, 2 * J, NT * P])
        pT_sb = sb("pT_sb", [P, 2, NT * S])
        hn = v_sb[0:S, 0, 0:2, :]
        gelu = v_sb[:, 0, 0:2, 0:HB * S]
        ident = sb("ident", [P, P])
        par = sb("par", [P, P_ALL])
        wrow = sb("wrow", [P, 3, D])
        bo_bc = sb("bo_bc", [S, D])
        stats = sb("stats", [S, B, 6])
        mv = sb("mv", [S, B, 2])
        rstd = sb("rstd", [S, 3, B])
        nmax = sb("nmax", [S, 2, J])
        rmax = sb("rmax", [S, 2, J])
        zsum = sb("zsum", [S, 2, J])
        rz = sb("rz", [S, 2, J])
        wkv_raw = w_raw[:, 0, 0:2 * C * P].rearrange("p (k c n) -> p k c n", k=2, c=C)
        pT1 = w_raw[:, :, :].rearrange("p s n -> p (s n)")[:, 2 * C * P:2 * C * P + 2 * NT * HB * S].rearrange(
            "p (s i n) -> p s i n", s=2, i=NT)
        wk1_s = w_split[:, 2, 0, 0:2 * C * P].rearrange("p (l c n) -> p l c n", l=2, c=C)
        v_wide = v_all[:, 0:NT * KV * P].rearrange("p (i k n) -> p i k n", i=NT, k=KV)
        kb_sb = sb("kb_sb", [P, T])
        mask_sb = sb("mask_sb", [S, 2, T])
        gb = hT[:, :, :, :].rearrange("p c b q -> p (c b q)")[0:S, 0:2 * D].rearrange("p (k n) -> p k n", k=2)

        x_loaded, par_loaded, out_stored, consts = sem("x_loaded"), sem("par_loaded"), sem("out_stored"), sem("consts")
        waited = sem("waited")
        ctx_loaded = [sem("ctx_loaded0"), sem("ctx_loaded1")]
        w_loaded = [sem("w_loaded0"), sem("w_loaded1")]
        mask_loaded = [sem("mask_loaded0"), sem("mask_loaded1")]
        bo_loaded, wrow_loaded, gb_loaded, wkv_loaded = sem("bo_loaded"), sem("wrow_loaded"), sem("gb_loaded"), sem("wkv_loaded")
        by_pe = {n: sem(n) for n in ("q_mm", "qt_mm", "k_mm", "s_mm", "t_mm", "pv_mm", "v_mm", "y_mm", "ht_mm",
                                     "fc1_mm", "fc2_mm", "vc_mm", "kc_mm", "s1_mm", "t1_mm", "pv1_mm")}
        by_act = {n: sem(n) for n in ("w_hi", "ctx_hi", "hb_hi", "qt_hi", "k_hi", "exp_done", "pt_out", "o_hi", "root",
                                      "ht_even", "hm_hi", "gelu_done", "g_hi", "k1_hi", "exp1", "pt1_out")}
        by_dve = {n: sem(n) for n in ("w_lo", "ctx_lo", "hb_lo", "q_out", "qt_lo", "k_lo", "max_done", "z_inv", "p_norm",
                                      "v_out", "o_lo", "y_add", "ln_step", "hn_out", "ht_odd", "kbias", "hm_lo", "g_lo",
                                      "kb_out", "vc_out", "k1_lo", "rmax1", "nmax1", "z1_inv", "p1_norm", "m_add", "fin")}
        by_pool = {n: sem(n) for n in ("k_col", "v_row", "bo_add", "pool_step", "wide_zero")}
        q_mm, qt_mm, k_mm, s_mm, t_mm, pv_mm, v_mm, y_mm, ht_mm, fc1_mm, fc2_mm, vc_mm, kc_mm, s1_mm, t1_mm, pv1_mm = by_pe.values()
        (w_hi, ctx_hi, hb_hi, qt_hi, k_hi, exp_done, pt_out, o_hi, root, ht_even, hm_hi, gelu_done, g_hi, k1_hi, exp1,
         pt1_out) = by_act.values()
        (w_lo, ctx_lo, hb_lo, q_out, qt_lo, k_lo, max_done, z_inv, p_norm, v_out, o_lo, y_add, ln_step, hn_out, ht_odd,
         kbias, hm_lo, g_lo, kb_out, vc_out, k1_lo, rmax1, nmax1, z1_inv, p1_norm, m_add, fin) = by_dve.values()
        k_col, v_row, bo_add, pool_step, wide_zero = by_pool.values()

        def credit(eng, sems):
            for s in sems.values():
                eng.sem_inc(s, CREDIT)

        def settle(eng):
            eng.sem_inc(waited, 1)

        def f32(ap):
            return ap.bitcast(F32)

        def w_of(kind, lo):
            return w_split[:, kind, lo, :].rearrange("p (c n) -> p c n", c=4)

        WV, WQ, WK, WO = range(4)
        W1, W2 = 0, 1
        LQ, LO = 0, 1

        block = st.enter_context(nc.Block())

        @block.sync
        def _(sp):
            def context(n, b, slot):
                sp.wait_ge(ctx_lo, n - 1 + CREDIT)
                sp.dma_start(ctx_raw[:, slot], ctx_d[b]).then_inc(ctx_loaded[slot], 16)

            sp.dma_start(x_sb[:, :, :], x_d.rearrange("b s d -> s b d")).then_inc(x_loaded, 16)
            sp.dma_start(par[:, :], par_d).then_inc(par_loaded, 16)
            for s in range(2):
                sp.dma_start(ctx_raw[:, s], ctx_d[s]).then_inc(ctx_loaded[s], 16)
                sp.dma_start(w_raw[:, s, :], w_d[s]).then_inc(w_loaded[s], 16)
            with sp.Fori(0, LAYERS) as lay:
                sp.wait_ge(bo_add, lay * B + CREDIT)
                sp.dma_start(bo_bc[:, :], rows_d[lay, :].partition_broadcast(S)).then_inc(bo_loaded, 16)
                with sp.Fori(0, G) as g:
                    w = lay * G + g
                    sp.wait_ge(q_out, w * B + CREDIT)
                    sp.wait_ge(v_out, w * B * NT + CREDIT)
                    sp.wait_ge(v_row, w * B + CREDIT)
                    sp.dma_start(wrow[:, :, :], wrow_d[w].partition_broadcast(P)).then_inc(wrow_loaded, 16)
                    for j in range(2, 6):
                        sp.wait_ge(w_lo, 16 * w + 4 * (j - 1) + CREDIT)
                        sp.dma_start(w_raw[:, j % 2, :], w_d[4 * w + j]).then_inc(w_loaded[j % 2], 16)
                    with sp.Fori(0, B // 2 - 1) as bp:
                        for bb in range(2):
                            context(w * B + 2 * bp + bb + 2, 2 * bp + bb + 2, bb)
                    for bb in range(2):
                        context(w * B + B + bb, bb, bb)
            if stop_after == "L0":
                sp.wait_ge(y_add, BODIES + CREDIT)
                sp.dma_start(out_d.rearrange("b s d -> s b d"), x_sb[:, :, :]).then_inc(out_stored, 16)
                sp.wait_ge(out_stored, 16)
                for s in range(2):
                    sp.wait_ge(ctx_loaded[s], 16 * (BODIES // 2 + 1))
                    sp.wait_ge(w_loaded[s], 16 * (MLP_BLOCK // 2 + 1))
                return
            sp.wait_ge(bo_add, LAYERS * B + CREDIT)
            sp.dma_start(bo_bc[:, :], rows_d[LAYERS, :].partition_broadcast(S)).then_inc(bo_loaded, 16)
            with sp.Fori(0, MG) as m:
                for j in range(2):
                    sp.wait_ge(w_lo, 4 * (MLP_BLOCK + 2 * m + j + 1) + CREDIT)
                    sp.dma_start(w_raw[:, j, :], w_d[MLP_BLOCK + 2 * m + j + 2]).then_inc(w_loaded[j], 16)
            sp.wait_ge(bo_add, (LAYERS + 1) * B + CREDIT)
            sp.dma_start(bo_bc[:, :], rows_d[LAYERS + 1, :].partition_broadcast(S)).then_inc(bo_loaded, 16)
            sp.dma_start(wrow[:, :, :], wrow_d[SETS].partition_broadcast(P)).then_inc(wrow_loaded, 16)
            for s in range(2):
                sp.dma_start(mask_sb[:, s, :], mask_d[s]).then_inc(mask_loaded[s], 16)
            sp.wait_ge(w_lo, 4 * (LAST_BLOCK + 1) + CREDIT)
            sp.dma_start(wkv_raw, wkv_d).then_inc(wkv_loaded, 16)
            with sp.Fori(1, B // 2) as t:
                for bb in range(2):
                    i = 2 * t + bb
                    sp.wait_ge(vc_mm, i - 1 + CREDIT)
                    settle(sp)
                    context(BODIES + i, i, bb)
                    sp.wait_ge(rmax1, KV * J * (i - 1) + CREDIT)
                    sp.dma_start(mask_sb[:, bb, :], mask_d[i]).then_inc(mask_loaded[bb], 16)
            sp.wait_ge(hb_lo, BODIES + B + CREDIT)
            sp.dma_start(gb, gb_d.partition_broadcast(S)).then_inc(gb_loaded, 16)
            for b in range(B):
                sp.wait_ge(fin, b + 1 + CREDIT)
                sp.dma_start(out_d[b], x_sb[:, b, :]).then_inc(out_stored, 16)
            sp.wait_ge(out_stored, 16 * B)

        @block.gpsimd
        def _(pool):
            credit(pool, by_pool)
            pool.memset(ident[:, :], 0.0).then_inc(pool_step, 1)
            pool.wait_ge(pool_step, 1 + CREDIT)
            pool.affine_select(out=ident[:, :], in_=ident[:, :], compare_op=ALU.not_equal, fill=1.0, base=0,
                               pattern=[[-1, P]], channel_multiplier=1).then_inc(consts, 1)
            for s in range(2):
                pool.memset(f32(ctx_s[:, s, :, :, 0:1]), 0.0).then_inc(consts, 1)
                pool.memset(p_sb[:, s, T1:NT * P], 0.0).then_inc(consts, 1)

            def add_bias_rows(times):
                pool.wait_ge(bo_loaded, (times + 1) * 16)
                for b in range(B):
                    pool.wait_ge(hn_out, times * B + b + 1 + CREDIT)
                    pool.tensor_tensor(x_sb[:, b, :], x_sb[:, b, :], bo_bc[:, :], ALU.add).then_inc(bo_add, 1)

            def body(n, bb, g):
                pool.wait_ge(v_out, NT * n + 1 + CREDIT)
                settle(pool)
                pool.tensor_copy(v_sb[0:1, bb, 0, :], wrow[0:1, 2, :]).then_inc(v_row, 1)
                for h in range(HG):
                    pool.wait_ge(s_mm, HG * n + h - 1 + CREDIT)
                    settle(pool)
                    pool.tensor_copy(kT_s[:, h % 2, :, 0:1], f32(kbias_s[:, :, bass.ds(g * HG + h, 1)])).then_inc(k_col, 1)

            with pool.Fori(0, LAYERS) as lay:
                add_bias_rows(lay)
                pool.wait_ge(kbias, 2 * lay + 2 + CREDIT)
                settle(pool)
                with pool.Fori(0, G) as g:
                    w = lay * G + g
                    pool.wait_ge(wrow_loaded, (w + 1) * 16)
                    settle(pool)
                    with pool.Fori(0, B // 2) as bp:
                        for bb in range(2):
                            body(w * B + bp * 2 + bb, bb, g)
            if stop_after == "L0":
                return
            add_bias_rows(LAYERS)
            pool.wait_ge(fc2_mm, MG * B + CREDIT)
            pool.wait_ge(g_lo, MG * FT * 2 + CREDIT)
            pool.memset(v_all[:, :], 0.0).then_inc(wide_zero, 1)
            for s in range(2 * J):
                pool.memset(p_sb[:, s, T:NT * P], 0.0).then_inc(wide_zero, 1)
            pool.wait_ge(bo_loaded, (LAYERS + 2) * 16)
            for b in range(B):
                pool.wait_ge(ht_mm, LAYERS * B + B + b + 1 + CREDIT)
                pool.tensor_tensor(x_sb[:, b, :], x_sb[:, b, :], bo_bc[:, :], ALU.add).then_inc(bo_add, 1)

        @block.scalar
        def _(act):
            credit(act, by_act)
            act.wait_ge(par_loaded, 16)

            def split_block(kind, slot, loads, chunks=range(4)):
                act.wait_ge(w_loaded[slot], loads * 16)
                for c in chunks:
                    cols = slice(c * D, (c + 1) * D)
                    act.activation(w_split[:, kind, 0, cols], w_raw[:, slot, cols], ACT.Copy).then_inc(w_hi, 1)

            def split_context(n, slot, loads):
                act.wait_ge(ctx_loaded[slot], 16 * loads)
                act.wait_ge(k_mm, HG * (n - 1) + CREDIT)
                act.activation(ctx_s[:, slot, 0, :, 1:T1], ctx_raw[:, slot], ACT.Copy).then_inc(ctx_hi, 1)

            def split_h(n, b):
                act.wait_ge(q_mm, n + CREDIT)
                settle(act)
                act.activation(hb_s[:, 0], hT[:, :, b, :], ACT.Copy).then_inc(hb_hi, 1)

            def key_hi(n, h, lay, g):
                act.wait_ge(k_mm, HG * n + h + 1 + CREDIT)
                act.wait_ge(s_mm, HG * n + h - 1 + CREDIT)
                settle(act)
                act.activation(kT_s[:, h % 2, 0, 1:T1], k_ps[h % 2][:, 1:T1], ACT.Identity,
                               bias=par[:, bass.ds(lay * P_LAYER + P_BK + g * HG + h, 1)]).then_inc(k_hi, 1)

            def exps(n, h):
                act.wait_ge(max_done, HG * n + h + 1 + CREDIT)
                act.wait_ge(t_mm, HG * n + h - 1 + CREDIT)
                act.activation(p_sb[:, h % 2, 0:T1], s_ps[h % 2][0:S, 0:T1], ACT.Exp, bias=nmax[:, 0, h:h + 1],
                               accum_out=zsum[:, 0, h:h + 1]).then_inc(exp_done, 1)

            def probs_out(n, h):
                act.wait_ge(t_mm, HG * n + h + 1 + CREDIT)
                act.wait_ge(pv_mm, HG * n + h - 1 + CREDIT)
                act.activation(pT_sb[:, h % 2, :], t_ps[:, 0:NT * S], ACT.Copy).then_inc(pt_out, 1)

            def heads_hi(n):
                act.wait_ge(pv_mm, HG * (n + 1) + CREDIT)
                act.wait_ge(y_mm, n + CREDIT)
                act.activation(oT_s[:, 0], o_ps[:, 0:HG * S].rearrange("p (h q) -> p h q", h=HG),
                               ACT.Copy).then_inc(o_hi, 1)

            def queries_hi(n, bk, scale):
                act.wait_ge(qt_mm, n + 1 + CREDIT)
                act.activation(qT_s[:, 0], bk[:, 0:HG * S].rearrange("p (h q) -> p h q", h=HG), ACT.Copy,
                               scale=scale).then_inc(qt_hi, 1)

            def body(n, bb, b, lay, g, w, loads, last):
                split_context(n + 1, 1 - bb, loads)
                key_hi(n, 0, lay, g)
                queries_hi(n, b_ps, SCALE0)
                key_hi(n, 1, lay, g)
                if not last:
                    split_h(n + 1, b + 1)
                exps(n, 0)
                key_hi(n, 2, lay, g)
                exps(n, 1)
                probs_out(n, 0)
                key_hi(n, 3, lay, g)
                if last:
                    split_block(WV, 0, 2 * w + 3)
                probs_out(n, 1)
                exps(n, 2)
                probs_out(n, 2)
                exps(n, 3)
                probs_out(n, 3)
                heads_hi(n)
                if last:
                    split_block(WQ, 1, 2 * w + 3)

            def norm(times):
                act.wait_ge(ln_step, LN_STEPS * times + 2 * B + 1 + CREDIT)
                act.activation(rstd[:, 1, :], rstd[:, 0, :], ACT.Sqrt).then_inc(root, 1)

            def input_out(times, par_at):
                for i in range(B // 2):
                    act.wait_ge(ht_mm, times * B + 2 * i + 1 + CREDIT)
                    settle(act)
                    for c in range(C):
                        cols = a_ps[:, c * S:(c + 1) * S]
                        if par_at is None:
                            act.activation(hT[:, c, 2 * i, :], cols, ACT.Copy).then_inc(ht_even, 1)
                        else:
                            act.activation(hT[:, c, 2 * i, :], cols, ACT.Identity,
                                           scale=par[:, bass.ds(par_at + c, 1)],
                                           bias=par[:, bass.ds(par_at + C + c, 1)]).then_inc(ht_even, 1)

            split_context(0, 0, 1)
            split_block(WV, 0, 1)
            split_block(WQ, 1, 1)
            with act.Fori(0, LAYERS) as lay:
                norm(lay)
                input_out(lay, P_NORM + lay * 2 * C)
                with act.Fori(0, G) as g:
                    w = lay * G + g
                    split_block(WK, 0, 2 * w + 2)
                    act.wait_ge(ht_even, B * C // 2 * (lay + 1) + CREDIT)
                    act.wait_ge(ht_odd, B * C // 2 * (lay + 1) + CREDIT)
                    split_h(w * B, 0)
                    act.wait_ge(y_mm, B * w + CREDIT)
                    split_block(WO, 1, 2 * w + 2)
                    with act.Fori(0, B // 2 - 1) as bp:
                        t = w * (B // 2) + bp
                        for bb in range(2):
                            body(2 * t + bb, bb, 2 * bp + bb, lay, g, w, t + 1 + bb, False)
                    t = w * (B // 2) + B // 2 - 1
                    for bb in range(2):
                        body(2 * t + bb, bb, B - 2 + bb, lay, g, w, t + 1 + bb, bb == 1)
            if stop_after == "L0":
                return

            norm(LAYERS)
            input_out(LAYERS, P_NORM + LAYERS * 2 * C)
            act.wait_ge(ht_even, B * C // 2 * (LAYERS + 1) + CREDIT)
            act.wait_ge(ht_odd, B * C // 2 * (LAYERS + 1) + CREDIT)
            act.wait_ge(y_mm, BODIES + CREDIT)
            for c in range(C):
                for half in range(2):
                    cols = slice(half * HB * S, (half + 1) * HB * S)
                    act.activation(hm_s[:, 0, c, cols], hT[:, c, half * HB:(half + 1) * HB, :].rearrange("p b q -> p (b q)"),
                                   ACT.Copy).then_inc(hm_hi, 1)
            with act.Fori(0, MG) as m:
                for half in range(2):
                    for f in range(FT):
                        k = half * FT + f
                        cols = slice(half * HB * S, (half + 1) * HB * S)
                        act.wait_ge(fc1_mm, 2 * FT * m + k + 1 + CREDIT)
                        act.wait_ge(g_lo, 2 * FT * m + k - 1 + CREDIT)
                        settle(act)
                        act.activation(gelu[:, k % 2, :], bank[k % 4][:, 0:HB * S], ACT.Gelu,
                                       bias=par[:, bass.ds(P_FC1 + m * FT + f, 1)]).then_inc(gelu_done, 1)
                        act.wait_ge(gelu_done, 2 * FT * m + k + 1 + CREDIT)
                        act.activation(g_s[:, 0, f, cols], gelu[:, k % 2, :], ACT.Copy).then_inc(g_hi, 1)
                split_block(W1, 0, MLP_BLOCK // 2 + m + 2)
                act.wait_ge(fc2_mm, B * (m + 1) + CREDIT)
                split_block(W2, 1, MLP_BLOCK // 2 + m + 2)

            input_out(LAYERS + 1, None)
            act.wait_ge(ht_even, B * C // 2 * (LAYERS + 2) + CREDIT)
            act.wait_ge(ht_odd, B * C // 2 * (LAYERS + 2) + CREDIT)
            act.wait_ge(wkv_loaded, 16)
            act.activation(wk1_s[:, 0].rearrange("p c n -> p (c n)"), wkv_raw[:, 0].rearrange("p c n -> p (c n)"),
                           ACT.Copy).then_inc(w_hi, 1)

            def key1_hi(i, kv):
                act.wait_ge(kb_out, i + 1 + CREDIT)
                act.wait_ge(s1_mm, J * (KV * i + kv - 1) + CREDIT)
                act.activation(kT_s[:, kv % 2, 0, 1:T1], kb_sb[:, :], ACT.Copy,
                               scale=par[:, P_MASK + kv:P_MASK + kv + 1]).then_inc(k1_hi, 1)

            def exps1(i, kv):
                act.wait_ge(nmax1, KV * i + kv + 1 + CREDIT)
                for j in range(J):
                    slot = p_sb[:, kv % 2 * J + j, 0:T]
                    act.activation(slot, slot, ACT.Exp, bias=nmax[:, kv % 2, j:j + 1],
                                   accum_out=zsum[:, kv % 2, j:j + 1]).then_inc(exp1, 1)

            def probs1_out(i, kv):
                act.wait_ge(pv1_mm, KV * i + kv - 1 + CREDIT)
                for t in range(NT):
                    act.wait_ge(t1_mm, NT * (KV * i + kv) + t + 1 + CREDIT)
                    act.activation(pT1[:, kv % 2, t, :], (t_ps, a_ps, b_ps)[t][:, 0:J * S], ACT.Copy).then_inc(pt1_out, 1)

            def body1(i, slot, loads, last):
                n = BODIES + i
                split_h(n, i)
                key1_hi(i, 0)
                key1_hi(i, 1)
                queries_hi(n, t_ps, SCALE1)
                for kv in range(KV):
                    exps1(i, kv)
                    if kv >= 1:
                        probs1_out(i, kv - 1)
                    if kv + 2 < KV:
                        key1_hi(i, kv + 2)
                    if kv == 2 and not last:
                        split_context1(n + 1, i + 1, 1 - slot, loads)
                probs1_out(i, KV - 1)
                act.wait_ge(pv1_mm, KV * (i + 1) + CREDIT)
                act.wait_ge(y_mm, n + CREDIT)
                act.activation(oT_s[:, 0], o_ps[:, 0:J * S].rearrange("p (h q) -> p h q", h=J), ACT.Copy).then_inc(o_hi, 1)

            def split_context1(n, i, slot, loads):
                act.wait_ge(ctx_loaded[slot], 16 * loads)
                act.wait_ge(kc_mm, i - 1 + CREDIT)
                act.activation(ctx_s[:, slot, 0, :, 1:T1], ctx_raw[:, slot], ACT.Copy).then_inc(ctx_hi, 1)

            with act.Fori(0, B // 2 - 1) as t:
                for bb in range(2):
                    body1(2 * t + bb, bb, BODIES // 2 + t + 1 + bb, False)
            for bb in range(2):
                body1(B - 2 + bb, bb, BODIES // 2 + B // 2 + bb, bb == 1)
            norm(LAYERS + 1)

        @block.tensor
        def _(pe):
            credit(pe, by_pe)
            pe.wait_ge(consts, 5)

            def product(out, pairs, part=None):
                for i in part or range(len(pairs)):
                    l, r = pairs[i]
                    for k, (a, b) in enumerate(PASSES):
                        mm = pe.matmul(out, l(a), r(b), start=(i == 0 and k == 0),
                                       stop=(i == len(pairs) - 1 and k == len(PASSES) - 1))
                return mm

            def values(n, i, slot, w, part=None):
                first, rows = TILES[i]
                if i == 0:
                    pe.wait_ge(ctx_lo, n + 1 + CREDIT)
                    pe.wait_ge(w_lo, 16 * w + 4 + CREDIT)
                out = (a_ps, b_ps, a_ps)[i]
                if i == 2 and (part is None or 0 in part):
                    pe.wait_ge(v_out, NT * n + 1 + CREDIT)
                mm = product(out[0:rows, :], [
                    (lambda l, c=c: ctx_s[:, slot, l, c, first:first + rows], lambda l, c=c: w_of(WV, l)[:, c, :])
                    for c in range(C)], part)
                if part is None or C - 1 in part:
                    mm.then_inc(v_mm, 1)

            def queries(n, kind):
                pe.wait_ge(hb_lo, n + 1 + CREDIT)
                product(a_ps[0:S, :], [(lambda l, c=c: hb_s[:, l, c, :], lambda l, c=c: w_of(kind, l)[:, c, :])
                                       for c in range(C)]).then_inc(q_mm, 1)

            def queries_turn(n, out):
                pe.wait_ge(q_out, n + 1 + CREDIT)
                for h in range(HG):
                    mm = pe.transpose(out[:, h * S:(h + 1) * S], q_sb[:, h * P:(h + 1) * P], ident[0:S, 0:S])
                mm.then_inc(qt_mm, 1)

            def keys(n, h, slot):
                pe.wait_ge(k_lo, HG * n + h - 1 + CREDIT)
                product(k_ps[h % 2][:, 0:T1], [
                    (lambda l, c=c: w_of(WK, l)[:, c, h * P:(h + 1) * P], lambda l, c=c: ctx_s[:, slot, l, c, :])
                    for c in range(C)]).then_inc(k_mm, 1)

            def scores(n, h):
                pe.wait_ge(qt_lo, n + 1 + CREDIT)
                pe.wait_ge(k_lo, HG * n + h + 1 + CREDIT)
                pe.wait_ge(k_col, HG * n + h + 1 + CREDIT)
                pe.wait_ge(exp_done, HG * n + h - 1 + CREDIT)
                product(s_ps[h % 2][0:S, 0:T1], [(lambda l: qT_s[:, l, h, :], lambda l: kT_s[:, h % 2, l, :])]).then_inc(s_mm, 1)

            def probs_turn(n, h):
                pe.wait_ge(p_norm, HG * n + h + 1 + CREDIT)
                pe.wait_ge(pt_out, HG * n + h + CREDIT)
                for t in range(NT):
                    mm = pe.transpose(t_ps[:, t * S:(t + 1) * S], p_sb[:, h % 2, t * P:(t + 1) * P], ident[0:S, 0:S])
                mm.then_inc(t_mm, 1)

            def head_out(n, h, slot):
                pe.wait_ge(pt_out, HG * n + h + 1 + CREDIT)
                if h == 0:
                    pe.wait_ge(v_out, NT * (n + 1) + CREDIT)
                    pe.wait_ge(v_row, n + 1 + CREDIT)
                    pe.wait_ge(o_lo, n + CREDIT)
                for t, (_, rows) in enumerate(TILES):
                    mm = pe.matmul(o_ps[:, h * S:(h + 1) * S], v_sb[0:rows, slot, t, h * P:(h + 1) * P],
                                   pT_sb[0:rows, h % 2, t * S:(t + 1) * S], start=(t == 0), stop=(t == NT - 1))
                mm.then_inc(pv_mm, 1)

            def project(n, kind):
                pe.wait_ge(o_lo, n + 1 + CREDIT)
                product(b_ps[0:S, :], [(lambda l, h=h: oT_s[:, l, h, :], lambda l, h=h: w_of(kind, l)[:, h, :])
                                       for h in range(HG)]).then_inc(y_mm, 1)

            def body(n, bb, w, last):
                if bb == 0:
                    pe.wait_ge(w_lo, 16 * w + 8 + CREDIT)
                pe.wait_ge(v_out, NT * (n + 1) + CREDIT)
                queries(n, WQ)
                pe.wait_ge(w_lo, 16 * w + 12 + CREDIT)
                keys(n, 0, bb)
                pe.wait_ge(y_add, n + CREDIT)
                queries_turn(n, b_ps)
                keys(n, 1, bb)
                scores(n, 0)
                keys(n, 2, bb)
                scores(n, 1)
                probs_turn(n, 0)
                keys(n, 3, bb)
                head_out(n, 0, bb)
                probs_turn(n, 1)
                scores(n, 2)
                if not last:
                    values(n + 1, 0, 1 - bb, w)
                head_out(n, 1, bb)
                probs_turn(n, 2)
                scores(n, 3)
                if not last:
                    values(n + 1, 1, 1 - bb, w)
                head_out(n, 2, bb)
                probs_turn(n, 3)
                if not last:
                    values(n + 1, 2, 1 - bb, w, range(0, 1))
                head_out(n, 3, bb)
                if not last:
                    values(n + 1, 2, 1 - bb, w, range(1, C))
                pe.wait_ge(w_lo, 16 * w + 16 + CREDIT)
                if not last:
                    pe.wait_ge(v_out, NT * (n + 1) + 2 + CREDIT)
                project(n, WO)

            def turn_input(times, plain=False):
                for b in range(B):
                    if plain:
                        pe.wait_ge(m_add, B * (MG - 1) + b + 1 + CREDIT)
                    else:
                        pe.wait_ge(hn_out, times * B + b + 1 + CREDIT)
                    if b % 2:
                        pe.wait_ge(ht_odd, C * (times * B // 2 + b // 2) + CREDIT)
                    else:
                        pe.wait_ge(ht_even, C * (times * B // 2 + b // 2) + CREDIT)
                    for c in range(C):
                        src = x_sb[:, b, c * P:(c + 1) * P] if plain else hn[:, b % 2, c * P:(c + 1) * P]
                        mm = pe.transpose((a_ps, b_ps)[b % 2][:, c * S:(c + 1) * S], src, ident[0:S, 0:S])
                    mm.then_inc(ht_mm, 1)

            with pe.Fori(0, LAYERS) as lay:
                turn_input(lay)
                with pe.Fori(0, G) as g:
                    w = lay * G + g
                    pe.wait_ge(ht_even, B * C // 2 * (lay + 1) + CREDIT)
                    pe.wait_ge(ht_odd, B * C // 2 * (lay + 1) + CREDIT)
                    values(w * B, 0, 0, w)
                    pe.wait_ge(y_add, w * B + CREDIT)
                    values(w * B, 1, 0, w)
                    values(w * B, 2, 0, w)
                    with pe.Fori(0, B // 2 - 1) as bp:
                        for bb in range(2):
                            body(w * B + 2 * bp + bb, bb, w, False)
                    for bb in range(2):
                        body(w * B + B - 2 + bb, bb, w, bb == 1)
            if stop_after == "L0":
                return

            turn_input(LAYERS)
            with pe.Fori(0, MG) as m:
                pe.wait_ge(w_lo, 4 * (MLP_BLOCK + 2 * m + 1) + CREDIT)
                for half in range(2):
                    for f in range(FT):
                        k = half * FT + f
                        cols = slice(half * HB * S, (half + 1) * HB * S)
                        if k < FT * 2:
                            pe.wait_ge(hm_lo, 2 * C + CREDIT)
                        pe.wait_ge(gelu_done, 2 * FT * m + k - 3 + CREDIT)
                        product(bank[k % 4][:, 0:HB * S], [
                            (lambda l, c=c: w_of(W1, l)[:, c, f * P:(f + 1) * P], lambda l, c=c: hm_s[:, l, c, cols])
                            for c in range(C)]).then_inc(fc1_mm, 1)
                pe.wait_ge(w_lo, 4 * (MLP_BLOCK + 2 * m + 2) + CREDIT)
                for b in range(B):
                    pe.wait_ge(g_lo, 2 * FT * m + (FT if b < HB else 2 * FT) + CREDIT)
                    pe.wait_ge(m_add, B * m + b - 1 + CREDIT)
                    product(bank[4 + b % 2][0:S, :], [
                        (lambda l, f=f: g_s[:, l, f, b * S:(b + 1) * S], lambda l, f=f: w_of(W2, l)[:, f, :])
                        for f in range(FT)]).then_inc(fc2_mm, 1)

            turn_input(LAYERS + 1, plain=True)
            pe.wait_ge(ht_even, B * C // 2 * (LAYERS + 2) + CREDIT)
            pe.wait_ge(ht_odd, B * C // 2 * (LAYERS + 2) + CREDIT)
            pe.wait_ge(w_lo, 4 * (LAST_BLOCK + 2) + 1 + CREDIT)
            pe.wait_ge(wide_zero, 1 + 2 * J + CREDIT)
            pe.wait_ge(wkv_loaded, 16)

            def scores1(i, kv):
                pe.wait_ge(k1_lo, KV * i + kv + 1 + CREDIT)
                for j in range(J):
                    pe.wait_ge(rmax1, J * (KV * i + kv - 1) + j + 1 + CREDIT)
                    product((k_ps + s_ps)[j][0:S, 0:T1], [(lambda l: qT_s[:, l, j, :], lambda l: kT_s[:, kv % 2, l, :])]
                            ).then_inc(s1_mm, 1)

            def probs1_turn(i, kv):
                for t in range(NT):
                    pe.wait_ge(pt1_out, NT * (KV * i + kv - 1) + t + 1 + CREDIT)
                    for j in range(J):
                        if t == 0:
                            pe.wait_ge(p1_norm, J * (KV * i + kv) + j + 1 + CREDIT)
                        mm = pe.transpose((t_ps, a_ps, b_ps)[t][:, j * S:(j + 1) * S],
                                          p_sb[:, kv % 2 * J + j, t * P:(t + 1) * P], ident[0:S, 0:S])
                    mm.then_inc(t1_mm, 1)

            def head1_out(i, kv):
                if kv == 0:
                    pe.wait_ge(vc_out, i + 1 + CREDIT)
                    pe.wait_ge(o_lo, BODIES + i + CREDIT)
                for t in range(NT):
                    rows = P if t < NT - 1 else T - (NT - 1) * P
                    pe.wait_ge(pt1_out, NT * (KV * i + kv) + t + 1 + CREDIT)
                    mm = pe.matmul(o_ps[:, 0:J * S], v_wide[0:rows, t, kv, :], pT1[0:rows, kv % 2, t, :],
                                   start=(kv == 0 and t == 0), stop=(kv == KV - 1 and t == NT - 1))
                mm.then_inc(pv1_mm, 1)

            def body1(i, slot, loads):
                n = BODIES + i
                pe.wait_ge(ctx_loaded[slot], 16 * loads)
                pe.wait_ge(y_add, n + CREDIT)
                for t in range(NT):
                    rows = P if t < NT - 1 else T - (NT - 1) * P
                    for c in range(C):
                        mm = pe.matmul(b_ps[0:rows, t * P:(t + 1) * P], ctx_raw[:, slot, c, t * P:t * P + rows],
                                       wkv_raw[:, 1, c, :], start=(c == 0), stop=(c == C - 1))
                mm.then_inc(vc_mm, 1)
                pe.wait_ge(ctx_lo, n + 1 + CREDIT)
                pe.wait_ge(rmax1, J * KV * i + CREDIT)
                product(k_ps[0][:, 0:T1], [(lambda l, c=c: wk1_s[:, l, c, :], lambda l, c=c: ctx_s[:, slot, l, c, :])
                                           for c in range(C)]).then_inc(kc_mm, 1)
                pe.wait_ge(pt1_out, NT * KV * i + CREDIT)
                queries(n, LQ)
                queries_turn(n, t_ps)
                pe.wait_ge(kb_out, i + 1 + CREDIT)
                pe.wait_ge(qt_lo, n + 1 + CREDIT)
                scores1(i, 0)
                scores1(i, 1)
                pe.wait_ge(vc_out, i + 1 + CREDIT)
                probs1_turn(i, 0)
                for kv in range(1, KV):
                    if kv + 1 < KV:
                        scores1(i, kv + 1)
                    head1_out(i, kv - 1)
                    probs1_turn(i, kv)
                head1_out(i, KV - 1)
                pe.wait_ge(pt1_out, NT * KV * (i + 1) + CREDIT)
                project(n, LO)

            with pe.Fori(0, B // 2) as t:
                for bb in range(2):
                    body1(2 * t + bb, bb, BODIES // 2 + t + 1)

        @block.vector
        def _(dve):
            credit(dve, by_dve)
            dve.wait_ge(par_loaded, 16)

            def low(out_hi, out_lo, full, s_hi, count, s_lo):
                dve.wait_ge(s_hi, count + CREDIT)
                dve.tensor_tensor(out_lo, full, f32(out_hi), ALU.subtract).then_inc(s_lo, 1)

            def split_block(kind, slot, blocks, chunks=range(4)):
                for c in chunks:
                    cols = slice(c * D, (c + 1) * D)
                    low(w_split[:, kind, 0, cols], w_split[:, kind, 1, cols], w_raw[:, slot, cols], w_hi, 4 * blocks + c + 1, w_lo)

            def split_context(n, slot):
                low(ctx_s[:, slot, 0, :, 1:T1], ctx_s[:, slot, 1, :, 1:T1], ctx_raw[:, slot], ctx_hi, n + 1, ctx_lo)

            def split_h(n, b):
                low(hb_s[:, 0], hb_s[:, 1], hT[:, :, b, :], hb_hi, n + 1, hb_lo)

            def add_out(n, b):
                dve.wait_ge(y_mm, n + 1 + CREDIT)
                dve.tensor_tensor(x_sb[:, b, :], x_sb[:, b, :], b_ps[0:S, :], ALU.add).then_inc(y_add, 1)

            def queries_out(n):
                dve.wait_ge(q_mm, n + 1 + CREDIT)
                dve.tensor_tensor(q_sb[:, :], a_ps[0:S, :], wrow[0:S, 0, :], ALU.add).then_inc(q_out, 1)

            def queries_lo(n, bk, scale):
                dve.wait_ge(qt_hi, n + 1 + CREDIT)
                dve.scalar_tensor_tensor(qT_s[:, 1], bk[:, 0:HG * S].rearrange("p (h q) -> p h q", h=HG), scale,
                                         f32(qT_s[:, 0]), ALU.mult, ALU.subtract).then_inc(qt_lo, 1)

            def value_out(n, i, slot):
                dve.wait_ge(v_mm, NT * n + i + 1 + CREDIT)
                if i == 0:
                    dve.wait_ge(pv_mm, HG * (n - 1) + CREDIT)
                rows = TILES[i][1]
                dve.tensor_tensor(v_sb[0:rows, slot, i, :], (a_ps, b_ps, a_ps)[i][0:rows, :], wrow[0:rows, 1, :],
                                  ALU.add).then_inc(v_out, 1)

            def key_lo(n, h, lay, g):
                dve.wait_ge(k_hi, HG * n + h + 1 + CREDIT)
                dve.scalar_tensor_tensor(kT_s[:, h % 2, 1, 1:T1], k_ps[h % 2][:, 1:T1],
                                         par[:, bass.ds(lay * P_LAYER + P_BK + g * HG + h, 1)],
                                         f32(kT_s[:, h % 2, 0, 1:T1]), ALU.add, ALU.subtract).then_inc(k_lo, 1)

            def row_max(n, h):
                dve.wait_ge(s_mm, HG * n + h + 1 + CREDIT)
                dve.tensor_reduce(nmax[:, 0, h:h + 1], s_ps[h % 2][0:S, 0:T1], AX.X, ALU.max, negate=True).then_inc(max_done, 1)

            def normalise(n, h):
                dve.wait_ge(exp_done, HG * n + h + 1 + CREDIT)
                dve.reciprocal(rz[:, 0, h:h + 1], zsum[:, 0, h:h + 1]).then_inc(z_inv, 1)
                dve.wait_ge(z_inv, HG * n + h + 1 + CREDIT)
                dve.tensor_scalar(p_sb[:, h % 2, 0:T1], p_sb[:, h % 2, 0:T1], rz[:, 0, h:h + 1], None,
                                  ALU.mult).then_inc(p_norm, 1)

            def heads_lo(n):
                dve.wait_ge(o_hi, n + 1 + CREDIT)
                dve.tensor_tensor(oT_s[:, 1], o_ps[:, 0:HG * S].rearrange("p (h q) -> p h q", h=HG), f32(oT_s[:, 0]),
                                  ALU.subtract).then_inc(o_lo, 1)

            def body(n, bb, b, lay, g, w, last):
                split_context(n + 1, 1 - bb)
                queries_out(n)
                key_lo(n, 0, lay, g)
                queries_lo(n, b_ps, SCALE0)
                key_lo(n, 1, lay, g)
                row_max(n, 0)
                if not last:
                    split_h(n + 1, b + 1)
                normalise(n, 0)
                key_lo(n, 2, lay, g)
                row_max(n, 1)
                normalise(n, 1)
                key_lo(n, 3, lay, g)
                row_max(n, 2)
                if last:
                    split_block(WV, 0, 4 * w + 4)
                normalise(n, 2)
                if not last:
                    value_out(n + 1, 0, 1 - bb)
                row_max(n, 3)
                normalise(n, 3)
                if not last:
                    value_out(n + 1, 1, 1 - bb)
                heads_lo(n)
                if not last:
                    value_out(n + 1, 2, 1 - bb)
                else:
                    split_block(WQ, 1, 4 * w + 5)
                add_out(n, b)

            def norm(times, eps, first_batch_wait=None):
                base = LN_STEPS * times
                for b in range(B):
                    dve.bn_stats(stats[:, b, :], x_sb[:, b, :]).then_inc(ln_step, 1)
                for b in range(B):
                    dve.wait_ge(ln_step, base + b + 1 + CREDIT)
                    settle(dve)
                    dve.bn_aggr(mv[:, b, :], stats[:, b, :]).then_inc(ln_step, 1)
                dve.wait_ge(ln_step, base + 2 * B + CREDIT)
                dve.tensor_scalar(rstd[:, 0, :], mv[:, :, 1], eps, None, ALU.add).then_inc(ln_step, 1)
                dve.wait_ge(root, times + 1 + CREDIT)
                dve.reciprocal(rstd[:, 2, :], rstd[:, 1, :]).then_inc(ln_step, 1)
                r, a, v = rstd[:, 2, :], rstd[:, 1, :], rstd[:, 0, :]
                dve.wait_ge(ln_step, base + 2 * B + 2 + CREDIT)
                dve.tensor_tensor(a, r, r, ALU.mult).then_inc(ln_step, 1)
                dve.wait_ge(ln_step, base + 2 * B + 3 + CREDIT)
                dve.tensor_tensor(a, a, v, ALU.mult).then_inc(ln_step, 1)
                dve.wait_ge(ln_step, base + 2 * B + 4 + CREDIT)
                dve.tensor_scalar(a, a, -0.5, 1.5, ALU.mult, ALU.add).then_inc(ln_step, 1)
                dve.wait_ge(ln_step, base + 2 * B + 5 + CREDIT)
                dve.tensor_tensor(r, r, a, ALU.mult).then_inc(ln_step, 1)
                dve.wait_ge(ln_step, base + LN_STEPS + CREDIT)

            def normed(times, b):
                dve.wait_ge(ht_mm, times * B + b - 1 + CREDIT)
                dve.tensor_scalar(hn[:, b % 2, :], x_sb[:, b, :], mv[:, b, 0:1], rstd[:, 2, b:b + 1],
                                  ALU.subtract, ALU.mult).then_inc(hn_out, 1)

            def input_odd(times, b, par_at):
                dve.wait_ge(ht_mm, times * B + b + 1 + CREDIT)
                for c in range(C):
                    cols = b_ps[:, c * S:(c + 1) * S]
                    if par_at is None:
                        dve.tensor_copy(hT[:, c, b, :], cols).then_inc(ht_odd, 1)
                    else:
                        dve.tensor_scalar(hT[:, c, b, :], cols, par[:, bass.ds(par_at + c, 1)],
                                          par[:, bass.ds(par_at + C + c, 1)], ALU.mult, ALU.add).then_inc(ht_odd, 1)

            def input_norm(times, par_at):
                norm(times, EPS0)
                for b in range(B):
                    normed(times, b)
                    if b % 2 == 0 and b:
                        input_odd(times, b - 1, par_at)
                input_odd(times, B - 1, par_at)

            split_context(0, 0)
            split_block(WV, 0, 0)
            split_block(WQ, 1, 1)
            dve.wait_ge(x_loaded, 16)
            with dve.Fori(0, LAYERS) as lay:
                dve.wait_ge(y_add, lay * (BODIES // 2) + CREDIT)
                input_norm(lay, P_NORM + lay * 2 * C)
                dve.wait_ge(k_col, lay * (BODIES // 2) * HG + CREDIT)
                bias_k = par[:, bass.ds(lay * P_LAYER + P_BIASK, H)]
                dve.tensor_copy(kbias_s[:, 0, :], bias_k).then_inc(kbias, 1)
                low(kbias_s[:, 0, :], kbias_s[:, 1, :], bias_k, kbias, 2 * lay + 1, kbias)
                with dve.Fori(0, G) as g:
                    w = lay * G + g
                    split_block(WK, 0, 4 * w + 2)
                    split_h(w * B, 0)
                    dve.wait_ge(wrow_loaded, 16 * (w + 1))
                    value_out(w * B, 0, 0)
                    split_block(WO, 1, 4 * w + 3, range(0, 2))
                    value_out(w * B, 1, 0)
                    split_block(WO, 1, 4 * w + 3, range(2, 4))
                    value_out(w * B, 2, 0)
                    dve.wait_ge(bo_add, B * (lay + 1) + CREDIT)
                    settle(dve)
                    with dve.Fori(0, B // 2 - 1) as bp:
                        for bb in range(2):
                            body(w * B + 2 * bp + bb, bb, 2 * bp + bb, lay, g, w, False)
                    for bb in range(2):
                        body(w * B + B - 2 + bb, bb, B - 2 + bb, lay, g, w, bb == 1)
            if stop_after == "L0":
                return

            dve.wait_ge(y_add, BODIES + CREDIT)
            input_norm(LAYERS, P_NORM + LAYERS * 2 * C)
            for c in range(C):
                for half in range(2):
                    cols = slice(half * HB * S, (half + 1) * HB * S)
                    low(hm_s[:, 0, c, cols], hm_s[:, 1, c, cols],
                        hT[:, c, half * HB:(half + 1) * HB, :].rearrange("p b q -> p (b q)"), hm_hi, 2 * c + half + 1, hm_lo)
            dve.wait_ge(bo_add, B * (LAYERS + 1) + CREDIT)
            with dve.Fori(0, MG) as m:
                for half in range(2):
                    for f in range(FT):
                        k = half * FT + f
                        cols = slice(half * HB * S, (half + 1) * HB * S)
                        low(g_s[:, 0, f, cols], g_s[:, 1, f, cols], gelu[:, k % 2, :], g_hi, 2 * FT * m + k + 1, g_lo)
                for b in range(B):
                    if b == 2:
                        split_block(W1, 0, MLP_BLOCK + 2 * m + 2)
                    dve.wait_ge(fc2_mm, B * m + b + 1 + CREDIT)
                    dve.tensor_tensor(x_sb[:, b, :], x_sb[:, b, :], bank[4 + b % 2][0:S, :], ALU.add).then_inc(m_add, 1)
                split_block(W2, 1, MLP_BLOCK + 2 * m + 3)

            for b in range(1, B, 2):
                input_odd(LAYERS + 1, b, None)
            low(wk1_s[:, 0].rearrange("p c n -> p (c n)"), wk1_s[:, 1].rearrange("p c n -> p (c n)"),
                wkv_raw[:, 0].rearrange("p c n -> p (c n)"), w_hi, 4 * (LAST_BLOCK + 2) + 1, w_lo)
            dve.wait_ge(wrow_loaded, 16 * (SETS + 1))
            dve.wait_ge(wide_zero, 1 + 2 * J + CREDIT)
            dve.wait_ge(bo_add, B * (LAYERS + 2) + CREDIT)

            def values1_out(i):
                dve.wait_ge(vc_mm, i + 1 + CREDIT)
                dve.wait_ge(pv1_mm, KV * i + CREDIT)
                for t in range(NT):
                    rows = P if t < NT - 1 else T - (NT - 1) * P
                    diag = v_all[0:rows, t * KV * P:t * KV * P + DIAG].rearrange("p (k n) -> p k n", k=KV)[:, :, 0:HS]
                    ins = dve.tensor_tensor(diag, b_ps[0:rows, t * P:(t + 1) * P].rearrange("p (k n) -> p k n", k=KV),
                                            wrow[0:rows, 1, 0:P].rearrange("p (k n) -> p k n", k=KV), ALU.add)
                ins.then_inc(vc_out, 1)

            def key1_lo(i, kv):
                dve.wait_ge(k1_hi, KV * i + kv + 1 + CREDIT)
                dve.scalar_tensor_tensor(kT_s[:, kv % 2, 1, 1:T1], kb_sb[:, :], par[:, P_MASK + kv:P_MASK + kv + 1],
                                         f32(kT_s[:, kv % 2, 0, 1:T1]), ALU.mult, ALU.subtract).then_inc(k1_lo, 1)

            def masked(i, kv, slot):
                dve.wait_ge(t1_mm, NT * (KV * i + kv - 1) + CREDIT)
                for j in range(J):
                    dve.wait_ge(s1_mm, J * (KV * i + kv) + j + 1 + CREDIT)
                    settle(dve)
                    dve.tensor_tensor_reduce(p_sb[:, kv % 2 * J + j, 0:T], (k_ps + s_ps)[j][0:S, 1:T1],
                                             mask_sb[:, slot, :], 1.0, -3.4e38, ALU.add, ALU.max,
                                             rmax[:, kv % 2, j:j + 1]).then_inc(rmax1, 1)
                dve.wait_ge(rmax1, J * (KV * i + kv + 1) + CREDIT)
                dve.tensor_scalar(nmax[:, kv % 2, :], rmax[:, kv % 2, :], -1.0, None, ALU.mult).then_inc(nmax1, 1)

            def normalise1(i, kv):
                dve.wait_ge(exp1, J * (KV * i + kv + 1) + CREDIT)
                dve.reciprocal(rz[:, kv % 2, :], zsum[:, kv % 2, :]).then_inc(z1_inv, 1)
                dve.wait_ge(z1_inv, KV * i + kv + 1 + CREDIT)
                for j in range(J):
                    slot = p_sb[:, kv % 2 * J + j, 0:T]
                    dve.tensor_scalar(slot, slot, rz[:, kv % 2, j:j + 1], None, ALU.mult).then_inc(p1_norm, 1)

            def body1(i, slot, loads, last):
                n = BODIES + i
                values1_out(i)
                split_h(n, i)
                dve.wait_ge(kc_mm, i + 1 + CREDIT)
                dve.wait_ge(k1_hi, KV * i + CREDIT)
                dve.wait_ge(k1_lo, KV * i + CREDIT)
                dve.tensor_scalar(kb_sb[:, :], k_ps[0][:, 1:T1], par[:, P_BK1:P_BK1 + 1], None, ALU.add).then_inc(kb_out, 1)
                queries_out(n)
                key1_lo(i, 0)
                key1_lo(i, 1)
                queries_lo(n, t_ps, SCALE1)
                dve.wait_ge(mask_loaded[slot], 16 * loads)
                masked(i, 0, slot)
                for kv in range(KV):
                    if kv + 1 < KV:
                        masked(i, kv + 1, slot)
                    if kv + 2 < KV:
                        key1_lo(i, kv + 2)
                    normalise1(i, kv)
                    if kv == 3 and not last:
                        split_context(n + 1, 1 - slot)
                heads_lo(n)
                add_out(n, i)

            with dve.Fori(0, B // 2 - 1) as t:
                for bb in range(2):
                    body1(2 * t + bb, bb, t + 1, False)
            for bb in range(2):
                body1(B - 2 + bb, bb, B // 2, bb == 1)
            dve.wait_ge(y_add, BODIES + B + CREDIT)
            norm(LAYERS + 1, EPS1)
            dve.wait_ge(gb_loaded, 16)
            for b in range(B):
                dve.tensor_scalar(x_sb[:, b, :], x_sb[:, b, :], mv[:, b, 0:1], rstd[:, 2, b:b + 1],
                                  ALU.subtract, ALU.mult).then_inc(m_add, 1)
                dve.wait_ge(m_add, B * MG + 2 * b + 1 + CREDIT)
                dve.tensor_tensor(x_sb[:, b, :], x_sb[:, b, :], gb[:, 0, :], ALU.mult).then_inc(m_add, 1)
                dve.wait_ge(m_add, B * MG + 2 * b + 2 + CREDIT)
                dve.tensor_tensor(x_sb[:, b, :], x_sb[:, b, :], gb[:, 1, :], ALU.add).then_inc(fin, 1)


def lay_out(a):
    f = {k: np.asarray(v) for k, v in a.items()}

    def w_in(w):
        return w.reshape(C, P, -1).transpose(1, 0, 2).reshape(P, -1)

    L = lambda name, i: f[f"L0_xattn_{name}{i + 1}"]
    blocks = []
    for i in range(LAYERS):
        for g in range(G):
            cols = slice(g * D, (g + 1) * D)
            blocks += [w_in(L(n, i)[:, cols]) for n in ("wv", "wq", "wk")] + [w_in(L("wo", i)[cols, :])]
    for m in range(MG):
        cols = slice(m * D, (m + 1) * D)
        blocks += [w_in(f["L0_xattn_w_fc1"][:, cols]), w_in(f["L0_xattn_w_fc2"][cols, :])]
    by_j = lambda v: v.reshape(v.shape[:-1] + (KV, J, HS)).swapaxes(-3, -2).reshape(v.shape)
    blocks += [w_in(by_j(f["L1_xattn_Wq"])), w_in(by_j(f["L1_xattn_Wo"].T).T)]
    wkv = np.concatenate([w_in(f["L1_xattn_Wk"]), w_in(f["L1_xattn_Wv"])], axis=1)
    col = lambda v: v.reshape(-1, P).T
    par = []
    for i in range(LAYERS):
        par += [col(L("bk", i)), col(L("bias_k", i))]
    for s, o in (("ln1_scale", "ln1_offset"), ("ln2_scale", "ln2_offset"), ("ln_mlp_scale", "ln_mlp_offset")):
        par += [col(f["L0_xattn_" + s]), col(f["L0_xattn_" + o])]
    masks = np.repeat(np.eye(KV, dtype=np.float32), HS, axis=0)
    par += [col(f["L0_xattn_b_fc1"]), col(f["L1_xattn_bk"]), masks]
    rows = np.stack([L("bo", 0), L("bo", 1), f["L0_xattn_b_fc2"], f["L1_xattn_bo"]])
    wrow = [np.stack([L(n, i).reshape(-1)[g * D:(g + 1) * D] for n in ("bq", "bv", "bias_v")])
            for i in range(LAYERS) for g in range(G)]
    last = np.zeros((3, D), np.float32)
    last[0] = by_j(f["L1_xattn_bq"])
    last[1, 0:KV * HS] = f["L1_xattn_bv"]
    ctx = f["ctx_2048"].reshape(B, T, C, P).transpose(0, 3, 2, 1)
    return {
        "x": f["x"], "ctx": ctx, "mask": f["mask_Bx1xSxS2_ff0"].reshape(B, S, T), "w": np.stack(blocks),
        "wkv": wkv.reshape(P, 2, C, P), "par": np.concatenate(par, axis=1), "rows": rows,
        "wrow": np.stack(wrow + [last]), "gb": np.stack([f["L1_xattn_gamma"], f["L1_xattn_beta"]]),
    }


def kernel(**inputs):
    import concourse.bacc as bacc
    from concourse.bass_utils import run_bass_kernel_spmd

    nc = bacc.Bacc("TRN2", target_bir_lowering=False, num_devices=1)
    arrays = {f"in_{k}": np.ascontiguousarray(v) for k, v in lay_out(inputs).items()}
    args = [nc.dram_tensor(k, v.shape, mybir.dt.from_np(v.dtype), kind="ExternalInput").ap() for k, v in arrays.items()]
    out = nc.dram_tensor("out", (B, S, D), F32, kind="ExternalOutput").ap()
    build(nc, *args, out)
    r = run_bass_kernel_spmd(nc, [arrays], core_ids=[0])
    return r.results[0]["out"]
```

```python
from contextlib import ExitStack

import numpy as np
import concourse.bass as bass
from concourse import mybir
from concourse.alu_op_type import AluOpType as ALU

F32 = mybir.dt.float32
F32R = mybir.dt.float32r
ACT = mybir.ActivationFunctionType
AX = mybir.AxisListType

P = 128
B, S, D = 8, 112, 512
T = 375
T1 = T + 1
C = D // P
LAYERS = 2
H, HD = 16, 128
G = 4
HG = H // G
TILES = [(0, 128), (128, 128), (256, T1 - 256)]
NT = len(TILES)
F = 2048
MG = F // D
FT = D // P
KV, HS = 8, 16
J = 4
PAIRS = KV // 2
ORDER = [2 * p + a for a in range(2) for p in range(PAIRS)]
PICK = 2 * HS + PAIRS * P
HB = B // 2
SETS = LAYERS * G
BODIES = SETS * B
MLP_BLOCK = SETS * 4
LAST_BLOCK = MLP_BLOCK + 2 * MG
SCALE0 = float(HD) ** -0.5
SCALE1 = float(HS) ** -0.5
EPS0, EPS1 = 1e-5, 1e-6
CREDIT = 8
FIRST = 0
LN_STEPS = 2 * B + 6
PASSES = ((0, 0), (0, 1), (1, 0))

P_BK, P_BIASK, P_LAYER = 0, H, 2 * H
P_NORM = LAYERS * P_LAYER
P_FC1 = P_NORM + 3 * 2 * C
P_BK1 = P_FC1 + F // P
P_ALL = P_BK1 + 1


def build(nc, x_d, ctx_d, mask_d, w_d, wkv_d, par_d, pick_d, rows_d, wrow_d, gb_d, out_d, stop_after=None):
    st = ExitStack()
    with st:
        def sb(name, shape, dt=F32):
            return st.enter_context(nc.sbuf_tensor(name, shape, dt))

        def sem(name):
            return st.enter_context(nc.semaphore(name))

        def f32(ap):
            return ap.bitcast(F32)

        bank = [st.enter_context(nc.psum_tensor(f"bank{i}", [P, 512], F32)) for i in range(8)]
        k_ps, s_ps, t_ps, o_ps, a_ps, b_ps = bank[0:2], bank[2:4], bank[4], bank[5], bank[6], bank[7]
        x_sb = sb("x_sb", [S, B, D])
        hT = sb("hT", [P, C, B, S])
        w_split = sb("w_split", [P, 4, 2, 4 * D], F32R)
        w_raw = sb("w_raw", [P, 2, 4 * D])
        ctx_raw = sb("ctx_raw", [P, 2, C, T])

        sizes = [2 * 2 * C * T1, 2 * C * S, 2 * HG * S, 2 * 2 * T1, 2 * HG * S]
        arena_r = sb("arena_r", [P, sum(sizes)], F32R)
        at = [sum(sizes[:i]) for i in range(6)]
        ctx_s = arena_r[:, at[0]:at[1]].rearrange("p (s l c t) -> p s l c t", s=2, l=2, c=C)
        hb_s = arena_r[:, at[1]:at[2]].rearrange("p (l c q) -> p l c q", l=2, c=C)
        qT_s = arena_r[:, at[2]:at[3]].rearrange("p (l h q) -> p l h q", l=2, h=HG)
        kT_s = arena_r[:, at[3]:at[4]].rearrange("p (s l t) -> p s l t", s=2, l=2)
        oT_s = arena_r[:, at[4]:at[5]].rearrange("p (l h q) -> p l h q", l=2, h=HG)
        half_ctx = at[1] // 2
        hm_s = arena_r[:, half_ctx:half_ctx + 2 * C * B * S].rearrange("p (l c n) -> p l c n", l=2, c=C)
        g_s = w_split[:, 2:4].rearrange("p k l n -> p (k l n)")[:, 0:2 * FT * B * S].rearrange(
            "p (l f n) -> p l f n", l=2, f=FT)

        kbias_s = sb("kbias_s", [P, 2, H], F32R)
        v_all = sb("v_all", [P, 2 * NT * D])
        v_sb = v_all[:, :].rearrange("p (s i n) -> p s i n", s=2, i=NT)
        q_sb = sb("q_sb", [S, D])
        p_sb = sb("p_sb", [S, 2 * J, NT * P])
        kh_s = sb("kh_s", [P, 2, T1], F32R)
        pT_sb = f32(kh_s[:, :, :].rearrange("p l t -> p (l t)"))[:, 0:2 * NT * S].rearrange("p (s n) -> p s n", s=2)
        hn = v_sb[0:S, 0, 0:2, :]
        gelu = v_sb[:, 0, 0:2, 0:HB * S]
        ident = sb("ident", [P, P])
        par = sb("par", [P, P_ALL])
        wrow = sb("wrow", [P, 3, D])
        bo_bc = sb("bo_bc", [S, D])
        stats = sb("stats", [S, B, 6])
        mv = sb("mv", [S, B, 2])
        rstd = sb("rstd", [S, 3, B])
        nmax = sb("nmax", [S, 2, J])
        rmax = sb("rmax", [S, 2, J])
        zsum = sb("zsum", [S, 2, J])
        rz = sb("rz", [S, 2, J])
        wkv_raw = w_raw[:, 0, 0:2 * C * P].rearrange("p (k c n) -> p k c n", k=2, c=C)
        own = w_split[:, 2:4].rearrange("p k l n -> p (k l n)")
        sizes = [KV * T1, PAIRS * J * S, 2 * C * P, PICK]
        at = [sum(sizes[:i]) for i in range(5)]
        kh_all = own[:, at[0]:at[1]].rearrange("p (k t) -> p k t", k=KV)
        qh_all = own[:, at[1]:at[2]].rearrange("p (c j q) -> p c j q", c=PAIRS, j=J)
        wk1_s = own[:, at[2]:at[3]].rearrange("p (l c n) -> p l c n", l=2, c=C)
        pick = own[:, at[3]:at[4]]
        VW = NT * KV * 2 * HS
        v_wide = v_all[:, 0:2 * VW].rearrange("p (s i k n) -> p s i k n", s=2, i=NT, k=KV)
        PT = NT * J * S
        raw = w_raw[:, :, :].rearrange("p s n -> p (s n)")
        hT_flat = hT[:, :, :, :].rearrange("p c b q -> p (c b q)")
        free = [raw[:, 2 * C * P:2 * C * P + PT], raw[:, 2 * C * P + PT:2 * C * P + 2 * PT], hT_flat[:, 0:PT],
                hT_flat[:, PT:2 * PT], v_all[:, 2 * VW:2 * VW + PT]]
        pT1 = [[free[k].rearrange("p (i n) -> p i n", i=NT) for k in order]
               for order in ((0, 1, 2, 3, 4, 0, 1, 2), (3, 4, 0, 1, 2, 3, 4, 1))]
        SLOT_FREE = (-1, 0, 0, 0, 0, 1, 1, 1)
        xb_sb = hT_flat[0:S, 2 * PT:2 * PT + D]
        k_rows = [raw[:, 2 * C * P + 2 * PT:2 * C * P + 2 * PT + T], hT_flat[:, 2 * PT + D:2 * PT + D + T]]
        pick_raw = hT_flat[:, 0:PICK]
        c_ps, t1_ps = bank[1], (t_ps, a_ps, bank[0])
        on_sb = sb("on_sb", [P, J * S])
        zsum1 = sb("zsum1", [S, 2, J, KV])
        rz_wide = q_sb[:, :].rearrange("s (j k d) -> s j k d", j=J, k=KV)
        mask_sb = sb("mask_sb", [S, 2, T])
        gb = wrow[0:S, 1:3, :]

        x_loaded, par_loaded, out_stored, consts = sem("x_loaded"), sem("par_loaded"), sem("out_stored"), sem("consts")
        waited = sem("waited")
        ctx_loaded = [sem("ctx_loaded0"), sem("ctx_loaded1")]
        w_loaded = [sem("w_loaded0"), sem("w_loaded1")]
        mask_loaded = [sem("mask_loaded0"), sem("mask_loaded1")]
        bo_loaded, wrow_loaded, gb_loaded, wkv_loaded = sem("bo_loaded"), sem("wrow_loaded"), sem("gb_loaded"), sem("wkv_loaded")
        pick_loaded = sem("pick_loaded")
        by_sp = {n: sem(n) for n in ("rows_loaded0", "rows_loaded1")}
        rows_loaded = list(by_sp.values())
        by_pe = {n: sem(n) for n in ("q_mm", "qt_mm", "k_mm", "s_mm", "t_mm", "pv_mm", "v_mm", "y_mm", "ht_mm",
                                     "fc1_mm", "fc2_mm", "vc_mm", "kc_mm", "s1_mm", "t1_mm", "pv1_mm",
                                     "pick_mm", "z_mm")}
        by_act = {n: sem(n) for n in ("w_hi", "ctx_hi", "hb_hi", "qt_hi", "k_hi", "exp_done", "pt_out", "o_hi", "root",
                                      "ht_even", "hm_hi", "gelu_done", "g_hi", "k1_hi", "exp1", "pt1_out", "qh_out", "z_out", "z_wide", "pick_out")}
        by_dve = {n: sem(n) for n in ("w_lo", "ctx_lo", "hb_lo", "q_out", "qt_lo", "k_lo", "max_done", "z_inv", "p_norm",
                                      "v_out", "o_lo", "y_add", "ln_step", "hn_out", "ht_odd", "kbias", "hm_lo", "g_lo",
                                      "vc_out", "k1_lo", "rmax1", "nmax1", "z1_inv", "pt1_odd", "o_norm", "m_add", "fin")}
        by_pool = {n: sem(n) for n in ("k_col", "v_row", "bo_add", "pool_step", "wide_zero", "x_taken", "kh_out")}
        q_mm, qt_mm, k_mm, s_mm, t_mm, pv_mm, v_mm, y_mm, ht_mm, fc1_mm, fc2_mm, vc_mm, kc_mm, s1_mm, t1_mm, pv1_mm, pick_mm, z_mm = by_pe.values()
        (w_hi, ctx_hi, hb_hi, qt_hi, k_hi, exp_done, pt_out, o_hi, root, ht_even, hm_hi, gelu_done, g_hi, k1_hi, exp1,
         pt1_out, qh_out, z_out, z_wide, pick_out) = by_act.values()
        (w_lo, ctx_lo, hb_lo, q_out, qt_lo, k_lo, max_done, z_inv, p_norm, v_out, o_lo, y_add, ln_step, hn_out, ht_odd,
         kbias, hm_lo, g_lo, vc_out, k1_lo, rmax1, nmax1, z1_inv, pt1_odd, o_norm, m_add, fin) = by_dve.values()
        k_col, v_row, bo_add, pool_step, wide_zero, x_taken, kh_out = by_pool.values()

        def credit(eng, sems):
            for s in sems.values():
                eng.sem_inc(s, CREDIT)

        def settle(eng):
            eng.sem_inc(waited, 1)

        def w_of(kind, lo):
            return w_split[:, kind, lo, :].rearrange("p (c n) -> p c n", c=4)

        WV, WQ, WK, WO = range(4)
        W1, W2 = 0, 1
        LQ, LO = 0, 1

        block = st.enter_context(nc.Block())

        @block.sync
        def _(sp):
            def context(n, b, slot):
                sp.wait_ge(ctx_lo, n - 1 + CREDIT)
                sp.dma_start(ctx_raw[:, slot], ctx_d[b]).then_inc(ctx_loaded[slot], 16)

            credit(sp, by_sp)
            sp.dma_start(x_sb[:, :, :], x_d.rearrange("b s d -> s b d")).then_inc(x_loaded, 16)
            sp.dma_start(par[:, :], par_d).then_inc(par_loaded, 16)
            for s in range(2):
                sp.dma_start(ctx_raw[:, s], ctx_d[s]).then_inc(ctx_loaded[s], 16)
                sp.dma_start(w_raw[:, s, :], w_d[s]).then_inc(w_loaded[s], 16)
            with sp.Fori(0, LAYERS) as lay:
                sp.wait_ge(bo_add, lay * B + CREDIT)
                sp.dma_start(bo_bc[:, :], rows_d[lay, :].partition_broadcast(S)).then_inc(bo_loaded, 16)
                with sp.Fori(0, G) as g:
                    w = lay * G + g
                    sp.wait_ge(q_out, w * B + CREDIT)
                    sp.wait_ge(v_out, w * B * NT + CREDIT)
                    sp.wait_ge(v_row, w * B + CREDIT)
                    sp.dma_start(wrow[:, :, :], wrow_d[w].partition_broadcast(P)).then_inc(wrow_loaded, 16)
                    for j in range(2, 6):
                        sp.wait_ge(w_lo, 16 * w + 4 * (j - 1) + CREDIT)
                        sp.dma_start(w_raw[:, j % 2, :], w_d[4 * w + j]).then_inc(w_loaded[j % 2], 16)
                    with sp.Fori(0, B // 2 - 1) as bp:
                        for bb in range(2):
                            context(w * B + 2 * bp + bb + 2, 2 * bp + bb + 2, bb)
                    for bb in range(2):
                        context(w * B + B + bb, bb, bb)
            if stop_after == "L0":
                sp.wait_ge(y_add, BODIES + CREDIT)
                sp.dma_start(out_d.rearrange("b s d -> s b d"), x_sb[:, :, :]).then_inc(out_stored, 16)
                sp.wait_ge(out_stored, 16)
                for s in range(2):
                    sp.wait_ge(ctx_loaded[s], 16 * (BODIES // 2 + 1))
                    sp.wait_ge(w_loaded[s], 16 * (MLP_BLOCK // 2 + 1))
                return
            sp.wait_ge(bo_add, LAYERS * B + CREDIT)
            sp.dma_start(bo_bc[:, :], rows_d[LAYERS, :].partition_broadcast(S)).then_inc(bo_loaded, 16)
            with sp.Fori(0, MG) as m:
                for j in range(2):
                    sp.wait_ge(w_lo, 4 * (MLP_BLOCK + 2 * m + j + 1) + CREDIT)
                    sp.dma_start(w_raw[:, j, :], w_d[MLP_BLOCK + 2 * m + j + 2]).then_inc(w_loaded[j], 16)
            sp.wait_ge(bo_add, (LAYERS + 1) * B + CREDIT)
            sp.dma_start(bo_bc[:, :], rows_d[LAYERS + 1, :].partition_broadcast(S)).then_inc(bo_loaded, 16)
            sp.dma_start(wrow[:, :, :], wrow_d[SETS].partition_broadcast(P)).then_inc(wrow_loaded, 16)
            for s in range(2):
                sp.dma_start(mask_sb[:, s, :], mask_d[s]).then_inc(mask_loaded[s], 16)
            sp.wait_ge(w_lo, 4 * (LAST_BLOCK + 1) + CREDIT)
            sp.dma_start(wkv_raw, wkv_d).then_inc(wkv_loaded, 16)
            sp.wait_ge(hm_lo, 2 * C + CREDIT)
            sp.dma_start(pick_raw, pick_d).then_inc(pick_loaded, 16)

            def keys_of(i):
                sp.wait_ge(k1_lo, i + 1 + CREDIT)
                for k in range(KV):
                    kv = ORDER[k]
                    sp.wait_ge(kh_out, KV * i + k - 1 + CREDIT)
                    for part in range(4):
                        first = kv % 2 * 4 * HS + part * HS
                        sp.dma_start(k_rows[k % 2][first:first + HS, :], f32(kh_s[kv * HS:(kv + 1) * HS, part % 2, 1:T1])
                                     ).then_inc(rows_loaded[k % 2], 16)

            sp.wait_ge(w_lo, 4 * (LAST_BLOCK + 2) + CREDIT)
            keys_of(0)
            with sp.Fori(0, B // 2 - 1) as t:
                for bb in range(2):
                    i = 2 * t + bb
                    sp.wait_ge(vc_mm, i + 1 + CREDIT)
                    settle(sp)
                    context(BODIES + i + 2, i + 2, bb)
                    keys_of(i + 1)
                    sp.wait_ge(rmax1, KV * J * (i + 1) + CREDIT)
                    sp.dma_start(mask_sb[:, bb, :], mask_d[i + 2]).then_inc(mask_loaded[bb], 16)
            keys_of(B - 1)
            sp.wait_ge(vc_out, B + CREDIT)
            sp.dma_start(gb, gb_d.partition_broadcast(S)).then_inc(gb_loaded, 16)
            for b in range(B):
                sp.wait_ge(fin, b + 1 + CREDIT)
                sp.dma_start(out_d[b], x_sb[:, b, :]).then_inc(out_stored, 16)
            sp.wait_ge(out_stored, 16 * B)

        @block.gpsimd
        def _(pool):
            credit(pool, by_pool)
            pool.memset(ident[:, :], 0.0).then_inc(pool_step, 1)
            pool.wait_ge(pool_step, 1 + CREDIT)
            pool.affine_select(out=ident[:, :], in_=ident[:, :], compare_op=ALU.not_equal, fill=1.0, base=0,
                               pattern=[[-1, P]], channel_multiplier=1).then_inc(consts, 1)
            for s in range(2):
                pool.memset(f32(ctx_s[:, s, :, :, 0:1]), 0.0).then_inc(consts, 1)
                pool.memset(p_sb[:, s, T1:NT * P], 0.0).then_inc(consts, 1)

            def add_bias_rows(times):
                pool.wait_ge(bo_loaded, (times + 1) * 16)
                for b in range(B):
                    pool.wait_ge(hn_out, times * B + b + 1 + CREDIT)
                    pool.tensor_tensor(x_sb[:, b, :], x_sb[:, b, :], bo_bc[:, :], ALU.add).then_inc(bo_add, 1)

            def body(n, bb, g):
                pool.wait_ge(v_out, NT * n + 1 + CREDIT)
                settle(pool)
                pool.tensor_copy(v_sb[0:1, bb, 0, :], wrow[0:1, 2, :]).then_inc(v_row, 1)
                for h in range(HG):
                    pool.wait_ge(s_mm, HG * n + h - 1 + CREDIT)
                    settle(pool)
                    pool.tensor_copy(kT_s[:, h % 2, :, 0:1], f32(kbias_s[:, :, bass.ds(g * HG + h, 1)])).then_inc(k_col, 1)

            with pool.Fori(0, LAYERS) as lay:
                add_bias_rows(lay)
                pool.wait_ge(kbias, 2 * lay + 2 + CREDIT)
                settle(pool)
                with pool.Fori(0, G) as g:
                    w = lay * G + g
                    pool.wait_ge(wrow_loaded, (w + 1) * 16)
                    settle(pool)
                    with pool.Fori(0, B // 2) as bp:
                        for bb in range(2):
                            body(w * B + bp * 2 + bb, bb, g)
            if stop_after == "L0":
                return
            add_bias_rows(LAYERS)
            pool.wait_ge(fc2_mm, MG * B + CREDIT)
            pool.wait_ge(g_lo, MG * FT * 2 + CREDIT)
            pool.memset(f32(own[:, 0:at[1]]), 0.0).then_inc(wide_zero, 1)
            pool.memset(v_all[:, 0:2 * VW], 0.0).then_inc(wide_zero, 1)
            for s in range(2 * J):
                pool.memset(p_sb[:, s, T:NT * P], 0.0).then_inc(wide_zero, 1)

            def take_x(b):
                pool.wait_ge(ht_mm, (LAYERS + 1) * B + b + CREDIT)
                settle(pool)
                pool.tensor_copy(xb_sb.unsqueeze(1), x_sb[:, bass.ds(b, 1), :]).then_inc(x_taken, 1)
                pool.tensor_tensor(x_sb[:, bass.ds(b, 1), :], x_sb[:, bass.ds(b, 1), :], bo_bc[:, :].unsqueeze(1),
                                   ALU.add).then_inc(bo_add, 1)

            pool.wait_ge(bo_loaded, (LAYERS + 2) * 16)
            pool.wait_ge(m_add, MG * B + CREDIT)
            take_x(0)

            def context_lo(i, slot):
                pool.wait_ge(ctx_hi, BODIES + i + 1 + CREDIT)
                settle(pool)
                pool.tensor_tensor(ctx_s[:, slot, 1, :, 1:T1], ctx_raw[:, slot], f32(ctx_s[:, slot, 0, :, 1:T1]),
                                   ALU.subtract).then_inc(ctx_lo, 1)

            def keys_out(i, ks, ctxs):
                for k in ks:
                    kv = ORDER[k]
                    rows = slice(kv % 2 * 4 * HS, (kv % 2 + 1) * 4 * HS)
                    if kv % 2:
                        pool.wait_ge(kh_out, KV * i + k + CREDIT)
                        pool.wait_ge(ctx_lo, BODIES + ctxs + CREDIT)
                    pool.wait_ge(rows_loaded[k % 2], 64 * (KV // 2 * i + k // 2 + 1) + CREDIT)
                    if i is not FIRST:
                        pool.wait_ge(s1_mm, J * (KV * (i - 1) + k + 1) + CREDIT)
                    settle(pool)
                    pool.tensor_copy(kh_all[rows, kv, 1:T1], k_rows[k % 2][rows, :]).then_inc(kh_out, 1)
                if KV - 1 in ks:
                    pool.wait_ge(kh_out, KV * (i + 1) + CREDIT)

            context_lo(1, 1)
            keys_out(FIRST, range(KV), 2)
            take_x(1)
            with pool.Fori(0, B // 2 - 1) as t:
                for bb in range(2):
                    i = 2 * t + bb
                    take_x(i + 2)
                    keys_out(i + 1, range(0, 4), i + 2)
                    context_lo(i + 2, bb)
                    keys_out(i + 1, range(4, KV), i + 3)
            keys_out(B - 1, range(KV), B)

        @block.scalar
        def _(act):
            credit(act, by_act)
            act.wait_ge(par_loaded, 16)

            def split_block(kind, slot, loads, chunks=range(4)):
                act.wait_ge(w_loaded[slot], loads * 16)
                for c in chunks:
                    cols = slice(c * D, (c + 1) * D)
                    act.activation(w_split[:, kind, 0, cols], w_raw[:, slot, cols], ACT.Copy).then_inc(w_hi, 1)

            def split_context(n, slot, loads):
                act.wait_ge(ctx_loaded[slot], 16 * loads)
                act.wait_ge(k_mm, HG * (n - 1) + CREDIT)
                act.activation(ctx_s[:, slot, 0, :, 1:T1], ctx_raw[:, slot], ACT.Copy).then_inc(ctx_hi, 1)

            def split_h(n, b):
                act.wait_ge(q_mm, n + CREDIT)
                settle(act)
                act.activation(hb_s[:, 0], hT[:, :, b, :], ACT.Copy).then_inc(hb_hi, 1)

            def key_hi(n, h, lay, g):
                act.wait_ge(k_mm, HG * n + h + 1 + CREDIT)
                act.wait_ge(s_mm, HG * n + h - 1 + CREDIT)
                settle(act)
                act.activation(kT_s[:, h % 2, 0, 1:T1], k_ps[h % 2][:, 1:T1], ACT.Identity,
                               bias=par[:, bass.ds(lay * P_LAYER + P_BK + g * HG + h, 1)]).then_inc(k_hi, 1)

            def exps(n, h):
                act.wait_ge(max_done, HG * n + h + 1 + CREDIT)
                act.wait_ge(t_mm, HG * n + h - 1 + CREDIT)
                act.activation(p_sb[:, h % 2, 0:T1], s_ps[h % 2][0:S, 0:T1], ACT.Exp, bias=nmax[:, 0, h:h + 1],
                               accum_out=zsum[:, 0, h:h + 1]).then_inc(exp_done, 1)

            def probs_out(n, h):
                act.wait_ge(t_mm, HG * n + h + 1 + CREDIT)
                act.wait_ge(pv_mm, HG * n + h - 1 + CREDIT)
                act.activation(pT_sb[:, h % 2, :], t_ps[:, 0:NT * S], ACT.Copy).then_inc(pt_out, 1)

            def heads_hi(n):
                act.wait_ge(pv_mm, HG * (n + 1) + CREDIT)
                act.wait_ge(y_mm, n + CREDIT)
                act.activation(oT_s[:, 0], o_ps[:, 0:HG * S].rearrange("p (h q) -> p h q", h=HG),
                               ACT.Copy).then_inc(o_hi, 1)

            def queries_hi(n, bk, scale):
                act.wait_ge(qt_mm, n + 1 + CREDIT)
                act.activation(qT_s[:, 0], bk[:, 0:HG * S].rearrange("p (h q) -> p h q", h=HG), ACT.Copy,
                               scale=scale).then_inc(qt_hi, 1)

            def body(n, bb, b, lay, g, w, loads, last):
                split_context(n + 1, 1 - bb, loads)
                key_hi(n, 0, lay, g)
                queries_hi(n, b_ps, SCALE0)
                key_hi(n, 1, lay, g)
                if not last:
                    split_h(n + 1, b + 1)
                exps(n, 0)
                key_hi(n, 2, lay, g)
                exps(n, 1)
                probs_out(n, 0)
                key_hi(n, 3, lay, g)
                if last:
                    split_block(WV, 0, 2 * w + 3)
                probs_out(n, 1)
                exps(n, 2)
                probs_out(n, 2)
                exps(n, 3)
                probs_out(n, 3)
                heads_hi(n)
                if last:
                    split_block(WQ, 1, 2 * w + 3)

            def norm(times):
                act.wait_ge(ln_step, LN_STEPS * times + 2 * B + 1 + CREDIT)
                act.activation(rstd[:, 1, :], rstd[:, 0, :], ACT.Sqrt).then_inc(root, 1)

            def input_out(times, par_at):
                for i in range(B // 2):
                    act.wait_ge(ht_mm, times * B + 2 * i + 1 + CREDIT)
                    settle(act)
                    for c in range(C):
                        cols = a_ps[:, c * S:(c + 1) * S]
                        if par_at is None:
                            act.activation(hT[:, c, 2 * i, :], cols, ACT.Copy).then_inc(ht_even, 1)
                        else:
                            act.activation(hT[:, c, 2 * i, :], cols, ACT.Identity,
                                           scale=par[:, bass.ds(par_at + c, 1)],
                                           bias=par[:, bass.ds(par_at + C + c, 1)]).then_inc(ht_even, 1)

            split_context(0, 0, 1)
            split_block(WV, 0, 1)
            split_block(WQ, 1, 1)
            with act.Fori(0, LAYERS) as lay:
                norm(lay)
                input_out(lay, P_NORM + lay * 2 * C)
                with act.Fori(0, G) as g:
                    w = lay * G + g
                    split_block(WK, 0, 2 * w + 2)
                    act.wait_ge(ht_even, B * C // 2 * (lay + 1) + CREDIT)
                    act.wait_ge(ht_odd, B * C // 2 * (lay + 1) + CREDIT)
                    split_h(w * B, 0)
                    act.wait_ge(y_mm, B * w + CREDIT)
                    split_block(WO, 1, 2 * w + 2)
                    with act.Fori(0, B // 2 - 1) as bp:
                        t = w * (B // 2) + bp
                        for bb in range(2):
                            body(2 * t + bb, bb, 2 * bp + bb, lay, g, w, t + 1 + bb, False)
                    t = w * (B // 2) + B // 2 - 1
                    for bb in range(2):
                        body(2 * t + bb, bb, B - 2 + bb, lay, g, w, t + 1 + bb, bb == 1)
            if stop_after == "L0":
                return

            norm(LAYERS)
            input_out(LAYERS, P_NORM + LAYERS * 2 * C)
            act.wait_ge(ht_even, B * C // 2 * (LAYERS + 1) + CREDIT)
            act.wait_ge(ht_odd, B * C // 2 * (LAYERS + 1) + CREDIT)
            act.wait_ge(y_mm, BODIES + CREDIT)
            for c in range(C):
                for half in range(2):
                    cols = slice(half * HB * S, (half + 1) * HB * S)
                    act.activation(hm_s[:, 0, c, cols], hT[:, c, half * HB:(half + 1) * HB, :].rearrange("p b q -> p (b q)"),
                                   ACT.Copy).then_inc(hm_hi, 1)
            with act.Fori(0, MG) as m:
                for half in range(2):
                    for f in range(FT):
                        k = half * FT + f
                        cols = slice(half * HB * S, (half + 1) * HB * S)
                        act.wait_ge(fc1_mm, 2 * FT * m + k + 1 + CREDIT)
                        act.wait_ge(g_lo, 2 * FT * m + k - 1 + CREDIT)
                        settle(act)
                        act.activation(gelu[:, k % 2, :], bank[k % 4][:, 0:HB * S], ACT.Gelu,
                                       bias=par[:, bass.ds(P_FC1 + m * FT + f, 1)]).then_inc(gelu_done, 1)
                        act.wait_ge(gelu_done, 2 * FT * m + k + 1 + CREDIT)
                        act.activation(g_s[:, 0, f, cols], gelu[:, k % 2, :], ACT.Copy).then_inc(g_hi, 1)
                split_block(W1, 0, MLP_BLOCK // 2 + m + 2)
                act.wait_ge(fc2_mm, B * (m + 1) + CREDIT)
                split_block(W2, 1, MLP_BLOCK // 2 + m + 2)

            act.wait_ge(wkv_loaded, 16)
            act.wait_ge(fc2_mm, MG * B + CREDIT)
            act.activation(wk1_s[:, 0].rearrange("p c n -> p (c n)"), wkv_raw[:, 0].rearrange("p c n -> p (c n)"),
                           ACT.Copy).then_inc(w_hi, 1)

            act.wait_ge(pick_loaded, 16)
            act.activation(pick, pick_raw, ACT.Copy).then_inc(pick_out, 1)

            def split_context1(i, slot, loads):
                act.wait_ge(ctx_loaded[slot], 16 * loads)
                act.wait_ge(kc_mm, i - 1 + CREDIT)
                act.activation(ctx_s[:, slot, 0, :, 1:T1], ctx_raw[:, slot], ACT.Copy).then_inc(ctx_hi, 1)

            def input_hi(i):
                act.wait_ge(ht_mm, (LAYERS + 1) * B + i + 1 + CREDIT)
                act.wait_ge(q_mm, BODIES + i + CREDIT)
                act.activation(hb_s[:, 0], b_ps[:, 0:C * S].rearrange("p (c q) -> p c q", c=C), ACT.Copy).then_inc(hb_hi, 1)

            def keys1_hi(i):
                act.wait_ge(kc_mm, i + 1 + CREDIT)
                act.wait_ge(kh_out, KV * i + CREDIT)
                act.activation(kh_s[:, 0, 1:T1], c_ps[:, 1:T1], ACT.Identity, bias=par[:, P_BK1:P_BK1 + 1]).then_inc(k1_hi, 1)

            def picked_out(i, c):
                act.wait_ge(pick_mm, PAIRS * i + c + 1 + CREDIT)
                if i is not FIRST:
                    act.wait_ge(s1_mm, J * (KV * (i - 1) + PAIRS + c + 1) + CREDIT)
                act.activation(qh_all[:, c], (b_ps, c_ps)[c % 2][:, 0:J * S].rearrange("p (j q) -> p j q", j=J), ACT.Copy).then_inc(qh_out, 1)

            def exps1(i, slot, k, js):
                act.wait_ge(nmax1, KV * i + k + 1 + CREDIT)
                for j in js:
                    p = p_sb[:, k % 2 * J + j, 0:T]
                    act.activation(p, p, ACT.Exp, bias=nmax[:, k % 2, j:j + 1],
                                   accum_out=zsum1[:, slot, j, ORDER[k]:ORDER[k] + 1]).then_inc(exp1, 1)

            def probs1_out(i, slot, k, t):
                if t == 0:
                    act.wait_ge(pv1_mm, 2 * i + SLOT_FREE[k] + CREDIT)
                act.wait_ge(t1_mm, NT * (KV * i + k) + t + 1 + CREDIT)
                act.activation(pT1[slot][k][:, t, :], t1_ps[t][:, 0:J * S], ACT.Copy).then_inc(pt1_out, 1)

            def sums_wide(i, slot, last):
                act.wait_ge(z1_inv, i + 1 + CREDIT)
                act.wait_ge(qt_mm, BODIES + i + (1 if last else 2) + CREDIT)
                act.activation(rz_wide, zsum1[:, slot].unsqueeze(3).broadcast_to([S, J, KV, HS]), ACT.Copy).then_inc(z_wide, 1)

            def sums_out(i):
                act.wait_ge(z_mm, i + 1 + CREDIT)
                act.wait_ge(o_lo, BODIES + i + CREDIT)
                act.activation(on_sb[:, :], b_ps[:, 0:J * S], ACT.Copy).then_inc(z_out, 1)

            def heads1_hi(i):
                act.wait_ge(o_norm, i + 1 + CREDIT)
                act.wait_ge(y_mm, BODIES + i + CREDIT)
                act.activation(oT_s[:, 0], on_sb[:, :].rearrange("p (j q) -> p j q", j=J), ACT.Copy).then_inc(o_hi, 1)

            def step(i, slot, k, late=None, soon=None, following=True):
                e = (i, slot, k + 1) if k + 1 < KV else (i + 1, 1 - slot, 0)
                probs1_out(i, slot, k, 0)
                if following:
                    exps1(*e, range(0, 1))
                if late:
                    late()
                probs1_out(i, slot, k, 2)
                if following:
                    exps1(*e, range(1, 4))
                if soon:
                    soon()

            def body1(i, slot, loads, last):
                if last:
                    for k in range(2, KV):
                        step(i, slot, k, following=k + 1 < KV)
                    sums_wide(i, slot, last)
                    sums_out(i)
                    heads1_hi(i)
                    return
                step(i, slot, 2, late=lambda: input_hi(i + 1))
                step(i, slot, 3, late=lambda: keys1_hi(i + 1))
                if loads is not None:
                    split_context1(i + 2, slot, loads)
                step(i, slot, 4, late=lambda: queries_hi(BODIES + i + 1, b_ps, SCALE1))
                step(i, slot, 5, soon=lambda: picked_out(i + 1, 0))
                step(i, slot, 6, late=lambda: picked_out(i + 1, 1), soon=lambda: picked_out(i + 1, 2))
                step(i, slot, 7, late=lambda: sums_wide(i, slot, last), soon=lambda: picked_out(i + 1, 3))
                step(i + 1, 1 - slot, 0, late=lambda: sums_out(i))
                heads1_hi(i)
                step(i + 1, 1 - slot, 1)

            input_hi(0)
            split_context1(1, 1, BODIES // 2 + 1)
            keys1_hi(0)
            queries_hi(BODIES, b_ps, SCALE1)
            for c in range(PAIRS):
                picked_out(FIRST, c)
            exps1(0, 0, 0, range(J))
            step(0, 0, 0)
            step(0, 0, 1)
            with act.Fori(0, B // 2 - 1) as t:
                for bb in range(2):
                    body1(2 * t + bb, bb, BODIES // 2 + t + 2, False)
            for bb in range(2):
                body1(B - 2 + bb, bb, None, bb == 1)
            norm(LAYERS + 1)

        @block.tensor
        def _(pe):
            credit(pe, by_pe)
            pe.wait_ge(consts, 5)

            def product(out, pairs, part=None):
                for i in part or range(len(pairs)):
                    l, r = pairs[i]
                    for k, (a, b) in enumerate(PASSES):
                        mm = pe.matmul(out, l(a), r(b), start=(i == 0 and k == 0),
                                       stop=(i == len(pairs) - 1 and k == len(PASSES) - 1))
                return mm

            def values(n, i, slot, w, part=None):
                first, rows = TILES[i]
                if i == 0:
                    pe.wait_ge(ctx_lo, n + 1 + CREDIT)
                    pe.wait_ge(w_lo, 16 * w + 4 + CREDIT)
                out = (a_ps, b_ps, a_ps)[i]
                if i == 2 and (part is None or 0 in part):
                    pe.wait_ge(v_out, NT * n + 1 + CREDIT)
                mm = product(out[0:rows, :], [
                    (lambda l, c=c: ctx_s[:, slot, l, c, first:first + rows], lambda l, c=c: w_of(WV, l)[:, c, :])
                    for c in range(C)], part)
                if part is None or C - 1 in part:
                    mm.then_inc(v_mm, 1)

            def queries(n, kind):
                pe.wait_ge(hb_lo, n + 1 + CREDIT)
                product(a_ps[0:S, :], [(lambda l, c=c: hb_s[:, l, c, :], lambda l, c=c: w_of(kind, l)[:, c, :])
                                       for c in range(C)]).then_inc(q_mm, 1)

            def queries_turn(n, out):
                pe.wait_ge(q_out, n + 1 + CREDIT)
                for h in range(HG):
                    mm = pe.transpose(out[:, h * S:(h + 1) * S], q_sb[:, h * P:(h + 1) * P], ident[0:S, 0:S])
                mm.then_inc(qt_mm, 1)

            def keys(n, h, slot):
                pe.wait_ge(k_lo, HG * n + h - 1 + CREDIT)
                product(k_ps[h % 2][:, 0:T1], [
                    (lambda l, c=c: w_of(WK, l)[:, c, h * P:(h + 1) * P], lambda l, c=c: ctx_s[:, slot, l, c, :])
                    for c in range(C)]).then_inc(k_mm, 1)

            def scores(n, h):
                pe.wait_ge(qt_lo, n + 1 + CREDIT)
                pe.wait_ge(k_lo, HG * n + h + 1 + CREDIT)
                pe.wait_ge(k_col, HG * n + h + 1 + CREDIT)
                pe.wait_ge(exp_done, HG * n + h - 1 + CREDIT)
                product(s_ps[h % 2][0:S, 0:T1], [(lambda l: qT_s[:, l, h, :], lambda l: kT_s[:, h % 2, l, :])]).then_inc(s_mm, 1)

            def probs_turn(n, h):
                pe.wait_ge(p_norm, HG * n + h + 1 + CREDIT)
                pe.wait_ge(pt_out, HG * n + h + CREDIT)
                for t in range(NT):
                    mm = pe.transpose(t_ps[:, t * S:(t + 1) * S], p_sb[:, h % 2, t * P:(t + 1) * P], ident[0:S, 0:S])
                mm.then_inc(t_mm, 1)

            def head_out(n, h, slot):
                pe.wait_ge(pt_out, HG * n + h + 1 + CREDIT)
                if h == 0:
                    pe.wait_ge(v_out, NT * (n + 1) + CREDIT)
                    pe.wait_ge(v_row, n + 1 + CREDIT)
                    pe.wait_ge(o_lo, n + CREDIT)
                for t, (_, rows) in enumerate(TILES):
                    mm = pe.matmul(o_ps[:, h * S:(h + 1) * S], v_sb[0:rows, slot, t, h * P:(h + 1) * P],
                                   pT_sb[0:rows, h % 2, t * S:(t + 1) * S], start=(t == 0), stop=(t == NT - 1))
                mm.then_inc(pv_mm, 1)

            def project(n, kind, bk=b_ps):
                pe.wait_ge(o_lo, n + 1 + CREDIT)
                product(bk[0:S, :], [(lambda l, h=h: oT_s[:, l, h, :], lambda l, h=h: w_of(kind, l)[:, h, :])
                                       for h in range(HG)]).then_inc(y_mm, 1)

            def body(n, bb, w, last):
                if bb == 0:
                    pe.wait_ge(w_lo, 16 * w + 8 + CREDIT)
                pe.wait_ge(v_out, NT * (n + 1) + CREDIT)
                queries(n, WQ)
                pe.wait_ge(w_lo, 16 * w + 12 + CREDIT)
                keys(n, 0, bb)
                pe.wait_ge(y_add, n + CREDIT)
                queries_turn(n, b_ps)
                keys(n, 1, bb)
                scores(n, 0)
                keys(n, 2, bb)
                scores(n, 1)
                probs_turn(n, 0)
                keys(n, 3, bb)
                head_out(n, 0, bb)
                probs_turn(n, 1)
                scores(n, 2)
                if not last:
                    values(n + 1, 0, 1 - bb, w)
                head_out(n, 1, bb)
                probs_turn(n, 2)
                scores(n, 3)
                if not last:
                    values(n + 1, 1, 1 - bb, w)
                head_out(n, 2, bb)
                probs_turn(n, 3)
                if not last:
                    values(n + 1, 2, 1 - bb, w, range(0, 1))
                head_out(n, 3, bb)
                if not last:
                    values(n + 1, 2, 1 - bb, w, range(1, C))
                pe.wait_ge(w_lo, 16 * w + 16 + CREDIT)
                if not last:
                    pe.wait_ge(v_out, NT * (n + 1) + 2 + CREDIT)
                project(n, WO)

            def turn_input(times):
                for b in range(B):
                    pe.wait_ge(hn_out, times * B + b + 1 + CREDIT)
                    if b % 2:
                        pe.wait_ge(ht_odd, C * (times * B // 2 + b // 2) + CREDIT)
                    else:
                        pe.wait_ge(ht_even, C * (times * B // 2 + b // 2) + CREDIT)
                    for c in range(C):
                        mm = pe.transpose((a_ps, b_ps)[b % 2][:, c * S:(c + 1) * S], hn[:, b % 2, c * P:(c + 1) * P],
                                          ident[0:S, 0:S])
                    mm.then_inc(ht_mm, 1)

            with pe.Fori(0, LAYERS) as lay:
                turn_input(lay)
                with pe.Fori(0, G) as g:
                    w = lay * G + g
                    pe.wait_ge(ht_even, B * C // 2 * (lay + 1) + CREDIT)
                    pe.wait_ge(ht_odd, B * C // 2 * (lay + 1) + CREDIT)
                    values(w * B, 0, 0, w)
                    pe.wait_ge(y_add, w * B + CREDIT)
                    values(w * B, 1, 0, w)
                    values(w * B, 2, 0, w)
                    with pe.Fori(0, B // 2 - 1) as bp:
                        for bb in range(2):
                            body(w * B + 2 * bp + bb, bb, w, False)
                    for bb in range(2):
                        body(w * B + B - 2 + bb, bb, w, bb == 1)
            if stop_after == "L0":
                return

            turn_input(LAYERS)
            with pe.Fori(0, MG) as m:
                pe.wait_ge(w_lo, 4 * (MLP_BLOCK + 2 * m + 1) + CREDIT)
                for half in range(2):
                    for f in range(FT):
                        k = half * FT + f
                        cols = slice(half * HB * S, (half + 1) * HB * S)
                        if k < FT * 2:
                            pe.wait_ge(hm_lo, 2 * C + CREDIT)
                        pe.wait_ge(gelu_done, 2 * FT * m + k - 3 + CREDIT)
                        product(bank[k % 4][:, 0:HB * S], [
                            (lambda l, c=c: w_of(W1, l)[:, c, f * P:(f + 1) * P], lambda l, c=c: hm_s[:, l, c, cols])
                            for c in range(C)]).then_inc(fc1_mm, 1)
                pe.wait_ge(w_lo, 4 * (MLP_BLOCK + 2 * m + 2) + CREDIT)
                for b in range(B):
                    pe.wait_ge(g_lo, 2 * FT * m + (FT if b < HB else 2 * FT) + CREDIT)
                    pe.wait_ge(m_add, B * m + b - 1 + CREDIT)
                    product(bank[4 + b % 2][0:S, :], [
                        (lambda l, f=f: g_s[:, l, f, b * S:(b + 1) * S], lambda l, f=f: w_of(W2, l)[:, f, :])
                        for f in range(FT)]).then_inc(fc2_mm, 1)

            pe.wait_ge(ht_even, B * C // 2 * (LAYERS + 1) + CREDIT)
            pe.wait_ge(ht_odd, B * C // 2 * (LAYERS + 1) + CREDIT)

            def input_turn(i):
                pe.wait_ge(x_taken, i + 1 + CREDIT)
                pe.wait_ge(z_out, i - 1 + CREDIT)
                for c in range(C):
                    mm = pe.transpose(b_ps[:, c * S:(c + 1) * S], xb_sb[:, c * P:(c + 1) * P], ident[0:S, 0:S])
                mm.then_inc(ht_mm, 1)

            def keys1(i, slot):
                pe.wait_ge(y_add, BODIES + i - 1 + CREDIT)
                pe.wait_ge(ctx_lo, BODIES + i + 1 + CREDIT)
                product(c_ps[:, 0:T1], [(lambda l, c=c: wk1_s[:, l, c, :], lambda l, c=c: ctx_s[:, slot, l, c, :])
                                        for c in range(C)]).then_inc(kc_mm, 1)

            def queries1(i):
                pe.wait_ge(hb_lo, BODIES + i + 1 + CREDIT)
                product(b_ps[0:S, :], [(lambda l, c=c: hb_s[:, l, c, :], lambda l, c=c: w_of(LQ, l)[:, c, :])
                                       for c in range(C)]).then_inc(q_mm, 1)

            def values1(i, slot, loads):
                pe.wait_ge(k1_lo, i + 1 + CREDIT)
                pe.wait_ge(ctx_loaded[slot], 16 * loads)
                for t in range(NT):
                    rows = P if t < NT - 1 else T - (NT - 1) * P
                    for c in range(C):
                        mm = pe.matmul(c_ps[0:rows, t * P:(t + 1) * P], ctx_raw[:, slot, c, t * P:t * P + rows],
                                       wkv_raw[:, 1, c, :], start=(c == 0), stop=(c == C - 1))
                mm.then_inc(vc_mm, 1)

            def pick_pair(i, c):
                if c == 0:
                    pe.wait_ge(qt_lo, BODIES + i + 1 + CREDIT)
                if c == 1:
                    pe.wait_ge(vc_out, i + 1 + CREDIT)
                if c >= 2:
                    pe.wait_ge(qh_out, PAIRS * i + c - 1 + CREDIT)
                for l in range(2):
                    first = c * P + 2 * HS * (1 - l)
                    mm = pe.matmul((b_ps, c_ps)[c % 2][:, 0:J * S], pick[:, first:first + P],
                                   qT_s[:, l, :, :].rearrange("p j q -> p (j q)"), start=(l == 0), stop=(l == 1))
                mm.then_inc(pick_mm, 1)

            def scores1(i, k, js):
                kv = ORDER[k]
                pe.wait_ge(qh_out, PAIRS * i + kv // 2 + 1 + CREDIT)
                pe.wait_ge(kh_out, KV * i + k + 1 + CREDIT)
                for j in js:
                    pe.wait_ge(rmax1, J * (KV * i + k) + j - 1 + CREDIT)
                    pe.matmul(s_ps[j % 2][0:S, 0:T1], qh_all[:, kv // 2, j, :], kh_all[:, kv, :],
                              start=True, stop=True).then_inc(s1_mm, 1)

            def probs1_turn(i, k):
                pe.wait_ge(exp1, J * (KV * i + k + 1) + CREDIT)
                for t in range(NT):
                    if t == 1:
                        pe.wait_ge(pt1_odd, KV * i + k + CREDIT)
                    else:
                        pe.wait_ge(pt1_out, 2 * (KV * i + k) + t // 2 - 1 + CREDIT)
                    for j in range(J):
                        mm = pe.transpose(t1_ps[t][:, j * S:(j + 1) * S],
                                          p_sb[:, k % 2 * J + j, t * P:(t + 1) * P], ident[0:S, 0:S])
                    mm.then_inc(t1_mm, 1)

            def heads1_out(i, slot, half):
                if half == 0:
                    pe.wait_ge(vc_out, i + 1 + CREDIT)
                    pe.wait_ge(o_norm, i + CREDIT)
                pe.wait_ge(pt1_out, 2 * (KV * i + PAIRS * (half + 1)) + CREDIT)
                pe.wait_ge(pt1_odd, KV * i + PAIRS * (half + 1) + CREDIT)
                for t in range(NT):
                    rows = P if t < NT - 1 else T - (NT - 1) * P
                    for c in range(PAIRS):
                        k = PAIRS * half + c
                        mm = pe.matmul(o_ps[2 * HS * c:2 * HS * (c + 1), 0:J * S], v_wide[0:rows, slot, t, ORDER[k], :],
                                       pT1[slot][k][0:rows, t, :], start=(half == 0 and t == 0), stop=(half == 1 and t == NT - 1))
                mm.then_inc(pv1_mm, 1)

            def sums_turn(i):
                pe.wait_ge(z_wide, i + 1 + CREDIT)
                for j in range(J):
                    mm = pe.transpose(b_ps[:, j * S:(j + 1) * S], q_sb[:, j * P:(j + 1) * P], ident[0:S, 0:S])
                mm.then_inc(z_mm, 1)

            def body1(i, slot, loads, last):
                probs1_turn(i, 2)
                scores1(i, 4, range(0, 2))
                if not last:
                    input_turn(i + 1)
                scores1(i, 4, range(2, 3))
                if not last:
                    keys1(i + 1, 1 - slot)
                scores1(i, 4, range(3, 4))

                probs1_turn(i, 3)
                scores1(i, 5, range(0, 2))
                if not last:
                    queries1(i + 1)
                scores1(i, 5, range(2, 4))

                probs1_turn(i, 4)
                scores1(i, 6, range(0, 2))
                if not last:
                    queries_turn(BODIES + i + 1, b_ps)
                scores1(i, 6, range(2, 3))
                heads1_out(i, slot, 0)
                scores1(i, 6, range(3, 4))

                probs1_turn(i, 5)
                scores1(i, 7, range(0, 2))
                if not last:
                    pick_pair(i + 1, 0)
                scores1(i, 7, range(2, 3))
                if not last:
                    values1(i + 1, 1 - slot, loads)
                scores1(i, 7, range(3, 4))

                probs1_turn(i, 6)
                if not last:
                    scores1(i + 1, 0, range(0, 2))
                    pick_pair(i + 1, 1)
                    scores1(i + 1, 0, range(2, 3))
                    pick_pair(i + 1, 2)
                    scores1(i + 1, 0, range(3, 4))

                probs1_turn(i, 7)
                if not last:
                    scores1(i + 1, 1, range(0, 2))
                    pick_pair(i + 1, 3)
                    scores1(i + 1, 1, range(2, 4))

                    probs1_turn(i + 1, 0)
                    scores1(i + 1, 2, range(0, 2))
                    pe.wait_ge(qh_out, PAIRS * (i + 1) + 3 + CREDIT)
                sums_turn(i)
                heads1_out(i, slot, 1)
                if not last:
                    scores1(i + 1, 2, range(2, 4))

                    probs1_turn(i + 1, 1)
                    scores1(i + 1, 3, range(0, 3))
                    pe.wait_ge(qh_out, PAIRS * (i + 2) + CREDIT)
                project(BODIES + i, LO, c_ps)
                if not last:
                    scores1(i + 1, 3, range(3, 4))

            pe.wait_ge(m_add, B * MG + CREDIT)
            input_turn(0)
            pe.wait_ge(w_lo, 4 * (LAST_BLOCK + 2) + 1 + CREDIT)
            keys1(0, 0)
            queries1(0)
            pe.wait_ge(wkv_loaded, 16)
            values1(0, 0, BODIES // 2 + 1)
            queries_turn(BODIES, b_ps)
            pe.wait_ge(pick_out, 1 + CREDIT)
            for c in range(PAIRS):
                pick_pair(0, c)
            scores1(0, 0, range(J))
            scores1(0, 1, range(J))
            pe.wait_ge(wide_zero, 2 + 2 * J + CREDIT)
            for k in range(2):
                probs1_turn(0, k)
                scores1(0, k + 2, range(J))
            with pe.Fori(0, B // 2 - 1) as t:
                for bb in range(2):
                    body1(2 * t + bb, bb, BODIES // 2 + t + 1 + bb, False)
            for bb in range(2):
                body1(B - 2 + bb, bb, BODIES // 2 + B // 2, bb == 1)

        @block.vector
        def _(dve):
            credit(dve, by_dve)
            dve.wait_ge(par_loaded, 16)

            def low(out_hi, out_lo, full, s_hi, count, s_lo):
                dve.wait_ge(s_hi, count + CREDIT)
                dve.tensor_tensor(out_lo, full, f32(out_hi), ALU.subtract).then_inc(s_lo, 1)

            def split_block(kind, slot, blocks, chunks=range(4)):
                for c in chunks:
                    cols = slice(c * D, (c + 1) * D)
                    low(w_split[:, kind, 0, cols], w_split[:, kind, 1, cols], w_raw[:, slot, cols], w_hi, 4 * blocks + c + 1, w_lo)

            def split_context(n, slot):
                low(ctx_s[:, slot, 0, :, 1:T1], ctx_s[:, slot, 1, :, 1:T1], ctx_raw[:, slot], ctx_hi, n + 1, ctx_lo)

            def split_h(n, b):
                low(hb_s[:, 0], hb_s[:, 1], hT[:, :, b, :], hb_hi, n + 1, hb_lo)

            def add_out(n, b, bk=b_ps):
                dve.wait_ge(y_mm, n + 1 + CREDIT)
                dve.tensor_tensor(x_sb[:, b, :], x_sb[:, b, :], bk[0:S, :], ALU.add).then_inc(y_add, 1)

            def queries_out(n, bk=a_ps):
                dve.wait_ge(q_mm, n + 1 + CREDIT)
                dve.tensor_tensor(q_sb[:, :], bk[0:S, :], wrow[0:S, 0, :], ALU.add).then_inc(q_out, 1)

            def queries_lo(n, bk, scale):
                dve.wait_ge(qt_hi, n + 1 + CREDIT)
                dve.scalar_tensor_tensor(qT_s[:, 1], bk[:, 0:HG * S].rearrange("p (h q) -> p h q", h=HG), scale,
                                         f32(qT_s[:, 0]), ALU.mult, ALU.subtract).then_inc(qt_lo, 1)

            def value_out(n, i, slot):
                dve.wait_ge(v_mm, NT * n + i + 1 + CREDIT)
                if i == 0:
                    dve.wait_ge(pv_mm, HG * (n - 1) + CREDIT)
                rows = TILES[i][1]
                dve.tensor_tensor(v_sb[0:rows, slot, i, :], (a_ps, b_ps, a_ps)[i][0:rows, :], wrow[0:rows, 1, :],
                                  ALU.add).then_inc(v_out, 1)

            def key_lo(n, h, lay, g):
                dve.wait_ge(k_hi, HG * n + h + 1 + CREDIT)
                dve.scalar_tensor_tensor(kT_s[:, h % 2, 1, 1:T1], k_ps[h % 2][:, 1:T1],
                                         par[:, bass.ds(lay * P_LAYER + P_BK + g * HG + h, 1)],
                                         f32(kT_s[:, h % 2, 0, 1:T1]), ALU.add, ALU.subtract).then_inc(k_lo, 1)

            def row_max(n, h):
                dve.wait_ge(s_mm, HG * n + h + 1 + CREDIT)
                dve.tensor_reduce(nmax[:, 0, h:h + 1], s_ps[h % 2][0:S, 0:T1], AX.X, ALU.max, negate=True).then_inc(max_done, 1)

            def normalise(n, h):
                dve.wait_ge(exp_done, HG * n + h + 1 + CREDIT)
                dve.reciprocal(rz[:, 0, h:h + 1], zsum[:, 0, h:h + 1]).then_inc(z_inv, 1)
                dve.wait_ge(z_inv, HG * n + h + 1 + CREDIT)
                dve.tensor_scalar(p_sb[:, h % 2, 0:T1], p_sb[:, h % 2, 0:T1], rz[:, 0, h:h + 1], None,
                                  ALU.mult).then_inc(p_norm, 1)

            def heads_lo(n):
                dve.wait_ge(o_hi, n + 1 + CREDIT)
                dve.tensor_tensor(oT_s[:, 1], o_ps[:, 0:HG * S].rearrange("p (h q) -> p h q", h=HG), f32(oT_s[:, 0]),
                                  ALU.subtract).then_inc(o_lo, 1)

            def body(n, bb, b, lay, g, w, last):
                split_context(n + 1, 1 - bb)
                queries_out(n)
                key_lo(n, 0, lay, g)
                queries_lo(n, b_ps, SCALE0)
                key_lo(n, 1, lay, g)
                row_max(n, 0)
                if not last:
                    split_h(n + 1, b + 1)
                normalise(n, 0)
                key_lo(n, 2, lay, g)
                row_max(n, 1)
                normalise(n, 1)
                key_lo(n, 3, lay, g)
                row_max(n, 2)
                if last:
                    split_block(WV, 0, 4 * w + 4)
                normalise(n, 2)
                if not last:
                    value_out(n + 1, 0, 1 - bb)
                row_max(n, 3)
                normalise(n, 3)
                if not last:
                    value_out(n + 1, 1, 1 - bb)
                heads_lo(n)
                if not last:
                    value_out(n + 1, 2, 1 - bb)
                else:
                    split_block(WQ, 1, 4 * w + 5)
                add_out(n, b)

            def norm(times, eps, first_batch_wait=None):
                base = LN_STEPS * times
                for b in range(B):
                    dve.bn_stats(stats[:, b, :], x_sb[:, b, :]).then_inc(ln_step, 1)
                for b in range(B):
                    dve.wait_ge(ln_step, base + b + 1 + CREDIT)
                    settle(dve)
                    dve.bn_aggr(mv[:, b, :], stats[:, b, :]).then_inc(ln_step, 1)
                dve.wait_ge(ln_step, base + 2 * B + CREDIT)
                dve.tensor_scalar(rstd[:, 0, :], mv[:, :, 1], eps, None, ALU.add).then_inc(ln_step, 1)
                dve.wait_ge(root, times + 1 + CREDIT)
                dve.reciprocal(rstd[:, 2, :], rstd[:, 1, :]).then_inc(ln_step, 1)
                r, a, v = rstd[:, 2, :], rstd[:, 1, :], rstd[:, 0, :]
                dve.wait_ge(ln_step, base + 2 * B + 2 + CREDIT)
                dve.tensor_tensor(a, r, r, ALU.mult).then_inc(ln_step, 1)
                dve.wait_ge(ln_step, base + 2 * B + 3 + CREDIT)
                dve.tensor_tensor(a, a, v, ALU.mult).then_inc(ln_step, 1)
                dve.wait_ge(ln_step, base + 2 * B + 4 + CREDIT)
                dve.tensor_scalar(a, a, -0.5, 1.5, ALU.mult, ALU.add).then_inc(ln_step, 1)
                dve.wait_ge(ln_step, base + 2 * B + 5 + CREDIT)
                dve.tensor_tensor(r, r, a, ALU.mult).then_inc(ln_step, 1)
                dve.wait_ge(ln_step, base + LN_STEPS + CREDIT)

            def normed(times, b):
                dve.wait_ge(ht_mm, times * B + b - 1 + CREDIT)
                dve.tensor_scalar(hn[:, b % 2, :], x_sb[:, b, :], mv[:, b, 0:1], rstd[:, 2, b:b + 1],
                                  ALU.subtract, ALU.mult).then_inc(hn_out, 1)

            def input_odd(times, b, par_at):
                dve.wait_ge(ht_mm, times * B + b + 1 + CREDIT)
                for c in range(C):
                    cols = b_ps[:, c * S:(c + 1) * S]
                    if par_at is None:
                        dve.tensor_copy(hT[:, c, b, :], cols).then_inc(ht_odd, 1)
                    else:
                        dve.tensor_scalar(hT[:, c, b, :], cols, par[:, bass.ds(par_at + c, 1)],
                                          par[:, bass.ds(par_at + C + c, 1)], ALU.mult, ALU.add).then_inc(ht_odd, 1)

            def input_norm(times, par_at):
                norm(times, EPS0)
                for b in range(B):
                    normed(times, b)
                    if b % 2 == 0 and b:
                        input_odd(times, b - 1, par_at)
                input_odd(times, B - 1, par_at)

            split_context(0, 0)
            split_block(WV, 0, 0)
            split_block(WQ, 1, 1)
            dve.wait_ge(x_loaded, 16)
            with dve.Fori(0, LAYERS) as lay:
                dve.wait_ge(y_add, lay * (BODIES // 2) + CREDIT)
                input_norm(lay, P_NORM + lay * 2 * C)
                dve.wait_ge(k_col, lay * (BODIES // 2) * HG + CREDIT)
                bias_k = par[:, bass.ds(lay * P_LAYER + P_BIASK, H)]
                dve.tensor_copy(kbias_s[:, 0, :], bias_k).then_inc(kbias, 1)
                low(kbias_s[:, 0, :], kbias_s[:, 1, :], bias_k, kbias, 2 * lay + 1, kbias)
                with dve.Fori(0, G) as g:
                    w = lay * G + g
                    split_block(WK, 0, 4 * w + 2)
                    split_h(w * B, 0)
                    dve.wait_ge(wrow_loaded, 16 * (w + 1))
                    value_out(w * B, 0, 0)
                    split_block(WO, 1, 4 * w + 3, range(0, 2))
                    value_out(w * B, 1, 0)
                    split_block(WO, 1, 4 * w + 3, range(2, 4))
                    value_out(w * B, 2, 0)
                    dve.wait_ge(bo_add, B * (lay + 1) + CREDIT)
                    settle(dve)
                    with dve.Fori(0, B // 2 - 1) as bp:
                        for bb in range(2):
                            body(w * B + 2 * bp + bb, bb, 2 * bp + bb, lay, g, w, False)
                    for bb in range(2):
                        body(w * B + B - 2 + bb, bb, B - 2 + bb, lay, g, w, bb == 1)
            if stop_after == "L0":
                return

            dve.wait_ge(y_add, BODIES + CREDIT)
            input_norm(LAYERS, P_NORM + LAYERS * 2 * C)
            for c in range(C):
                for half in range(2):
                    cols = slice(half * HB * S, (half + 1) * HB * S)
                    low(hm_s[:, 0, c, cols], hm_s[:, 1, c, cols],
                        hT[:, c, half * HB:(half + 1) * HB, :].rearrange("p b q -> p (b q)"), hm_hi, 2 * c + half + 1, hm_lo)
            dve.wait_ge(bo_add, B * (LAYERS + 1) + CREDIT)
            with dve.Fori(0, MG) as m:
                for half in range(2):
                    for f in range(FT):
                        k = half * FT + f
                        cols = slice(half * HB * S, (half + 1) * HB * S)
                        low(g_s[:, 0, f, cols], g_s[:, 1, f, cols], gelu[:, k % 2, :], g_hi, 2 * FT * m + k + 1, g_lo)
                for b in range(B):
                    if b == 2:
                        split_block(W1, 0, MLP_BLOCK + 2 * m + 2)
                    dve.wait_ge(fc2_mm, B * m + b + 1 + CREDIT)
                    dve.tensor_tensor(x_sb[:, b, :], x_sb[:, b, :], bank[4 + b % 2][0:S, :], ALU.add).then_inc(m_add, 1)
                split_block(W2, 1, MLP_BLOCK + 2 * m + 3)

            low(wk1_s[:, 0].rearrange("p c n -> p (c n)"), wk1_s[:, 1].rearrange("p c n -> p (c n)"),
                wkv_raw[:, 0].rearrange("p c n -> p (c n)"), w_hi, 4 * (LAST_BLOCK + 2) + 1, w_lo)

            def values1_out(i, slot):
                dve.wait_ge(vc_mm, i + 1 + CREDIT)
                dve.wait_ge(pv1_mm, 2 * i - 2 + CREDIT)
                for t in range(NT):
                    rows = P if t < NT - 1 else T - (NT - 1) * P
                    for a in range(2):
                        dst = v_wide[0:rows, slot, t, a::2, a * HS:(a + 1) * HS]
                        src = c_ps[0:rows, t * P:(t + 1) * P].rearrange("p (c n) -> p c n", c=PAIRS)
                        bias = wrow[0:rows, 1, 0:P].rearrange("p (c n) -> p c n", c=PAIRS)
                        ins = dve.tensor_tensor(dst, src[:, :, a * HS:(a + 1) * HS], bias[:, :, a * HS:(a + 1) * HS], ALU.add)
                ins.then_inc(vc_out, 1)

            def input_lo(i):
                low(hb_s[:, 0], hb_s[:, 1], b_ps[:, 0:C * S].rearrange("p (c q) -> p c q", c=C), hb_hi, BODIES + i + 1, hb_lo)

            def keys1_lo(i):
                dve.wait_ge(k1_hi, i + 1 + CREDIT)
                dve.scalar_tensor_tensor(kh_s[:, 1, 1:T1], c_ps[:, 1:T1], par[:, P_BK1:P_BK1 + 1],
                                         f32(kh_s[:, 0, 1:T1]), ALU.add, ALU.subtract).then_inc(k1_lo, 1)

            def masked(i, slot, k, js=range(J)):
                dve.wait_ge(t1_mm, NT * (KV * i + k - 1) + CREDIT)
                for j in js:
                    dve.wait_ge(s1_mm, J * (KV * i + k) + j + 1 + CREDIT)
                    settle(dve)
                    dve.tensor_tensor_reduce(p_sb[:, k % 2 * J + j, 0:T], s_ps[j % 2][0:S, 1:T1],
                                             mask_sb[:, slot, :], 1.0, -3.4e38, ALU.add, ALU.max,
                                             rmax[:, k % 2, j:j + 1]).then_inc(rmax1, 1)
                if js[-1] == J - 1:
                    dve.wait_ge(rmax1, J * (KV * i + k + 1) + CREDIT)
                    dve.tensor_scalar(nmax[:, k % 2, :], rmax[:, k % 2, :], -1.0, None, ALU.mult).then_inc(nmax1, 1)

            def probs1_odd(i, slot, k):
                dve.wait_ge(pv1_mm, 2 * i + SLOT_FREE[k] + CREDIT)
                dve.wait_ge(t1_mm, NT * (KV * i + k) + 2 + CREDIT)
                dve.tensor_copy(pT1[slot][k][:, 1, :], t1_ps[1][:, 0:J * S]).then_inc(pt1_odd, 1)

            def sums_inverse(i, slot):
                dve.wait_ge(exp1, J * KV * (i + 1) + CREDIT)
                dve.reciprocal(zsum1[:, slot], zsum1[:, slot]).then_inc(z1_inv, 1)

            def heads1_norm(i):
                dve.wait_ge(z_out, i + 1 + CREDIT)
                dve.wait_ge(pv1_mm, 2 * (i + 1) + CREDIT)
                dve.tensor_tensor(on_sb[:, :], o_ps[:, 0:J * S], on_sb[:, :], ALU.mult).then_inc(o_norm, 1)

            def heads1_lo(i):
                low(oT_s[:, 0], oT_s[:, 1], on_sb[:, :].rearrange("p (j q) -> p j q", j=J), o_hi, BODIES + i + 1, o_lo)

            def step(i, slot, k, late=None, soon=None, following=True):
                m = (i, slot, k + 2) if k + 2 < KV else (i + 1, 1 - slot, k + 2 - KV)
                if following:
                    masked(*m, range(0, 2))
                probs1_odd(i, slot, k)
                if late:
                    late()
                if following:
                    masked(*m, range(2, 4))
                if soon:
                    soon()

            def body1(i, slot, loads, last):
                if last:
                    for k in range(2, KV):
                        if k == 7:
                            sums_inverse(i, slot)
                        step(i, slot, k, following=k + 2 < KV)
                    heads1_norm(i)
                    heads1_lo(i)
                    dve.wait_ge(bo_add, B * (LAYERS + 1) + i + 1 + CREDIT)
                    add_out(BODIES + i, i, c_ps)
                    return
                step(i, slot, 2, soon=lambda: input_lo(i + 1))
                step(i, slot, 3, late=lambda: keys1_lo(i + 1), soon=lambda: queries_out(BODIES + i + 1, b_ps))
                step(i, slot, 4, soon=lambda: queries_lo(BODIES + i + 1, b_ps, SCALE1))
                step(i, slot, 5, soon=lambda: values1_out(i + 1, 1 - slot))
                dve.wait_ge(mask_loaded[1 - slot], 16 * B // 2 if loads is None else 16 * (loads - 1 + slot))
                step(i, slot, 6)
                sums_inverse(i, slot)
                step(i, slot, 7)
                step(i + 1, 1 - slot, 0, late=lambda: heads1_norm(i), soon=lambda: heads1_lo(i))
                step(i + 1, 1 - slot, 1)
                dve.wait_ge(bo_add, B * (LAYERS + 1) + i + 1 + CREDIT)
                add_out(BODIES + i, i, c_ps)

            input_lo(0)
            keys1_lo(0)
            dve.wait_ge(wrow_loaded, 16 * (SETS + 1))
            queries_out(BODIES, b_ps)
            dve.wait_ge(wide_zero, 2 + CREDIT)
            values1_out(0, 0)
            queries_lo(BODIES, b_ps, SCALE1)
            dve.wait_ge(mask_loaded[0], 16)
            masked(0, 0, 0)
            masked(0, 0, 1)
            step(0, 0, 0)
            step(0, 0, 1)
            with dve.Fori(0, B // 2 - 1) as t:
                for bb in range(2):
                    body1(2 * t + bb, bb, t + 2, False)
            for bb in range(2):
                body1(B - 2 + bb, bb, None, bb == 1)
            dve.wait_ge(y_add, BODIES + B + CREDIT)
            norm(LAYERS + 1, EPS1)
            dve.wait_ge(gb_loaded, 16)
            for b in range(B):
                dve.tensor_scalar(x_sb[:, b, :], x_sb[:, b, :], mv[:, b, 0:1], rstd[:, 2, b:b + 1],
                                  ALU.subtract, ALU.mult).then_inc(m_add, 1)
                dve.wait_ge(m_add, B * MG + 2 * b + 1 + CREDIT)
                dve.tensor_tensor(x_sb[:, b, :], x_sb[:, b, :], gb[:, 0, :], ALU.mult).then_inc(m_add, 1)
                dve.wait_ge(m_add, B * MG + 2 * b + 2 + CREDIT)
                dve.tensor_tensor(x_sb[:, b, :], x_sb[:, b, :], gb[:, 1, :], ALU.add).then_inc(fin, 1)


def lay_out(a):
    f = {k: np.asarray(v) for k, v in a.items()}

    def w_in(w):
        return w.reshape(C, P, -1).transpose(1, 0, 2).reshape(P, -1)

    L = lambda name, i: f[f"L0_xattn_{name}{i + 1}"]
    blocks = []
    for i in range(LAYERS):
        for g in range(G):
            cols = slice(g * D, (g + 1) * D)
            blocks += [w_in(L(n, i)[:, cols]) for n in ("wv", "wq", "wk")] + [w_in(L("wo", i)[cols, :])]
    for m in range(MG):
        cols = slice(m * D, (m + 1) * D)
        blocks += [w_in(f["L0_xattn_w_fc1"][:, cols]), w_in(f["L0_xattn_w_fc2"][cols, :])]
    by_j = lambda v: v.reshape(v.shape[:-1] + (KV, J, HS)).swapaxes(-3, -2).reshape(v.shape)
    blocks += [w_in(by_j(f["L1_xattn_Wq"])), w_in(by_j(f["L1_xattn_Wo"].T).T)]
    wkv = np.concatenate([w_in(f["L1_xattn_Wk"]), w_in(f["L1_xattn_Wv"])], axis=1)
    col = lambda v: v.reshape(-1, P).T
    par = []
    for i in range(LAYERS):
        par += [col(L("bk", i)), col(L("bias_k", i))]
    for s, o in (("ln1_scale", "ln1_offset"), ("ln2_scale", "ln2_offset"), ("ln_mlp_scale", "ln_mlp_offset")):
        par += [col(f["L0_xattn_" + s]), col(f["L0_xattn_" + o])]
    par += [col(f["L0_xattn_b_fc1"]), col(f["L1_xattn_bk"])]
    pick = np.zeros((PAIRS, 2, HS, PICK), np.float32)
    for c in range(PAIRS):
        for a in range(2):
            for part in range(2):
                for d in range(HS):
                    pick[c, a, d, 2 * HS + c * P + a * 4 * HS + part * HS + d] = 1
    rows = np.stack([L("bo", 0), L("bo", 1), f["L0_xattn_b_fc2"], f["L1_xattn_bo"]])
    wrow = [np.stack([L(n, i).reshape(-1)[g * D:(g + 1) * D] for n in ("bq", "bv", "bias_v")])
            for i in range(LAYERS) for g in range(G)]
    last = np.zeros((3, D), np.float32)
    last[0] = by_j(f["L1_xattn_bq"])
    last[1, 0:KV * HS] = f["L1_xattn_bv"]
    ctx = f["ctx_2048"].reshape(B, T, C, P).transpose(0, 3, 2, 1)
    return {
        "x": f["x"], "ctx": ctx, "mask": f["mask_Bx1xSxS2_ff0"].reshape(B, S, T), "w": np.stack(blocks),
        "wkv": wkv.reshape(P, 2, C, P), "par": np.concatenate(par, axis=1),
        "pick": pick.reshape(P, PICK), "rows": rows,
        "wrow": np.stack(wrow + [last]), "gb": np.stack([f["L1_xattn_gamma"], f["L1_xattn_beta"]]),
    }


def kernel(**inputs):
    import concourse.bacc as bacc
    from concourse.bass_utils import run_bass_kernel_spmd

    nc = bacc.Bacc("TRN2", target_bir_lowering=False, num_devices=1)
    arrays = {f"in_{k}": np.ascontiguousarray(v) for k, v in lay_out(inputs).items()}
    args = [nc.dram_tensor(k, v.shape, mybir.dt.from_np(v.dtype), kind="ExternalInput").ap() for k, v in arrays.items()]
    out = nc.dram_tensor("out", (B, S, D), F32, kind="ExternalOutput").ap()
    build(nc, *args, out)
    r = run_bass_kernel_spmd(nc, [arrays], core_ids=[0])
    return r.results[0]["out"]
```

```python
from contextlib import ExitStack

import numpy as np
import concourse.bass as bass
from concourse import mybir
from concourse.alu_op_type import AluOpType as ALU

F32 = mybir.dt.float32
F32R = mybir.dt.float32r
ACT = mybir.ActivationFunctionType
AX = mybir.AxisListType

P = 128
B, S, D = 8, 112, 512
T = 375
T1 = T + 1
C = D // P
LAYERS = 2
H, HD = 16, 128
G = 4
HG = H // G
TILES = [(0, 128), (128, 128), (256, T1 - 256)]
NT = len(TILES)
F = 2048
MG = F // D
FT = D // P
KV, HS = 8, 16
J = 4
PAIRS = KV // 2
ORDER = [2 * p + a for a in range(2) for p in range(PAIRS)]
PICK = 2 * HS + PAIRS * P
HB = B // 2
SETS = LAYERS * G
BODIES = SETS * B
MLP_BLOCK = SETS * 4
LAST_BLOCK = MLP_BLOCK + 2 * MG
SCALE0 = float(HD) ** -0.5
SCALE1 = float(HS) ** -0.5
EPS0, EPS1 = 1e-5, 1e-6
CREDIT = 8
FIRST = 0
LN_STEPS = B + 6
LAST_STEPS = LN_STEPS * (LAYERS + 1)
PASSES = ((0, 0), (0, 1), (1, 0))

P_BK, P_BIASK, P_LAYER = 0, H, 2 * H
P_NORM = LAYERS * P_LAYER
P_FC1 = P_NORM + 3 * 2 * C
P_BK1 = P_FC1 + F // P
P_ALL = P_BK1 + 1


def build(nc, x_d, ctx_d, mask_d, w_d, wkv_d, par_d, pick_d, rows_d, wrow_d, gb_d, out_d, stop_after=None):
    st = ExitStack()
    with st:
        def sb(name, shape, dt=F32):
            return st.enter_context(nc.sbuf_tensor(name, shape, dt))

        def sem(name):
            return st.enter_context(nc.semaphore(name))

        def f32(ap):
            return ap.bitcast(F32)

        bank = [st.enter_context(nc.psum_tensor(f"bank{i}", [P, 512], F32)) for i in range(8)]
        k_ps, s_ps, t_ps, o_ps, a_ps, b_ps = bank[0:2], bank[2:4], bank[4], bank[5], bank[6], bank[7]
        x_sb = sb("x_sb", [S, B, D])
        hT = sb("hT", [P, C, B, S])
        w_split = sb("w_split", [P, 4, 2, 4 * D], F32R)
        w_raw = sb("w_raw", [P, 2, 4 * D])
        ctx_raw = sb("ctx_raw", [P, 2, C, T])

        sizes = [2 * 2 * C * T1, 2 * C * S, 2 * HG * S, 2 * 2 * T1, 2 * HG * S]
        arena_r = sb("arena_r", [P, sum(sizes)], F32R)
        at = [sum(sizes[:i]) for i in range(6)]
        ctx_s = arena_r[:, at[0]:at[1]].rearrange("p (s l c t) -> p s l c t", s=2, l=2, c=C)
        hb_s = arena_r[:, at[1]:at[2]].rearrange("p (l c q) -> p l c q", l=2, c=C)
        qT_s = arena_r[:, at[2]:at[3]].rearrange("p (l h q) -> p l h q", l=2, h=HG)
        kT_s = arena_r[:, at[3]:at[4]].rearrange("p (s l t) -> p s l t", s=2, l=2)
        oT_s = arena_r[:, at[4]:at[5]].rearrange("p (l h q) -> p l h q", l=2, h=HG)
        half_ctx = at[1] // 2
        hm_s = arena_r[:, half_ctx:half_ctx + 2 * C * B * S].rearrange("p (l c n) -> p l c n", l=2, c=C)
        g_s = w_split[:, 2:4].rearrange("p k l n -> p (k l n)")[:, 0:2 * FT * B * S].rearrange(
            "p (l f n) -> p l f n", l=2, f=FT)

        kbias_s = sb("kbias_s", [P, 2, H], F32R)
        v_all = sb("v_all", [P, 2 * NT * D])
        v_sb = v_all[:, :].rearrange("p (s i n) -> p s i n", s=2, i=NT)
        q_sb = sb("q_sb", [S, D])
        p_sb = sb("p_sb", [S, 2 * J, NT * P])
        kh_s = sb("kh_s", [P, 2, T1], F32R)
        pT_sb = f32(kh_s[:, :, :].rearrange("p l t -> p (l t)"))[:, 0:2 * NT * S].rearrange("p (s n) -> p s n", s=2)
        hn = v_sb[0:S, 1, 0:2, :]
        gelu = v_sb[:, 0, 0:2, 0:HB * S]
        ident = sb("ident", [P, P])
        par = sb("par", [P, P_ALL])
        wrow = sb("wrow", [P, 3, D])
        bo_bc = sb("bo_bc", [S, D])
        stats = sb("stats", [S, B, 6])
        mv = sb("mv", [S, B, 2])
        rstd = sb("rstd", [S, 3, B])
        nmax = sb("nmax", [S, 2, J])
        rmax = sb("rmax", [S, 2, J])
        zsum = sb("zsum", [S, 2, J])
        rz = sb("rz", [S, 2, J])
        wkv_raw = w_raw[:, 0, 0:2 * C * P].rearrange("p (k c n) -> p k c n", k=2, c=C)
        own = w_split[:, 2:4].rearrange("p k l n -> p (k l n)")
        own_sizes = [KV * T1, PAIRS * J * S, 2 * C * P, PICK]
        own_at = [sum(own_sizes[:i]) for i in range(5)]
        kh_all = own[:, own_at[0]:own_at[1]].rearrange("p (k t) -> p k t", k=KV)
        qh_all = own[:, own_at[1]:own_at[2]].rearrange("p (c j q) -> p c j q", c=PAIRS, j=J)
        wk1_s = own[:, own_at[2]:own_at[3]].rearrange("p (l c n) -> p l c n", l=2, c=C)
        pick = own[:, own_at[3]:own_at[4]]
        VW = NT * KV * 2 * HS
        v_wide = v_all[:, 0:2 * VW].rearrange("p (s i k n) -> p s i k n", s=2, i=NT, k=KV)
        PT = NT * J * S
        raw = w_raw[:, :, :].rearrange("p s n -> p (s n)")
        hT_flat = hT[:, :, :, :].rearrange("p c b q -> p (c b q)")
        free = [raw[:, 2 * C * P:2 * C * P + PT], raw[:, 2 * C * P + PT:2 * C * P + 2 * PT], hT_flat[:, 0:PT],
                hT_flat[:, PT:2 * PT], v_all[:, 2 * VW:2 * VW + PT]]
        pT1 = [[free[k].rearrange("p (i n) -> p i n", i=NT) for k in order]
               for order in ((0, 1, 2, 3, 4, 0, 1, 2), (3, 4, 0, 1, 2, 3, 4, 1))]
        SLOT_FREE = (-1, 0, 0, 0, 0, 1, 1, 1)
        xb_sb = hT_flat[0:S, 2 * PT:2 * PT + D]
        k_rows = [raw[:, 2 * C * P + 2 * PT:2 * C * P + 2 * PT + T], hT_flat[:, 2 * PT + D:2 * PT + D + T]]
        pick_raw = hT_flat[:, 0:PICK]
        c_ps, t1_ps = bank[1], (t_ps, a_ps, bank[0])
        on_sb = sb("on_sb", [P, J * S])
        zsum1 = sb("zsum1", [S, 2, J, KV])
        rz_wide = q_sb[:, :].rearrange("s (j k d) -> s j k d", j=J, k=KV)
        mask_sb = sb("mask_sb", [S, 2, T])
        gb = wrow[0:S, 1:3, :]

        x_loaded, par_loaded, out_stored, consts = sem("x_loaded"), sem("par_loaded"), sem("out_stored"), sem("consts")
        waited = sem("waited")
        ctx_loaded = [sem("ctx_loaded0"), sem("ctx_loaded1")]
        w_loaded = [sem("w_loaded0"), sem("w_loaded1")]
        mask_loaded = [sem("mask_loaded0"), sem("mask_loaded1")]
        bo_loaded, wrow_loaded, gb_loaded, wkv_loaded = sem("bo_loaded"), sem("wrow_loaded"), sem("gb_loaded"), sem("wkv_loaded")
        pick_loaded = sem("pick_loaded")
        by_sp = {n: sem(n) for n in ("rows_loaded0", "rows_loaded1")}
        rows_loaded = list(by_sp.values())
        by_pe = {n: sem(n) for n in ("q_mm", "qt_mm", "k_mm", "s_mm", "t_mm", "pv_mm", "v_mm", "y_mm", "ht_mm",
                                     "fc1_mm", "fc2_mm", "vc_mm", "kc_mm", "s1_mm", "t1_mm", "pv1_mm",
                                     "pick_mm", "z_mm")}
        by_act = {n: sem(n) for n in ("w_hi", "ctx_hi", "hb_hi", "qt_hi", "k_hi", "exp_done", "pt_out", "o_hi", "root",
                                      "ht_even", "hm_hi", "gelu_done", "g_hi", "k1_hi", "exp1", "pt1_out", "qh_out", "z_out", "pick_out")}
        by_dve = {n: sem(n) for n in ("w_lo", "ctx_lo", "hb_lo", "q_out", "qt_lo", "k_lo", "max_done", "z_inv", "p_norm",
                                      "v_out", "o_lo", "y_add", "ln_step", "row_step", "hn_out", "ht_odd", "kbias", "hm_lo", "g_lo",
                                      "vc_out", "k1_lo", "rmax1", "nmax1", "z1_inv", "z_wide", "pt1_odd", "o_norm", "m_add", "fin")}
        by_pool = {n: sem(n) for n in ("k_col", "v_row", "bo_add", "pool_step", "wide_zero", "x_taken", "kh_out")}
        q_mm, qt_mm, k_mm, s_mm, t_mm, pv_mm, v_mm, y_mm, ht_mm, fc1_mm, fc2_mm, vc_mm, kc_mm, s1_mm, t1_mm, pv1_mm, pick_mm, z_mm = by_pe.values()
        (w_hi, ctx_hi, hb_hi, qt_hi, k_hi, exp_done, pt_out, o_hi, root, ht_even, hm_hi, gelu_done, g_hi, k1_hi, exp1,
         pt1_out, qh_out, z_out, pick_out) = by_act.values()
        (w_lo, ctx_lo, hb_lo, q_out, qt_lo, k_lo, max_done, z_inv, p_norm, v_out, o_lo, y_add, ln_step, row_step, hn_out, ht_odd,
         kbias, hm_lo, g_lo, vc_out, k1_lo, rmax1, nmax1, z1_inv, z_wide, pt1_odd, o_norm, m_add, fin) = by_dve.values()
        k_col, v_row, bo_add, pool_step, wide_zero, x_taken, kh_out = by_pool.values()

        def credit(eng, sems):
            for s in sems.values():
                eng.sem_inc(s, CREDIT)

        def settle(eng):
            eng.sem_inc(waited, 1)

        def w_of(kind, lo):
            return w_split[:, kind, lo, :].rearrange("p (c n) -> p c n", c=4)

        WV, WQ, WK, WO = range(4)
        W1, W2 = 0, 1
        LQ, LO = 0, 1

        block = st.enter_context(nc.Block())

        @block.sync
        def _(sp):
            def context(n, b, slot):
                sp.wait_ge(ctx_lo, n - 1 + CREDIT)
                sp.dma_start(ctx_raw[:, slot], ctx_d[b]).then_inc(ctx_loaded[slot], 16)

            credit(sp, by_sp)
            sp.dma_start(ctx_raw[:, 0], ctx_d[0]).then_inc(ctx_loaded[0], 16)
            sp.dma_start(w_raw[:, 0, :], w_d[0]).then_inc(w_loaded[0], 16)
            sp.dma_start(par[:, :], par_d).then_inc(par_loaded, 16)
            sp.dma_start(x_sb[:, :, :], x_d.rearrange("b s d -> s b d")).then_inc(x_loaded, 16)
            sp.dma_start(w_raw[:, 1, :], w_d[1]).then_inc(w_loaded[1], 16)
            sp.dma_start(ctx_raw[:, 1], ctx_d[1]).then_inc(ctx_loaded[1], 16)
            with sp.Fori(0, LAYERS) as lay:
                sp.wait_ge(bo_add, lay * B + CREDIT)
                sp.dma_start(bo_bc[:, :], rows_d[lay, :].partition_broadcast(S)).then_inc(bo_loaded, 16)
                with sp.Fori(0, G) as g:
                    w = lay * G + g
                    sp.wait_ge(q_out, w * B + CREDIT)
                    sp.wait_ge(v_out, w * B * NT + CREDIT)
                    sp.wait_ge(v_row, w * B + CREDIT)
                    sp.dma_start(wrow[:, :, :], wrow_d[w].partition_broadcast(P)).then_inc(wrow_loaded, 16)
                    for j in range(2, 6):
                        sp.wait_ge(w_lo, 16 * w + 4 * (j - 1) + CREDIT)
                        sp.dma_start(w_raw[:, j % 2, :], w_d[4 * w + j]).then_inc(w_loaded[j % 2], 16)
                    with sp.Fori(0, B // 2 - 1) as bp:
                        for bb in range(2):
                            context(w * B + 2 * bp + bb + 2, 2 * bp + bb + 2, bb)
                    for bb in range(2):
                        context(w * B + B + bb, bb, bb)
            if stop_after == "L0":
                sp.wait_ge(y_add, BODIES + CREDIT)
                sp.dma_start(out_d.rearrange("b s d -> s b d"), x_sb[:, :, :]).then_inc(out_stored, 16)
                sp.wait_ge(out_stored, 16)
                for s in range(2):
                    sp.wait_ge(ctx_loaded[s], 16 * (BODIES // 2 + 1))
                    sp.wait_ge(w_loaded[s], 16 * (MLP_BLOCK // 2 + 1))
                return
            sp.wait_ge(bo_add, LAYERS * B + CREDIT)
            sp.dma_start(bo_bc[:, :], rows_d[LAYERS, :].partition_broadcast(S)).then_inc(bo_loaded, 16)
            with sp.Fori(0, MG) as m:
                for j in range(2):
                    sp.wait_ge(w_lo, 4 * (MLP_BLOCK + 2 * m + j + 1) + CREDIT)
                    sp.dma_start(w_raw[:, j, :], w_d[MLP_BLOCK + 2 * m + j + 2]).then_inc(w_loaded[j], 16)
            sp.wait_ge(bo_add, (LAYERS + 1) * B + CREDIT)
            sp.dma_start(bo_bc[:, :], rows_d[LAYERS + 1, :].partition_broadcast(S)).then_inc(bo_loaded, 16)
            sp.dma_start(wrow[:, :, :], wrow_d[SETS].partition_broadcast(P)).then_inc(wrow_loaded, 16)
            for s in range(2):
                sp.dma_start(mask_sb[:, s, :], mask_d[s]).then_inc(mask_loaded[s], 16)
            sp.wait_ge(w_lo, 4 * (LAST_BLOCK + 1) + CREDIT)
            sp.dma_start(wkv_raw, wkv_d).then_inc(wkv_loaded, 16)
            sp.wait_ge(hm_lo, 2 * C + CREDIT)
            sp.dma_start(pick_raw, pick_d).then_inc(pick_loaded, 16)

            def keys_of(i):
                sp.wait_ge(k1_lo, i + 1 + CREDIT)
                for k in range(KV):
                    kv = ORDER[k]
                    sp.wait_ge(kh_out, KV * i + k - 1 + CREDIT)
                    for part in range(4):
                        first = kv % 2 * 4 * HS + part * HS
                        sp.dma_start(k_rows[k % 2][first:first + HS, :], f32(kh_s[kv * HS:(kv + 1) * HS, part % 2, 1:T1])
                                     ).then_inc(rows_loaded[k % 2], 16)

            sp.wait_ge(w_lo, 4 * (LAST_BLOCK + 2) + CREDIT)
            keys_of(0)
            with sp.Fori(0, B // 2 - 1) as t:
                for bb in range(2):
                    i = 2 * t + bb
                    sp.wait_ge(vc_mm, i + 1 + CREDIT)
                    settle(sp)
                    context(BODIES + i + 2, i + 2, bb)
                    keys_of(i + 1)
                    sp.wait_ge(rmax1, KV * J * (i + 1) + CREDIT)
                    sp.dma_start(mask_sb[:, bb, :], mask_d[i + 2]).then_inc(mask_loaded[bb], 16)
            keys_of(B - 1)
            sp.wait_ge(vc_out, B + CREDIT)
            sp.dma_start(gb, gb_d.partition_broadcast(S)).then_inc(gb_loaded, 16)
            for b in range(B):
                sp.wait_ge(fin, b + 1 + CREDIT)
                sp.dma_start(out_d[b], x_sb[:, b, :]).then_inc(out_stored, 16)
            sp.wait_ge(out_stored, 16 * B)

        @block.gpsimd
        def _(pool):
            credit(pool, by_pool)
            pool.memset(ident[:, :], 0.0).then_inc(pool_step, 1)
            pool.wait_ge(pool_step, 1 + CREDIT)
            pool.affine_select(out=ident[:, :], in_=ident[:, :], compare_op=ALU.not_equal, fill=1.0, base=0,
                               pattern=[[-1, P]], channel_multiplier=1).then_inc(consts, 1)
            for s in range(2):
                pool.memset(f32(ctx_s[:, s, :, :, 0:1]), 0.0).then_inc(consts, 1)
                pool.memset(p_sb[:, s, T1:NT * P], 0.0).then_inc(consts, 1)

            def add_bias_rows(times):
                pool.wait_ge(bo_loaded, (times + 1) * 16)
                for b in range(B):
                    pool.wait_ge(hn_out, times * B + b + 1 + CREDIT)
                    pool.tensor_tensor(x_sb[:, b, :], x_sb[:, b, :], bo_bc[:, :], ALU.add).then_inc(bo_add, 1)

            def body(n, bb, g):
                pool.wait_ge(v_out, NT * n + 1 + CREDIT)
                settle(pool)
                pool.tensor_copy(v_sb[0:1, bb, 0, :], wrow[0:1, 2, :]).then_inc(v_row, 1)
                for h in range(HG):
                    pool.wait_ge(s_mm, HG * n + h - 1 + CREDIT)
                    settle(pool)
                    pool.tensor_copy(kT_s[:, h % 2, :, 0:1], f32(kbias_s[:, :, bass.ds(g * HG + h, 1)])).then_inc(k_col, 1)

            with pool.Fori(0, LAYERS) as lay:
                add_bias_rows(lay)
                pool.wait_ge(kbias, 2 * lay + 2 + CREDIT)
                settle(pool)
                with pool.Fori(0, G) as g:
                    w = lay * G + g
                    pool.wait_ge(wrow_loaded, (w + 1) * 16)
                    settle(pool)
                    with pool.Fori(0, B // 2) as bp:
                        for bb in range(2):
                            body(w * B + bp * 2 + bb, bb, g)
            if stop_after == "L0":
                return
            add_bias_rows(LAYERS)
            for s in range(2 * J):
                pool.memset(p_sb[:, s, T:NT * P], 0.0).then_inc(wide_zero, 1)

            def take_x(b):
                pool.wait_ge(ht_mm, (LAYERS + 1) * B + b + CREDIT)
                settle(pool)
                pool.tensor_copy(xb_sb.unsqueeze(1), x_sb[:, bass.ds(b, 1), :]).then_inc(x_taken, 1)
                pool.tensor_tensor(x_sb[:, bass.ds(b, 1), :], x_sb[:, bass.ds(b, 1), :], bo_bc[:, :].unsqueeze(1),
                                   ALU.add).then_inc(bo_add, 1)

            pool.wait_ge(bo_loaded, (LAYERS + 2) * 16)
            pool.wait_ge(m_add, (MG - 1) * B + 1 + CREDIT)
            take_x(0)
            pool.wait_ge(fc2_mm, MG * B + CREDIT)
            pool.memset(f32(own[:, 0:own_at[1]]), 0.0).then_inc(wide_zero, 1)
            pool.memset(v_all[:, 0:2 * VW], 0.0).then_inc(wide_zero, 1)
            pool.wait_ge(m_add, MG * B + CREDIT)

            def context_lo(i, slot):
                pool.wait_ge(ctx_hi, BODIES + i + 1 + CREDIT)
                settle(pool)
                pool.tensor_tensor(ctx_s[:, slot, 1, :, 1:T1], ctx_raw[:, slot], f32(ctx_s[:, slot, 0, :, 1:T1]),
                                   ALU.subtract).then_inc(ctx_lo, 1)

            def keys_out(i, ks, ctxs):
                for k in ks:
                    kv = ORDER[k]
                    rows = slice(kv % 2 * 4 * HS, (kv % 2 + 1) * 4 * HS)
                    if kv % 2:
                        pool.wait_ge(kh_out, KV * i + k + CREDIT)
                        pool.wait_ge(ctx_lo, BODIES + ctxs + CREDIT)
                    pool.wait_ge(rows_loaded[k % 2], 64 * (KV // 2 * i + k // 2 + 1) + CREDIT)
                    if i is not FIRST:
                        pool.wait_ge(s1_mm, J * (KV * (i - 1) + k + 1) + CREDIT)
                    settle(pool)
                    pool.tensor_copy(kh_all[rows, kv, 1:T1], k_rows[k % 2][rows, :]).then_inc(kh_out, 1)
                if KV - 1 in ks:
                    pool.wait_ge(kh_out, KV * (i + 1) + CREDIT)

            context_lo(1, 1)
            pool.wait_ge(wide_zero, 2 * J + 2 + CREDIT)
            keys_out(FIRST, range(KV), 2)
            take_x(1)
            with pool.Fori(0, B // 2 - 1) as t:
                for bb in range(2):
                    i = 2 * t + bb
                    take_x(i + 2)
                    keys_out(i + 1, range(0, 4), i + 2)
                    context_lo(i + 2, bb)
                    keys_out(i + 1, range(4, KV), i + 3)
            keys_out(B - 1, range(KV), B)

        @block.scalar
        def _(act):
            credit(act, by_act)

            def split_block(kind, slot, loads, chunks=range(4)):
                act.wait_ge(w_loaded[slot], loads * 16)
                for c in chunks:
                    cols = slice(c * D, (c + 1) * D)
                    act.activation(w_split[:, kind, 0, cols], w_raw[:, slot, cols], ACT.Copy).then_inc(w_hi, 1)

            def split_context(n, slot, loads):
                act.wait_ge(ctx_loaded[slot], 16 * loads)
                act.wait_ge(k_mm, HG * (n - 1) + CREDIT)
                act.activation(ctx_s[:, slot, 0, :, 1:T1], ctx_raw[:, slot], ACT.Copy).then_inc(ctx_hi, 1)

            def split_h(n, b):
                act.wait_ge(q_mm, n + CREDIT)
                settle(act)
                act.activation(hb_s[:, 0], hT[:, :, b, :], ACT.Copy).then_inc(hb_hi, 1)

            def key_hi(n, h, lay, g):
                act.wait_ge(k_mm, HG * n + h + 1 + CREDIT)
                act.wait_ge(s_mm, HG * n + h - 1 + CREDIT)
                settle(act)
                act.activation(kT_s[:, h % 2, 0, 1:T1], k_ps[h % 2][:, 1:T1], ACT.Identity,
                               bias=par[:, bass.ds(lay * P_LAYER + P_BK + g * HG + h, 1)]).then_inc(k_hi, 1)

            def exps(n, h):
                act.wait_ge(max_done, HG * n + h + 1 + CREDIT)
                act.wait_ge(t_mm, HG * n + h - 1 + CREDIT)
                act.activation(p_sb[:, h % 2, 0:T1], s_ps[h % 2][0:S, 0:T1], ACT.Exp, bias=nmax[:, 0, h:h + 1],
                               accum_out=zsum[:, 0, h:h + 1]).then_inc(exp_done, 1)

            def probs_out(n, h):
                act.wait_ge(t_mm, HG * n + h + 1 + CREDIT)
                act.wait_ge(pv_mm, HG * n + h - 1 + CREDIT)
                act.activation(pT_sb[:, h % 2, :], t_ps[:, 0:NT * S], ACT.Copy).then_inc(pt_out, 1)

            def heads_hi(n):
                act.wait_ge(pv_mm, HG * (n + 1) + CREDIT)
                act.wait_ge(y_mm, n + CREDIT)
                act.activation(oT_s[:, 0], o_ps[:, 0:HG * S].rearrange("p (h q) -> p h q", h=HG),
                               ACT.Copy).then_inc(o_hi, 1)

            def queries_hi(n, bk, scale):
                act.wait_ge(qt_mm, n + 1 + CREDIT)
                act.activation(qT_s[:, 0], bk[:, 0:HG * S].rearrange("p (h q) -> p h q", h=HG), ACT.Copy,
                               scale=scale).then_inc(qt_hi, 1)

            def body(n, bb, b, lay, g, w, loads, last=False, last_group=False):
                split_context(n + 1, 1 - bb, loads)
                if last:
                    act.wait_ge(v_mm, NT * (n + 1) + CREDIT)
                    split_block(WV, 0, 2 * w + 3)
                key_hi(n, 0, lay, g)
                queries_hi(n, b_ps, SCALE0)
                key_hi(n, 1, lay, g)
                if not last_group:
                    split_h(n + 1, 0 if last else b + 1)
                exps(n, 0)
                key_hi(n, 2, lay, g)
                probs_out(n, 0)
                exps(n, 1)
                key_hi(n, 3, lay, g)
                if last:
                    split_block(WQ, 1, 2 * w + 3)
                probs_out(n, 1)
                exps(n, 2)
                probs_out(n, 2)
                exps(n, 3)
                probs_out(n, 3)
                if last and not last_group:
                    split_block(WK, 0, 2 * w + 4)
                heads_hi(n)

            def norm(times, count, first=0, end=B):
                act.wait_ge(ln_step, count + CREDIT)
                act.activation(rstd[:, 1, first:end], rstd[:, 0, first:end], ACT.Sqrt).then_inc(root, 1)

            def input_out(times, par_at, turns=range(B // 2)):
                for i in turns:
                    act.wait_ge(ht_mm, times * B + 2 * i + 1 + CREDIT)
                    settle(act)
                    for c in range(C):
                        cols = a_ps[:, c * S:(c + 1) * S]
                        act.activation(hT[:, c, 2 * i, :], cols, ACT.Identity, scale=par[:, bass.ds(par_at + c, 1)],
                                       bias=par[:, bass.ds(par_at + C + c, 1)]).then_inc(ht_even, 1)

            def group(lay, g, last_group):
                w = lay * G + g
                act.wait_ge(y_mm, B * w + CREDIT)
                split_block(WO, 1, 2 * w + 2)
                with act.Fori(0, B // 2 - 1) as bp:
                    t = w * (B // 2) + bp
                    for bb in range(2):
                        body(2 * t + bb, bb, 2 * bp + bb, lay, g, w, t + 1 + bb)
                t = w * (B // 2) + B // 2 - 1
                for bb in range(2):
                    body(2 * t + bb, bb, B - 2 + bb, lay, g, w, t + 1 + bb, bb == 1, bb == 1 and last_group)

            split_context(0, 0, 1)
            split_block(WV, 0, 1)
            split_block(WQ, 1, 1)
            act.wait_ge(par_loaded, 16)
            with act.Fori(0, LAYERS) as lay:
                norm(lay, LN_STEPS * lay + B + 1)
                input_out(lay, P_NORM + lay * 2 * C, range(0, 1))
                act.wait_ge(ht_even, C * (B // 2 * lay + 1) + CREDIT)
                split_h(lay * BODIES // 2, 0)
                input_out(lay, P_NORM + lay * 2 * C, range(1, B // 2))
                act.wait_ge(ht_even, B * C // 2 * (lay + 1) + CREDIT)
                act.wait_ge(ht_odd, B * C // 2 * (lay + 1) + CREDIT)
                split_block(WK, 0, 2 * G * lay + 2)
                with act.Fori(0, G - 1) as g:
                    group(lay, g, False)
                group(lay, G - 1, True)
            if stop_after == "L0":
                return

            norm(LAYERS, LN_STEPS * LAYERS + B + 1)
            act.wait_ge(y_mm, BODIES + CREDIT)
            for half in range(2):
                turns = range(half * HB // 2, (half + 1) * HB // 2)
                input_out(LAYERS, P_NORM + LAYERS * 2 * C, turns)
                act.wait_ge(ht_even, C * (LAYERS * B // 2 + turns[-1] + 1) + CREDIT)
                act.wait_ge(ht_odd, C * (LAYERS * B // 2 + turns[-1] + 1) + CREDIT)
                cols = slice(half * HB * S, (half + 1) * HB * S)
                for c in range(C):
                    act.activation(hm_s[:, 0, c, cols], hT[:, c, half * HB:(half + 1) * HB, :].rearrange("p b q -> p (b q)"),
                                   ACT.Copy).then_inc(hm_hi, 1)
            with act.Fori(0, MG) as m:
                for half in range(2):
                    for f in range(FT):
                        k = half * FT + f
                        cols = slice(half * HB * S, (half + 1) * HB * S)
                        act.wait_ge(fc1_mm, 2 * FT * m + k + 1 + CREDIT)
                        act.wait_ge(g_lo, 2 * FT * m + k - 1 + CREDIT)
                        settle(act)
                        act.activation(gelu[:, k % 2, :], bank[k % 4][:, 0:HB * S], ACT.Gelu,
                                       bias=par[:, bass.ds(P_FC1 + m * FT + f, 1)]).then_inc(gelu_done, 1)
                        act.wait_ge(gelu_done, 2 * FT * m + k + 1 + CREDIT)
                        act.activation(g_s[:, 0, f, cols], gelu[:, k % 2, :], ACT.Copy).then_inc(g_hi, 1)
                split_block(W1, 0, MLP_BLOCK // 2 + m + 2)
                act.wait_ge(fc2_mm, B * (m + 1) + CREDIT)
                split_block(W2, 1, MLP_BLOCK // 2 + m + 2)

            act.wait_ge(wkv_loaded, 16)
            act.wait_ge(fc2_mm, MG * B + CREDIT)
            act.activation(wk1_s[:, 0].rearrange("p c n -> p (c n)"), wkv_raw[:, 0].rearrange("p c n -> p (c n)"),
                           ACT.Copy).then_inc(w_hi, 1)

            act.wait_ge(pick_loaded, 16)
            act.activation(pick, pick_raw, ACT.Copy).then_inc(pick_out, 1)

            def split_context1(i, slot, loads):
                act.wait_ge(ctx_loaded[slot], 16 * loads)
                act.wait_ge(kc_mm, i - 1 + CREDIT)
                act.activation(ctx_s[:, slot, 0, :, 1:T1], ctx_raw[:, slot], ACT.Copy).then_inc(ctx_hi, 1)

            def input_hi(i):
                act.wait_ge(ht_mm, (LAYERS + 1) * B + i + 1 + CREDIT)
                act.wait_ge(q_mm, BODIES + i + CREDIT)
                act.activation(hb_s[:, 0], b_ps[:, 0:C * S].rearrange("p (c q) -> p c q", c=C), ACT.Copy).then_inc(hb_hi, 1)

            def keys1_hi(i):
                act.wait_ge(kc_mm, i + 1 + CREDIT)
                act.wait_ge(kh_out, KV * i + CREDIT)
                act.activation(kh_s[:, 0, 1:T1], c_ps[:, 1:T1], ACT.Identity, bias=par[:, P_BK1:P_BK1 + 1]).then_inc(k1_hi, 1)

            def picked_out(i, c):
                act.wait_ge(pick_mm, PAIRS * i + c + 1 + CREDIT)
                if i is not FIRST:
                    act.wait_ge(s1_mm, J * (KV * (i - 1) + PAIRS + c + 1) + CREDIT)
                act.activation(qh_all[:, c], b_ps[:, 0:J * S].rearrange("p (j q) -> p j q", j=J), ACT.Copy).then_inc(qh_out, 1)

            def exps1(i, slot, k, js):
                act.wait_ge(nmax1, KV * i + k + 1 + CREDIT)
                for j in js:
                    p = p_sb[:, k % 2 * J + j, 0:T]
                    act.activation(p, p, ACT.Exp, bias=nmax[:, k % 2, j:j + 1],
                                   accum_out=zsum1[:, slot, j, ORDER[k]:ORDER[k] + 1]).then_inc(exp1, 1)

            def probs1_out(i, slot, k, t):
                if t == 0:
                    act.wait_ge(pv1_mm, 2 * i + SLOT_FREE[k] + CREDIT)
                act.wait_ge(t1_mm, NT * (KV * i + k) + t + 1 + CREDIT)
                act.activation(pT1[slot][k][:, t, :], t1_ps[t][:, 0:J * S], ACT.Copy).then_inc(pt1_out, 1)

            def sums_out(i):
                act.wait_ge(z_mm, i + 1 + CREDIT)
                act.wait_ge(o_lo, BODIES + i + CREDIT)
                act.activation(on_sb[:, :], c_ps[:, 0:J * S], ACT.Copy).then_inc(z_out, 1)

            def heads1_hi(i):
                act.wait_ge(o_norm, i + 1 + CREDIT)
                act.wait_ge(y_mm, BODIES + i + CREDIT)
                act.activation(oT_s[:, 0], on_sb[:, :].rearrange("p (j q) -> p j q", j=J), ACT.Copy).then_inc(o_hi, 1)

            def step(i, slot, k, late=None, soon=None, following=True):
                e = (i, slot, k + 1) if k + 1 < KV else (i + 1, 1 - slot, 0)
                probs1_out(i, slot, k, 0)
                if following:
                    exps1(*e, range(0, 1))
                if late:
                    late()
                probs1_out(i, slot, k, 2)
                if following:
                    exps1(*e, range(1, 4))
                if soon:
                    soon()

            def body1(i, slot, loads, last):
                if last:
                    for k in range(2, KV):
                        step(i, slot, k, following=k + 1 < KV)
                    sums_out(i)
                    norm(LAYERS + 1, LAST_STEPS + B, 0, B - 1)
                    heads1_hi(i)
                    return
                step(i, slot, 2, late=lambda: input_hi(i + 1))
                step(i, slot, 3, late=lambda: keys1_hi(i + 1))
                if loads is not None:
                    split_context1(i + 2, slot, loads)
                step(i, slot, 4, soon=lambda: queries_hi(BODIES + i + 1, b_ps, SCALE1))
                step(i, slot, 5, soon=lambda: picked_out(i + 1, 0))
                step(i, slot, 6, soon=lambda: picked_out(i + 1, 1))
                step(i, slot, 7, soon=lambda: picked_out(i + 1, 2))
                step(i + 1, 1 - slot, 0, late=lambda: sums_out(i), soon=lambda: picked_out(i + 1, 3))
                heads1_hi(i)
                step(i + 1, 1 - slot, 1)

            input_hi(0)
            split_context1(1, 1, BODIES // 2 + 1)
            keys1_hi(0)
            queries_hi(BODIES, b_ps, SCALE1)
            for c in range(PAIRS):
                picked_out(FIRST, c)
            exps1(0, 0, 0, range(J))
            step(0, 0, 0)
            step(0, 0, 1)
            with act.Fori(0, B // 2 - 1) as t:
                for bb in range(2):
                    body1(2 * t + bb, bb, BODIES // 2 + t + 2, False)
            for bb in range(2):
                body1(B - 2 + bb, bb, None, bb == 1)
            norm(LAYERS + 2, LAST_STEPS + LN_STEPS - 1 + 2, B - 1, B)

        @block.tensor
        def _(pe):
            credit(pe, by_pe)
            pe.wait_ge(consts, 5)

            def product(out, pairs, part=None):
                for i in part or range(len(pairs)):
                    l, r = pairs[i]
                    for k, (a, b) in enumerate(PASSES):
                        mm = pe.matmul(out, l(a), r(b), start=(i == 0 and k == 0),
                                       stop=(i == len(pairs) - 1 and k == len(PASSES) - 1))
                return mm

            def values(n, i, slot, w, part=None):
                first, rows = TILES[i]
                if i == 0:
                    pe.wait_ge(ctx_lo, n + 1 + CREDIT)
                    pe.wait_ge(w_lo, 16 * w + 4 + CREDIT)
                out = (a_ps, b_ps, a_ps)[i]
                if i == 2 and (part is None or 0 in part):
                    pe.wait_ge(v_out, NT * n + 1 + CREDIT)
                mm = product(out[0:rows, :], [
                    (lambda l, c=c: ctx_s[:, slot, l, c, first:first + rows], lambda l, c=c: w_of(WV, l)[:, c, :])
                    for c in range(C)], part)
                if part is None or C - 1 in part:
                    mm.then_inc(v_mm, 1)

            def queries(n, kind):
                pe.wait_ge(hb_lo, n + 1 + CREDIT)
                product(a_ps[0:S, :], [(lambda l, c=c: hb_s[:, l, c, :], lambda l, c=c: w_of(kind, l)[:, c, :])
                                       for c in range(C)]).then_inc(q_mm, 1)

            def queries_turn(n, out):
                pe.wait_ge(q_out, n + 1 + CREDIT)
                for h in range(HG):
                    mm = pe.transpose(out[:, h * S:(h + 1) * S], q_sb[:, h * P:(h + 1) * P], ident[0:S, 0:S])
                mm.then_inc(qt_mm, 1)

            def keys(n, h, slot):
                pe.wait_ge(k_lo, HG * n + h - 1 + CREDIT)
                product(k_ps[h % 2][:, 0:T1], [
                    (lambda l, c=c: w_of(WK, l)[:, c, h * P:(h + 1) * P], lambda l, c=c: ctx_s[:, slot, l, c, :])
                    for c in range(C)]).then_inc(k_mm, 1)

            def scores(n, h):
                pe.wait_ge(qt_lo, n + 1 + CREDIT)
                pe.wait_ge(k_lo, HG * n + h + 1 + CREDIT)
                pe.wait_ge(k_col, HG * n + h + 1 + CREDIT)
                pe.wait_ge(exp_done, HG * n + h - 1 + CREDIT)
                product(s_ps[h % 2][0:S, 0:T1], [(lambda l: qT_s[:, l, h, :], lambda l: kT_s[:, h % 2, l, :])]).then_inc(s_mm, 1)

            def probs_turn(n, h):
                pe.wait_ge(p_norm, HG * n + h + 1 + CREDIT)
                pe.wait_ge(pt_out, HG * n + h + CREDIT)
                for t in range(NT):
                    mm = pe.transpose(t_ps[:, t * S:(t + 1) * S], p_sb[:, h % 2, t * P:(t + 1) * P], ident[0:S, 0:S])
                mm.then_inc(t_mm, 1)

            def head_out(n, h, slot):
                pe.wait_ge(pt_out, HG * n + h + 1 + CREDIT)
                if h == 0:
                    pe.wait_ge(v_out, NT * (n + 1) + CREDIT)
                    pe.wait_ge(v_row, n + 1 + CREDIT)
                    pe.wait_ge(o_lo, n + CREDIT)
                for t, (_, rows) in enumerate(TILES):
                    mm = pe.matmul(o_ps[:, h * S:(h + 1) * S], v_sb[0:rows, slot, t, h * P:(h + 1) * P],
                                   pT_sb[0:rows, h % 2, t * S:(t + 1) * S], start=(t == 0), stop=(t == NT - 1))
                mm.then_inc(pv_mm, 1)

            def project(n, kind, bk=b_ps):
                pe.wait_ge(o_lo, n + 1 + CREDIT)
                product(bk[0:S, :], [(lambda l, h=h: oT_s[:, l, h, :], lambda l, h=h: w_of(kind, l)[:, h, :])
                                       for h in range(HG)]).then_inc(y_mm, 1)

            def body(n, bb, w, last=False, last_group=False):
                nxt = w + 1 if last else w
                if bb == 0:
                    pe.wait_ge(w_lo, 16 * w + 8 + CREDIT)
                pe.wait_ge(v_out, NT * (n + 1) + CREDIT)
                queries(n, WQ)
                pe.wait_ge(w_lo, 16 * w + 12 + CREDIT)
                keys(n, 0, bb)
                pe.wait_ge(y_add, n + CREDIT)
                queries_turn(n, b_ps)
                keys(n, 1, bb)
                scores(n, 0)
                keys(n, 2, bb)
                scores(n, 1)
                probs_turn(n, 0)
                keys(n, 3, bb)
                head_out(n, 0, bb)
                probs_turn(n, 1)
                scores(n, 2)
                if not last_group:
                    values(n + 1, 0, 1 - bb, nxt)
                head_out(n, 1, bb)
                probs_turn(n, 2)
                scores(n, 3)
                if not last_group:
                    values(n + 1, 1, 1 - bb, nxt)
                head_out(n, 2, bb)
                probs_turn(n, 3)
                if not last_group:
                    values(n + 1, 2, 1 - bb, nxt, range(0, 1))
                head_out(n, 3, bb)
                if not last_group:
                    values(n + 1, 2, 1 - bb, nxt, range(1, C))
                pe.wait_ge(w_lo, 16 * w + 16 + CREDIT)
                if not last_group:
                    pe.wait_ge(v_out, NT * (n + 1) + 2 + CREDIT)
                project(n, WO)

            def turn_input(times):
                for b in range(B):
                    pe.wait_ge(hn_out, times * B + b + 1 + CREDIT)
                    if b % 2:
                        pe.wait_ge(ht_odd, C * (times * B // 2 + b // 2) + CREDIT)
                    else:
                        pe.wait_ge(ht_even, C * (times * B // 2 + b // 2) + CREDIT)
                    for c in range(C):
                        mm = pe.transpose((a_ps, b_ps)[b % 2][:, c * S:(c + 1) * S], hn[:, b % 2, c * P:(c + 1) * P],
                                          ident[0:S, 0:S])
                    mm.then_inc(ht_mm, 1)

            def group(w, last_group):
                with pe.Fori(0, B // 2 - 1) as bp:
                    for bb in range(2):
                        body(w * B + 2 * bp + bb, bb, w)
                for bb in range(2):
                    body(w * B + B - 2 + bb, bb, w, bb == 1, bb == 1 and last_group)

            with pe.Fori(0, LAYERS) as lay:
                w = lay * G
                values(w * B, 0, 0, w)
                pe.wait_ge(y_add, w * B + CREDIT)
                values(w * B, 1, 0, w)
                values(w * B, 2, 0, w)
                pe.wait_ge(v_out, NT * (w * B + 1) + CREDIT)
                turn_input(lay)
                pe.wait_ge(ht_even, B * C // 2 * (lay + 1) + CREDIT)
                pe.wait_ge(ht_odd, B * C // 2 * (lay + 1) + CREDIT)
                settle(pe)
                with pe.Fori(0, G - 1) as g:
                    group(lay * G + g, False)
                group(lay * G + G - 1, True)
            if stop_after == "L0":
                return

            turn_input(LAYERS)
            with pe.Fori(0, MG) as m:
                pe.wait_ge(w_lo, 4 * (MLP_BLOCK + 2 * m + 1) + CREDIT)
                for half in range(2):
                    for f in range(FT):
                        k = half * FT + f
                        cols = slice(half * HB * S, (half + 1) * HB * S)
                        if f == 0:
                            pe.wait_ge(hm_lo, C * (half + 1) + CREDIT)
                        pe.wait_ge(gelu_done, 2 * FT * m + k - 3 + CREDIT)
                        product(bank[k % 4][:, 0:HB * S], [
                            (lambda l, c=c: w_of(W1, l)[:, c, f * P:(f + 1) * P], lambda l, c=c: hm_s[:, l, c, cols])
                            for c in range(C)]).then_inc(fc1_mm, 1)
                pe.wait_ge(w_lo, 4 * (MLP_BLOCK + 2 * m + 2) + CREDIT)
                for b in range(B):
                    pe.wait_ge(g_lo, 2 * FT * m + (FT if b < HB else 2 * FT) + CREDIT)
                    pe.wait_ge(m_add, B * m + b - 1 + CREDIT)
                    product(bank[4 + b % 2][0:S, :], [
                        (lambda l, f=f: g_s[:, l, f, b * S:(b + 1) * S], lambda l, f=f: w_of(W2, l)[:, f, :])
                        for f in range(FT)]).then_inc(fc2_mm, 1)

            pe.wait_ge(ht_even, B * C // 2 * (LAYERS + 1) + CREDIT)
            pe.wait_ge(ht_odd, B * C // 2 * (LAYERS + 1) + CREDIT)

            def input_turn(i):
                pe.wait_ge(x_taken, i + 1 + CREDIT)
                pe.wait_ge(qh_out, PAIRS * i + CREDIT)
                for c in range(C):
                    mm = pe.transpose(b_ps[:, c * S:(c + 1) * S], xb_sb[:, c * P:(c + 1) * P], ident[0:S, 0:S])
                mm.then_inc(ht_mm, 1)

            def keys1(i, slot):
                pe.wait_ge(y_add, BODIES + i - 1 + CREDIT)
                pe.wait_ge(ctx_lo, BODIES + i + 1 + CREDIT)
                product(c_ps[:, 0:T1], [(lambda l, c=c: wk1_s[:, l, c, :], lambda l, c=c: ctx_s[:, slot, l, c, :])
                                        for c in range(C)]).then_inc(kc_mm, 1)

            def queries1(i):
                pe.wait_ge(hb_lo, BODIES + i + 1 + CREDIT)
                product(b_ps[0:S, :], [(lambda l, c=c: hb_s[:, l, c, :], lambda l, c=c: w_of(LQ, l)[:, c, :])
                                       for c in range(C)]).then_inc(q_mm, 1)

            def values1(i, slot, loads, tiles=range(NT)):
                pe.wait_ge(k1_lo, i + 1 + CREDIT)
                pe.wait_ge(ctx_loaded[slot], 16 * loads)
                for t in tiles:
                    rows = P if t < NT - 1 else T - (NT - 1) * P
                    for c in range(C):
                        mm = pe.matmul(c_ps[0:rows, t * P:(t + 1) * P], ctx_raw[:, slot, c, t * P:t * P + rows],
                                       wkv_raw[:, 1, c, :], start=(c == 0), stop=(c == C - 1))
                if NT - 1 in tiles:
                    mm.then_inc(vc_mm, 1)

            def pick_pair(i, c):
                if c == 0:
                    pe.wait_ge(qt_lo, BODIES + i + 1 + CREDIT)
                else:
                    pe.wait_ge(qh_out, PAIRS * i + c + CREDIT)
                for l in range(2):
                    first = c * P + 2 * HS * (1 - l)
                    mm = pe.matmul(b_ps[:, 0:J * S], pick[:, first:first + P],
                                   qT_s[:, l, :, :].rearrange("p j q -> p (j q)"), start=(l == 0), stop=(l == 1))
                mm.then_inc(pick_mm, 1)

            def scores1(i, k, js):
                kv = ORDER[k]
                pe.wait_ge(qh_out, PAIRS * i + kv // 2 + 1 + CREDIT)
                pe.wait_ge(kh_out, KV * i + k + 1 + CREDIT)
                for j in js:
                    pe.wait_ge(rmax1, J * (KV * i + k) + j - 1 + CREDIT)
                    pe.matmul(s_ps[j % 2][0:S, 0:T1], qh_all[:, kv // 2, j, :], kh_all[:, kv, :],
                              start=True, stop=True).then_inc(s1_mm, 1)

            def probs1_turn(i, k):
                pe.wait_ge(exp1, J * (KV * i + k + 1) + CREDIT)
                for t in range(NT):
                    if t == 1:
                        pe.wait_ge(pt1_odd, KV * i + k + CREDIT)
                    else:
                        pe.wait_ge(pt1_out, 2 * (KV * i + k) + t // 2 - 1 + CREDIT)
                    for j in range(J):
                        mm = pe.transpose(t1_ps[t][:, j * S:(j + 1) * S],
                                          p_sb[:, k % 2 * J + j, t * P:(t + 1) * P], ident[0:S, 0:S])
                    mm.then_inc(t1_mm, 1)

            def heads1_out(i, slot, half):
                if half == 0:
                    pe.wait_ge(vc_out, i + 1 + CREDIT)
                    pe.wait_ge(o_norm, i + CREDIT)
                pe.wait_ge(pt1_out, 2 * (KV * i + PAIRS * (half + 1)) + CREDIT)
                pe.wait_ge(pt1_odd, KV * i + PAIRS * (half + 1) + CREDIT)
                for t in range(NT):
                    rows = P if t < NT - 1 else T - (NT - 1) * P
                    for c in range(PAIRS):
                        k = PAIRS * half + c
                        mm = pe.matmul(o_ps[2 * HS * c:2 * HS * (c + 1), 0:J * S], v_wide[0:rows, slot, t, ORDER[k], :],
                                       pT1[slot][k][0:rows, t, :], start=(half == 0 and t == 0), stop=(half == 1 and t == NT - 1))
                mm.then_inc(pv1_mm, 1)

            def sums_turn(i):
                pe.wait_ge(z_wide, i + 1 + CREDIT)
                for j in range(J):
                    mm = pe.transpose(c_ps[:, j * S:(j + 1) * S], q_sb[:, j * P:(j + 1) * P], ident[0:S, 0:S])
                mm.then_inc(z_mm, 1)

            def body1(i, slot, loads, last):
                probs1_turn(i, 2)
                scores1(i, 4, range(0, 2))
                if not last:
                    input_turn(i + 1)
                    keys1(i + 1, 1 - slot)
                scores1(i, 4, range(2, 4))

                probs1_turn(i, 3)
                scores1(i, 5, range(0, 2))
                if not last:
                    queries1(i + 1)
                scores1(i, 5, range(2, 4))

                probs1_turn(i, 4)
                scores1(i, 6, range(0, 2))
                heads1_out(i, slot, 0)
                if not last:
                    queries_turn(BODIES + i + 1, b_ps)
                scores1(i, 6, range(2, 4))

                probs1_turn(i, 5)
                scores1(i, 7, range(0, 2))
                if not last:
                    pick_pair(i + 1, 0)
                scores1(i, 7, range(2, 3))
                if not last:
                    values1(i + 1, 1 - slot, loads, range(0, 1))
                scores1(i, 7, range(3, 4))

                probs1_turn(i, 6)
                if not last:
                    scores1(i + 1, 0, range(0, 2))
                    pick_pair(i + 1, 1)
                    scores1(i + 1, 0, range(2, 3))
                    values1(i + 1, 1 - slot, loads, range(1, 2))
                    scores1(i + 1, 0, range(3, 4))

                probs1_turn(i, 7)
                if not last:
                    scores1(i + 1, 1, range(0, 2))
                    pick_pair(i + 1, 2)
                    scores1(i + 1, 1, range(2, 3))
                    values1(i + 1, 1 - slot, loads, range(2, 3))
                    scores1(i + 1, 1, range(3, 4))

                    probs1_turn(i + 1, 0)
                    scores1(i + 1, 2, range(0, 2))
                    pick_pair(i + 1, 3)
                    pe.wait_ge(vc_out, i + 2 + CREDIT)
                sums_turn(i)
                heads1_out(i, slot, 1)
                if not last:
                    scores1(i + 1, 2, range(2, 4))

                    probs1_turn(i + 1, 1)
                    scores1(i + 1, 3, range(0, 2))
                project(BODIES + i, LO, c_ps)
                if not last:
                    scores1(i + 1, 3, range(2, 4))

            input_turn(0)
            pe.wait_ge(w_lo, 4 * (LAST_BLOCK + 2) + 1 + CREDIT)
            keys1(0, 0)
            queries1(0)
            pe.wait_ge(wkv_loaded, 16)
            values1(0, 0, BODIES // 2 + 1)
            queries_turn(BODIES, b_ps)
            pe.wait_ge(pick_out, 1 + CREDIT)
            for c in range(PAIRS):
                pick_pair(0, c)
            scores1(0, 0, range(J))
            scores1(0, 1, range(J))
            pe.wait_ge(m_add, B * MG + CREDIT)
            for k in range(2):
                probs1_turn(0, k)
                scores1(0, k + 2, range(J))
            with pe.Fori(0, B // 2 - 1) as t:
                for bb in range(2):
                    body1(2 * t + bb, bb, BODIES // 2 + t + 1 + bb, False)
            for bb in range(2):
                body1(B - 2 + bb, bb, BODIES // 2 + B // 2, bb == 1)

        @block.vector
        def _(dve):
            credit(dve, by_dve)

            def low(out_hi, out_lo, full, s_hi, count, s_lo):
                dve.wait_ge(s_hi, count + CREDIT)
                dve.tensor_tensor(out_lo, full, f32(out_hi), ALU.subtract).then_inc(s_lo, 1)

            def split_block(kind, slot, blocks, chunks=range(4)):
                for c in chunks:
                    cols = slice(c * D, (c + 1) * D)
                    low(w_split[:, kind, 0, cols], w_split[:, kind, 1, cols], w_raw[:, slot, cols], w_hi, 4 * blocks + c + 1, w_lo)

            def split_context(n, slot):
                low(ctx_s[:, slot, 0, :, 1:T1], ctx_s[:, slot, 1, :, 1:T1], ctx_raw[:, slot], ctx_hi, n + 1, ctx_lo)

            def split_h(n, b):
                low(hb_s[:, 0], hb_s[:, 1], hT[:, :, b, :], hb_hi, n + 1, hb_lo)

            def add_out(n, b, bk=b_ps):
                dve.wait_ge(y_mm, n + 1 + CREDIT)
                dve.tensor_tensor(x_sb[:, b, :], x_sb[:, b, :], bk[0:S, :], ALU.add).then_inc(y_add, 1)

            def queries_out(n, bk=a_ps):
                dve.wait_ge(q_mm, n + 1 + CREDIT)
                dve.tensor_tensor(q_sb[:, :], bk[0:S, :], wrow[0:S, 0, :], ALU.add).then_inc(q_out, 1)

            def queries_lo(n, bk, scale):
                dve.wait_ge(qt_hi, n + 1 + CREDIT)
                dve.scalar_tensor_tensor(qT_s[:, 1], bk[:, 0:HG * S].rearrange("p (h q) -> p h q", h=HG), scale,
                                         f32(qT_s[:, 0]), ALU.mult, ALU.subtract).then_inc(qt_lo, 1)

            def value_out(n, i, slot):
                dve.wait_ge(v_mm, NT * n + i + 1 + CREDIT)
                if i == 0:
                    dve.wait_ge(pv_mm, HG * (n - 1) + CREDIT)
                rows = TILES[i][1]
                dve.tensor_tensor(v_sb[0:rows, slot, i, :], (a_ps, b_ps, a_ps)[i][0:rows, :], wrow[0:rows, 1, :],
                                  ALU.add).then_inc(v_out, 1)

            def key_lo(n, h, lay, g):
                dve.wait_ge(k_hi, HG * n + h + 1 + CREDIT)
                dve.scalar_tensor_tensor(kT_s[:, h % 2, 1, 1:T1], k_ps[h % 2][:, 1:T1],
                                         par[:, bass.ds(lay * P_LAYER + P_BK + g * HG + h, 1)],
                                         f32(kT_s[:, h % 2, 0, 1:T1]), ALU.add, ALU.subtract).then_inc(k_lo, 1)

            def row_max(n, h):
                dve.wait_ge(s_mm, HG * n + h + 1 + CREDIT)
                dve.tensor_reduce(nmax[:, 0, h:h + 1], s_ps[h % 2][0:S, 0:T1], AX.X, ALU.max, negate=True).then_inc(max_done, 1)

            def normalise(n, h):
                dve.wait_ge(exp_done, HG * n + h + 1 + CREDIT)
                dve.reciprocal(rz[:, 0, h:h + 1], zsum[:, 0, h:h + 1]).then_inc(z_inv, 1)
                dve.wait_ge(z_inv, HG * n + h + 1 + CREDIT)
                dve.tensor_scalar(p_sb[:, h % 2, 0:T1], p_sb[:, h % 2, 0:T1], rz[:, 0, h:h + 1], None,
                                  ALU.mult).then_inc(p_norm, 1)

            def heads_lo(n):
                dve.wait_ge(o_hi, n + 1 + CREDIT)
                dve.tensor_tensor(oT_s[:, 1], o_ps[:, 0:HG * S].rearrange("p (h q) -> p h q", h=HG), f32(oT_s[:, 0]),
                                  ALU.subtract).then_inc(o_lo, 1)

            def row_stats(b):
                dve.bn_stats(stats[:, b, :], x_sb[:, b, :]).then_inc(row_step, 1)

            def body(n, bb, b, lay, g, w, last=False, last_group=False):
                queries_out(n)
                split_context(n + 1, 1 - bb)
                key_lo(n, 0, lay, g)
                queries_lo(n, b_ps, SCALE0)
                if last:
                    split_block(WV, 0, 4 * w + 4, range(0, 2))
                row_max(n, 0)
                key_lo(n, 1, lay, g)
                if not last_group:
                    split_h(n + 1, 0 if last else b + 1)
                if last:
                    split_block(WV, 0, 4 * w + 4, range(2, 4))
                normalise(n, 0)
                row_max(n, 1)
                key_lo(n, 2, lay, g)
                normalise(n, 1)
                key_lo(n, 3, lay, g)
                row_max(n, 2)
                if last:
                    split_block(WQ, 1, 4 * w + 5, range(0, 2))
                normalise(n, 2)
                if last:
                    split_block(WQ, 1, 4 * w + 5, range(2, 4))
                if not last_group:
                    if last:
                        dve.wait_ge(wrow_loaded, 16 * (w + 2))
                    value_out(n + 1, 0, 1 - bb)
                row_max(n, 3)
                normalise(n, 3)
                if not last_group:
                    value_out(n + 1, 1, 1 - bb)
                if last and not last_group:
                    split_block(WK, 0, 4 * w + 6, range(0, 2))
                heads_lo(n)
                if last and not last_group:
                    split_block(WK, 0, 4 * w + 6, range(2, 4))
                if not last_group:
                    value_out(n + 1, 2, 1 - bb)
                add_out(n, b)
                dve.wait_ge(y_add, n + 1 + CREDIT)
                settle(dve)
                row_stats(b)

            def norm(times, eps, calls, base=None, first=0, end=B):
                if base is None:
                    base = LN_STEPS * times
                count = end - first
                dve.wait_ge(row_step, calls + CREDIT)
                settle(dve)
                for b in range(first, end):
                    dve.bn_aggr(mv[:, b, :], stats[:, b, :]).then_inc(ln_step, 1)
                r, a, v = rstd[:, 2, first:end], rstd[:, 1, first:end], rstd[:, 0, first:end]
                dve.wait_ge(ln_step, base + count + CREDIT)
                dve.tensor_scalar(v, mv[:, first:end, 1], eps, None, ALU.add).then_inc(ln_step, 1)
                dve.wait_ge(root, times + 1 + CREDIT)
                dve.reciprocal(r, a).then_inc(ln_step, 1)
                dve.wait_ge(ln_step, base + count + 2 + CREDIT)
                dve.tensor_tensor(a, r, r, ALU.mult).then_inc(ln_step, 1)
                dve.wait_ge(ln_step, base + count + 3 + CREDIT)
                dve.tensor_tensor(a, a, v, ALU.mult).then_inc(ln_step, 1)
                dve.wait_ge(ln_step, base + count + 4 + CREDIT)
                dve.tensor_scalar(a, a, -0.5, 1.5, ALU.mult, ALU.add).then_inc(ln_step, 1)
                dve.wait_ge(ln_step, base + count + 5 + CREDIT)
                dve.tensor_tensor(r, r, a, ALU.mult).then_inc(ln_step, 1)
                dve.wait_ge(ln_step, base + count + 6 + CREDIT)

            def normed(times, b):
                dve.wait_ge(ht_mm, times * B + b - 1 + CREDIT)
                dve.tensor_scalar(hn[:, b % 2, :], x_sb[:, b, :], mv[:, b, 0:1], rstd[:, 2, b:b + 1],
                                  ALU.subtract, ALU.mult).then_inc(hn_out, 1)

            def input_odd(times, b, par_at):
                dve.wait_ge(ht_mm, times * B + b + 1 + CREDIT)
                for c in range(C):
                    cols = b_ps[:, c * S:(c + 1) * S]
                    dve.tensor_scalar(hT[:, c, b, :], cols, par[:, bass.ds(par_at + c, 1)],
                                      par[:, bass.ds(par_at + C + c, 1)], ALU.mult, ALU.add).then_inc(ht_odd, 1)

            def input_norm(times, par_at, between=None):
                norm(times, EPS0, B + times * BODIES // 2)
                for b in range(B):
                    if between:
                        between(b)
                    normed(times, b)
                    if b % 2 == 0 and b:
                        input_odd(times, b - 1, par_at)
                input_odd(times, B - 1, par_at)

            def group(lay, g, last_group):
                w = lay * G + g
                split_block(WO, 1, 4 * w + 3)
                dve.wait_ge(bo_add, B * (lay + 1) + CREDIT)
                settle(dve)
                with dve.Fori(0, B // 2 - 1) as bp:
                    for bb in range(2):
                        body(w * B + 2 * bp + bb, bb, 2 * bp + bb, lay, g, w)
                for bb in range(2):
                    body(w * B + B - 2 + bb, bb, B - 2 + bb, lay, g, w, bb == 1, bb == 1 and last_group)

            split_context(0, 0)
            split_block(WV, 0, 0)
            dve.wait_ge(x_loaded, 16)
            for b in range(B):
                row_stats(b)
            split_block(WQ, 1, 1)
            dve.wait_ge(par_loaded, 16)
            with dve.Fori(0, LAYERS) as lay:
                first = lay * (BODIES // 2)

                def values_between(b):
                    if b + 1 < NT:
                        value_out(first, b + 1, 0)
                    if b == B - 2:
                        split_h(first, 0)

                dve.wait_ge(wrow_loaded, 16 * (lay * G + 1))
                value_out(first, 0, 0)
                dve.wait_ge(y_add, first + CREDIT)
                input_norm(lay, P_NORM + lay * 2 * C, values_between)
                dve.wait_ge(k_col, lay * (BODIES // 2) * HG + CREDIT)
                bias_k = par[:, bass.ds(lay * P_LAYER + P_BIASK, H)]
                dve.tensor_copy(kbias_s[:, 0, :], bias_k).then_inc(kbias, 1)
                low(kbias_s[:, 0, :], kbias_s[:, 1, :], bias_k, kbias, 2 * lay + 1, kbias)
                split_block(WK, 0, 4 * G * lay + 2)
                settle(dve)
                with dve.Fori(0, G - 1) as g:
                    group(lay, g, False)
                group(lay, G - 1, True)
            if stop_after == "L0":
                return

            dve.wait_ge(y_add, BODIES + CREDIT)

            def input_parts(half):
                cols = slice(half * HB * S, (half + 1) * HB * S)
                for c in range(C):
                    low(hm_s[:, 0, c, cols], hm_s[:, 1, c, cols],
                        hT[:, c, half * HB:(half + 1) * HB, :].rearrange("p b q -> p (b q)"), hm_hi, C * half + c + 1, hm_lo)

            input_norm(LAYERS, P_NORM + LAYERS * 2 * C, lambda b: input_parts(0) if b == B - 1 else None)
            input_parts(1)
            dve.wait_ge(bo_add, B * (LAYERS + 1) + CREDIT)
            with dve.Fori(0, MG) as m:
                for half in range(2):
                    for f in range(FT):
                        k = half * FT + f
                        cols = slice(half * HB * S, (half + 1) * HB * S)
                        low(g_s[:, 0, f, cols], g_s[:, 1, f, cols], gelu[:, k % 2, :], g_hi, 2 * FT * m + k + 1, g_lo)
                for b in range(B):
                    if b == 2:
                        split_block(W1, 0, MLP_BLOCK + 2 * m + 2)
                    dve.wait_ge(fc2_mm, B * m + b + 1 + CREDIT)
                    dve.tensor_tensor(x_sb[:, b, :], x_sb[:, b, :], bank[4 + b % 2][0:S, :], ALU.add).then_inc(m_add, 1)
                split_block(W2, 1, MLP_BLOCK + 2 * m + 3)

            low(wk1_s[:, 0].rearrange("p c n -> p (c n)"), wk1_s[:, 1].rearrange("p c n -> p (c n)"),
                wkv_raw[:, 0].rearrange("p c n -> p (c n)"), w_hi, 4 * (LAST_BLOCK + 2) + 1, w_lo)

            def values1_out(i, slot):
                dve.wait_ge(vc_mm, i + 1 + CREDIT)
                dve.wait_ge(pv1_mm, 2 * i - 2 + CREDIT)
                for t in range(NT):
                    rows = P if t < NT - 1 else T - (NT - 1) * P
                    for a in range(2):
                        dst = v_wide[0:rows, slot, t, a::2, a * HS:(a + 1) * HS]
                        src = c_ps[0:rows, t * P:(t + 1) * P].rearrange("p (c n) -> p c n", c=PAIRS)
                        bias = wrow[0:rows, 1, 0:P].rearrange("p (c n) -> p c n", c=PAIRS)
                        ins = dve.tensor_tensor(dst, src[:, :, a * HS:(a + 1) * HS], bias[:, :, a * HS:(a + 1) * HS], ALU.add)
                ins.then_inc(vc_out, 1)

            def input_lo(i):
                low(hb_s[:, 0], hb_s[:, 1], b_ps[:, 0:C * S].rearrange("p (c q) -> p c q", c=C), hb_hi, BODIES + i + 1, hb_lo)

            def keys1_lo(i):
                dve.wait_ge(k1_hi, i + 1 + CREDIT)
                dve.scalar_tensor_tensor(kh_s[:, 1, 1:T1], c_ps[:, 1:T1], par[:, P_BK1:P_BK1 + 1],
                                         f32(kh_s[:, 0, 1:T1]), ALU.add, ALU.subtract).then_inc(k1_lo, 1)

            def masked(i, slot, k, js=range(J)):
                dve.wait_ge(t1_mm, NT * (KV * i + k - 1) + CREDIT)
                for j in js:
                    dve.wait_ge(s1_mm, J * (KV * i + k) + j + 1 + CREDIT)
                    settle(dve)
                    dve.tensor_tensor_reduce(p_sb[:, k % 2 * J + j, 0:T], s_ps[j % 2][0:S, 1:T1],
                                             mask_sb[:, slot, :], 1.0, -3.4e38, ALU.add, ALU.max,
                                             rmax[:, k % 2, j:j + 1]).then_inc(rmax1, 1)
                if js[-1] == J - 1:
                    dve.wait_ge(rmax1, J * (KV * i + k + 1) + CREDIT)
                    dve.tensor_scalar(nmax[:, k % 2, :], rmax[:, k % 2, :], -1.0, None, ALU.mult).then_inc(nmax1, 1)

            def probs1_odd(i, slot, k):
                dve.wait_ge(pv1_mm, 2 * i + SLOT_FREE[k] + CREDIT)
                dve.wait_ge(t1_mm, NT * (KV * i + k) + 2 + CREDIT)
                dve.tensor_copy(pT1[slot][k][:, 1, :], t1_ps[1][:, 0:J * S]).then_inc(pt1_odd, 1)

            def sums_inverse(i, slot):
                dve.wait_ge(exp1, J * KV * (i + 1) + CREDIT)
                dve.reciprocal(zsum1[:, slot], zsum1[:, slot]).then_inc(z1_inv, 1)

            def out_scaled(b):
                dve.scalar_tensor_tensor(x_sb[:, b, :], x_sb[:, b, :], mv[:, b, 0:1], gb[:, 0, :], ALU.subtract, ALU.mult
                                         ).then_inc(m_add, 1)

            def out_shifted(b):
                dve.wait_ge(m_add, B * MG + b + 1 + CREDIT)
                dve.scalar_tensor_tensor(x_sb[:, b, :], x_sb[:, b, :], rstd[:, 2, b:b + 1], gb[:, 1, :], ALU.mult, ALU.add
                                         ).then_inc(fin, 1)

            def sums_wide(i, slot, last):
                dve.wait_ge(z1_inv, i + 1 + CREDIT)
                dve.wait_ge(qt_mm, BODIES + i + (1 if last else 2) + CREDIT)
                dve.tensor_copy(rz_wide, zsum1[:, slot].unsqueeze(3).broadcast_to([S, J, KV, HS])).then_inc(z_wide, 1)

            def heads1_norm(i):
                dve.wait_ge(z_out, i + 1 + CREDIT)
                dve.wait_ge(pv1_mm, 2 * (i + 1) + CREDIT)
                dve.tensor_tensor(on_sb[:, :], o_ps[:, 0:J * S], on_sb[:, :], ALU.mult).then_inc(o_norm, 1)

            def heads1_lo(i):
                low(oT_s[:, 0], oT_s[:, 1], on_sb[:, :].rearrange("p (j q) -> p j q", j=J), o_hi, BODIES + i + 1, o_lo)

            def step(i, slot, k, late=None, soon=None, following=True):
                m = (i, slot, k + 2) if k + 2 < KV else (i + 1, 1 - slot, k + 2 - KV)
                if following:
                    masked(*m, range(0, 2))
                probs1_odd(i, slot, k)
                if late:
                    late()
                if following:
                    masked(*m, range(2, 4))
                if soon:
                    soon()

            def body1(i, slot, loads, last):
                if last:
                    for k in range(2, KV):
                        if k == 7:
                            sums_inverse(i, slot)
                            sums_wide(i, slot, last)
                        step(i, slot, k, following=k + 2 < KV)
                    norm(LAYERS + 1, EPS1, B + BODIES + B - 1, LAST_STEPS, 0, B - 1)
                    heads1_norm(i)
                    dve.wait_ge(gb_loaded, 16)
                    out_scaled(0)
                    heads1_lo(i)
                    for b in range(1, B - 1):
                        out_scaled(b)
                        out_shifted(b - 1)
                    out_shifted(B - 2)
                    dve.wait_ge(bo_add, B * (LAYERS + 1) + i + 1 + CREDIT)
                    add_out(BODIES + i, i, c_ps)
                    dve.wait_ge(y_add, BODIES + i + 1 + CREDIT)
                    settle(dve)
                    row_stats(i)
                    return
                step(i, slot, 2, soon=lambda: input_lo(i + 1))
                step(i, slot, 3, late=lambda: keys1_lo(i + 1), soon=lambda: queries_out(BODIES + i + 1, b_ps))
                step(i, slot, 4, soon=lambda: queries_lo(BODIES + i + 1, b_ps, SCALE1))
                step(i, slot, 5)
                dve.wait_ge(mask_loaded[1 - slot], 16 * B // 2 if loads is None else 16 * (loads - 1 + slot))
                step(i, slot, 6)
                sums_inverse(i, slot)
                step(i, slot, 7, late=lambda: sums_wide(i, slot, last))
                values1_out(i + 1, 1 - slot)
                step(i + 1, 1 - slot, 0, late=lambda: heads1_norm(i), soon=lambda: heads1_lo(i))
                dve.wait_ge(bo_add, B * (LAYERS + 1) + i + 1 + CREDIT)
                step(i + 1, 1 - slot, 1, late=lambda: add_out(BODIES + i, i, c_ps))
                dve.wait_ge(y_add, BODIES + i + 1 + CREDIT)
                settle(dve)
                row_stats(i)

            input_lo(0)
            keys1_lo(0)
            dve.wait_ge(wrow_loaded, 16 * (SETS + 1))
            queries_out(BODIES, b_ps)
            dve.wait_ge(wide_zero, 2 * J + 2 + CREDIT)
            values1_out(0, 0)
            queries_lo(BODIES, b_ps, SCALE1)
            dve.wait_ge(mask_loaded[0], 16)
            masked(0, 0, 0)
            masked(0, 0, 1)
            step(0, 0, 0)
            step(0, 0, 1)
            with dve.Fori(0, B // 2 - 1) as t:
                for bb in range(2):
                    body1(2 * t + bb, bb, t + 2, False)
            for bb in range(2):
                body1(B - 2 + bb, bb, None, bb == 1)
            norm(LAYERS + 2, EPS1, B + BODIES + B, LAST_STEPS + LN_STEPS - 1, B - 1, B)
            out_scaled(B - 1)
            out_shifted(B - 1)


def lay_out(a):
    f = {k: np.asarray(v) for k, v in a.items()}

    def w_in(w):
        return w.reshape(C, P, -1).transpose(1, 0, 2).reshape(P, -1)

    L = lambda name, i: f[f"L0_xattn_{name}{i + 1}"]
    blocks = []
    for i in range(LAYERS):
        for g in range(G):
            cols = slice(g * D, (g + 1) * D)
            blocks += [w_in(L(n, i)[:, cols]) for n in ("wv", "wq", "wk")] + [w_in(L("wo", i)[cols, :])]
    for m in range(MG):
        cols = slice(m * D, (m + 1) * D)
        blocks += [w_in(f["L0_xattn_w_fc1"][:, cols]), w_in(f["L0_xattn_w_fc2"][cols, :])]
    by_j = lambda v: v.reshape(v.shape[:-1] + (KV, J, HS)).swapaxes(-3, -2).reshape(v.shape)
    blocks += [w_in(by_j(f["L1_xattn_Wq"])), w_in(by_j(f["L1_xattn_Wo"].T).T)]
    wkv = np.concatenate([w_in(f["L1_xattn_Wk"]), w_in(f["L1_xattn_Wv"])], axis=1)
    col = lambda v: v.reshape(-1, P).T
    par = []
    for i in range(LAYERS):
        par += [col(L("bk", i)), col(L("bias_k", i))]
    for s, o in (("ln1_scale", "ln1_offset"), ("ln2_scale", "ln2_offset"), ("ln_mlp_scale", "ln_mlp_offset")):
        par += [col(f["L0_xattn_" + s]), col(f["L0_xattn_" + o])]
    par += [col(f["L0_xattn_b_fc1"]), col(f["L1_xattn_bk"])]
    pick = np.zeros((PAIRS, 2, HS, PICK), np.float32)
    for c in range(PAIRS):
        for a in range(2):
            for part in range(2):
                for d in range(HS):
                    pick[c, a, d, 2 * HS + c * P + a * 4 * HS + part * HS + d] = 1
    rows = np.stack([L("bo", 0), L("bo", 1), f["L0_xattn_b_fc2"], f["L1_xattn_bo"]])
    wrow = [np.stack([L(n, i).reshape(-1)[g * D:(g + 1) * D] for n in ("bq", "bv", "bias_v")])
            for i in range(LAYERS) for g in range(G)]
    last = np.zeros((3, D), np.float32)
    last[0] = by_j(f["L1_xattn_bq"])
    last[1, 0:KV * HS] = f["L1_xattn_bv"]
    ctx = f["ctx_2048"].reshape(B, T, C, P).transpose(0, 3, 2, 1)
    return {
        "x": f["x"], "ctx": ctx, "mask": f["mask_Bx1xSxS2_ff0"].reshape(B, S, T), "w": np.stack(blocks),
        "wkv": wkv.reshape(P, 2, C, P), "par": np.concatenate(par, axis=1),
        "pick": pick.reshape(P, PICK), "rows": rows,
        "wrow": np.stack(wrow + [last]), "gb": np.stack([f["L1_xattn_gamma"], f["L1_xattn_beta"]]),
    }


def kernel(**inputs):
    import concourse.bacc as bacc
    from concourse.bass_utils import run_bass_kernel_spmd

    nc = bacc.Bacc("TRN2", target_bir_lowering=False, num_devices=1)
    arrays = {f"in_{k}": np.ascontiguousarray(v) for k, v in lay_out(inputs).items()}
    args = [nc.dram_tensor(k, v.shape, mybir.dt.from_np(v.dtype), kind="ExternalInput").ap() for k, v in arrays.items()]
    out = nc.dram_tensor("out", (B, S, D), F32, kind="ExternalOutput").ap()
    build(nc, *args, out)
    r = run_bass_kernel_spmd(nc, [arrays], core_ids=[0])
    return r.results[0]["out"]
```
